# Optimizing a Trainium2 kernel written in Bass

```python
import numpy as np
import jax
import jax.numpy as jnp

def _softmax(x, axis=-1):
    return jax.nn.softmax(x, axis=axis)

def _gelu(x):
    return jax.nn.gelu(x, approximate=True)

def _silu(x):
    return jax.nn.silu(x)

def _sigmoid(x):
    return jax.nn.sigmoid(x)

def _layernorm(x, axis=-1, eps=1e-05):
    m = jnp.mean(x, axis=axis, keepdims=True)
    v = jnp.var(x, axis=axis, keepdims=True)
    return (x - m) / jnp.sqrt(v + eps)

def _scatter_add(tgt, idx, src, axis=0):
    return tgt.at[idx].add(src)

def _segment_sum(src, seg, n):
    return jax.ops.segment_sum(src, seg, n)
kernel_name = 'mk_vit_tower_cls_d2_tok_img1024_r4_7b53d7'

def setup_inputs(seed: int=0):
    np.random.seed(seed)
    _w = jnp.asarray

    def _rec_inputs():
        import jax
        import jax.numpy as jnp
        _rk = jax.random.key(seed)
        x = -0.00016672 + 0.999947 * jax.random.normal(jax.random.fold_in(_rk, 1), (16, 3, 96, 96), jnp.float32)
        cls_tok = 0.02 * jax.random.normal(jax.random.fold_in(_rk, 5), (1, 1, 256), jnp.float32)
        return (x, cls_tok)
    x, cls_tok = _rec_inputs()

    def _L0_tok_setup():
        import jax, jax.numpy as jnp
        import numpy as np
        B, C, H, Wd = (64, 3, 96, 96)
        PH, PW, D = (16, 16, 256)
        PATCH_DIM = C * PH * PW
        N_TOK = H // PH * (Wd // PW)
        key = jax.random.key(seed)
        k1, k2, k3, k4, k5 = jax.random.split(key, 5)
        x = jax.random.normal(k1, (B, C, H, Wd), dtype=jnp.float32)
        W = jax.random.normal(k2, (D, PATCH_DIM), dtype=jnp.float32) * PATCH_DIM ** (-0.5)
        b = jax.random.normal(k3, (D,), dtype=jnp.float32) * 0.02
        cls_token = jax.random.normal(k4, (1, 1, D), dtype=jnp.float32)
        pos_embedding = jax.random.normal(k5, (1, N_TOK + 1, D), dtype=jnp.float32) * 0.02
        return {'x': x, 'W': W, 'b': b, 'cls_token': cls_token, 'pos_embedding': pos_embedding}
    _L0_tok_all = _L0_tok_setup()
    _L0_tok_in = {k: v for k, v in _L0_tok_all.items() if k in ('W', 'b', 'cls_token', 'pos_embedding')}
    del _L0_tok_all

    def _L0_attn_setup():
        import jax, jax.numpy as jnp
        import numpy as np
        B, T, C, H = (2, 512, 256, 16)
        D = C // H
        RW, RA, RG = (64, 64, 128)
        EPS = 1e-05

        def _rwkv7_scan(r, log_w, k, v, a, b):
            Bn, Tn, Hn, Dn = r.shape

            def step(S, xs):
                r_t, w_t, k_t, v_t, a_t, b_t = xs
                sa = jnp.einsum('bhij,bhj->bhi', S, a_t)
                S = S * jnp.exp(w_t)[:, :, None, :] + sa[..., None] * b_t[:, :, None, :] + v_t[..., None] * k_t[:, :, None, :]
                o_t = jnp.einsum('bhij,bhj->bhi', S, r_t)
                return (S, o_t)
            S0 = jnp.zeros((Bn, Hn, Dn, Dn), r.dtype)
            xs = tuple((jnp.swapaxes(x, 0, 1) for x in (r, log_w, k, v, a, b)))
            _, o = jax.lax.scan(step, S0, xs)
            return jnp.swapaxes(o, 0, 1)
        key = jax.random.key(seed)
        ks = iter(jax.random.split(key, 40))
        n = lambda s, sc=0.02: jax.random.normal(next(ks), s, jnp.float32) * sc
        u = lambda s: jax.random.uniform(next(ks), s, jnp.float32)
        return dict(hidden_states=jax.random.normal(next(ks), (B, T, C), jnp.float32), x_r=u((C,)), x_w=u((C,)), x_k=u((C,)), x_v=u((C,)), x_a=u((C,)), x_g=u((C,)), k_k=u((C,)), k_a=u((C,)), r_k=n((H, D), 0.1), W_r=n((C, C)), W_k=n((C, C)), W_v=n((C, C)), W_o=n((C, C)), w_lora_a=n((C, RW)), w_lora_b=n((RW, C)), w_lora_bias=n((C,), 0.1), a_lora_a=n((C, RA)), a_lora_b=n((RA, C)), a_lora_bias=jnp.zeros((C,), jnp.float32), g_lora_a=n((C, RG)), g_lora_b=n((RG, C)), g_lora_bias=jnp.zeros((C,), jnp.float32), gn_weight=jnp.ones((C,), jnp.float32), gn_bias=jnp.zeros((C,), jnp.float32))
    _L0_attn_all = _L0_attn_setup()
    _L0_attn_in = {k: v for k, v in _L0_attn_all.items() if k in ('x_r', 'x_w', 'x_k', 'x_v', 'x_a', 'x_g', 'k_k', 'k_a', 'r_k', 'W_r', 'W_k', 'W_v', 'W_o', 'w_lora_a', 'w_lora_b', 'w_lora_bias', 'a_lora_a', 'a_lora_b', 'a_lora_bias', 'g_lora_a', 'g_lora_b', 'g_lora_bias', 'gn_weight', 'gn_bias')}
    del _L0_attn_all

    def _L0_ffn_setup():
        import jax, jax.numpy as jnp
        import numpy as np
        LN_EPS = 1e-05

        def layer_norm(x, g, b):
            mu = jnp.mean(x, axis=-1, keepdims=True)
            var = jnp.mean(jnp.square(x - mu), axis=-1, keepdims=True)
            return (x - mu) * jax.lax.rsqrt(var + LN_EPS) * g + b

        def ternary_quant(w):
            scale = 1.0 / jnp.clip(jnp.mean(jnp.abs(w)), 1e-05)
            wq = jnp.clip(jnp.round(w * scale), -1.0, 1.0) / scale
            return w + jax.lax.stop_gradient(wq - w)
        key = jax.random.key(seed)
        ks = jax.random.split(key, 3)
        dim, hidden = (256, 1024)
        B, S = (8, 256)
        x = jax.random.normal(ks[0], (B, S, dim), dtype=jnp.float32)
        w1 = jax.random.normal(ks[1], (hidden, dim), dtype=jnp.float32) * 0.02
        w2 = jax.random.normal(ks[2], (dim, hidden), dtype=jnp.float32) * 0.02
        return {'x': x, 'ln1_g': jnp.ones((dim,), jnp.float32), 'ln1_b': jnp.zeros((dim,), jnp.float32), 'w1': w1, 'b1': jnp.zeros((hidden,), jnp.float32), 'ln2_g': jnp.ones((hidden,), jnp.float32), 'ln2_b': jnp.zeros((hidden,), jnp.float32), 'w2': w2, 'b2': jnp.zeros((dim,), jnp.float32)}
    _L0_ffn_all = _L0_ffn_setup()
    _L0_ffn_in = {k: v for k, v in _L0_ffn_all.items() if k in ('ln1_g', 'ln1_b', 'w1', 'b1', 'ln2_g', 'ln2_b', 'w2', 'b2')}
    del _L0_ffn_all

    def _L1_attn_setup():
        import jax, jax.numpy as jnp
        import numpy as np
        HIDDEN = 256
        HEADS = 16
        HEAD_DIM = HIDDEN // HEADS
        SPARSITY_RATIO = 0.5
        key = jax.random.key(seed)
        ks = jax.random.split(key, 6)
        B, S = (2, 512)
        lim = float(np.sqrt(6.0 / (HIDDEN + HIDDEN)))
        x = jax.random.normal(ks[0], (B, S, HIDDEN), dtype=jnp.float32)
        Wq = jax.random.uniform(ks[1], (HIDDEN, HIDDEN), minval=-lim, maxval=lim, dtype=jnp.float32)
        Wk = jax.random.uniform(ks[2], (HIDDEN, HIDDEN), minval=-lim, maxval=lim, dtype=jnp.float32)
        Wv = jax.random.uniform(ks[3], (HIDDEN, HIDDEN), minval=-lim, maxval=lim, dtype=jnp.float32)
        Wo = jax.random.uniform(ks[4], (HIDDEN, HIDDEN), minval=-lim, maxval=lim, dtype=jnp.float32)
        bo = jnp.zeros((HIDDEN,), dtype=jnp.float32)
        adaptive_threshold = jnp.asarray(0.1, dtype=jnp.float32)
        return {'x': x, 'Wq': Wq, 'Wk': Wk, 'Wv': Wv, 'Wo': Wo, 'bo': bo, 'adaptive_threshold': adaptive_threshold}
    _L1_attn_all = _L1_attn_setup()
    _L1_attn_in = {k: v for k, v in _L1_attn_all.items() if k in ('Wq', 'Wk', 'Wv', 'Wo', 'bo', 'adaptive_threshold')}
    del _L1_attn_all

    def _L1_ffn_setup():
        import jax, jax.numpy as jnp
        import numpy as np
        E = 16
        H = 256
        F = 512
        TOP_K = 1
        B, S = (2, 256)
        key = jax.random.key(seed)
        ks = jax.random.split(key, 7)
        s = 0.02
        return {'hidden_states': jax.random.normal(ks[0], (B, S, H), jnp.float32), 'w_router': jax.random.normal(ks[1], (E, H), jnp.float32) * s, 'gate_up_proj': jax.random.normal(ks[2], (E, H, 2 * F), jnp.float32) * s, 'down_proj': jax.random.normal(ks[3], (E, F, H), jnp.float32) * s, 'w_gate': jax.random.normal(ks[4], (F, H), jnp.float32) * s, 'w_up': jax.random.normal(ks[5], (F, H), jnp.float32) * s, 'w_down': jax.random.normal(ks[6], (H, F), jnp.float32) * s}
    _L1_ffn_all = _L1_ffn_setup()
    _L1_ffn_in = {k: v for k, v in _L1_ffn_all.items() if k in ('w_router', 'gate_up_proj', 'down_proj', 'w_gate', 'w_up', 'w_down')}
    del _L1_ffn_all
    return {'x': x, 'cls_tok': cls_tok, 'L0_tok_W': _L0_tok_in['W'], 'L0_tok_b': _L0_tok_in['b'], 'L0_tok_cls_token': _L0_tok_in['cls_token'], 'L0_tok_pos_embedding': _L0_tok_in['pos_embedding'], 'L0_attn_x_r': _L0_attn_in['x_r'], 'L0_attn_x_w': _L0_attn_in['x_w'], 'L0_attn_x_k': _L0_attn_in['x_k'], 'L0_attn_x_v': _L0_attn_in['x_v'], 'L0_attn_x_a': _L0_attn_in['x_a'], 'L0_attn_x_g': _L0_attn_in['x_g'], 'L0_attn_k_k': _L0_attn_in['k_k'], 'L0_attn_k_a': _L0_attn_in['k_a'], 'L0_attn_r_k': _L0_attn_in['r_k'], 'L0_attn_W_r': _L0_attn_in['W_r'], 'L0_attn_W_k': _L0_attn_in['W_k'], 'L0_attn_W_v': _L0_attn_in['W_v'], 'L0_attn_W_o': _L0_attn_in['W_o'], 'L0_attn_w_lora_a': _L0_attn_in['w_lora_a'], 'L0_attn_w_lora_b': _L0_attn_in['w_lora_b'], 'L0_attn_w_lora_bias': _L0_attn_in['w_lora_bias'], 'L0_attn_a_lora_a': _L0_attn_in['a_lora_a'], 'L0_attn_a_lora_b': _L0_attn_in['a_lora_b'], 'L0_attn_a_lora_bias': _L0_attn_in['a_lora_bias'], 'L0_attn_g_lora_a': _L0_attn_in['g_lora_a'], 'L0_attn_g_lora_b': _L0_attn_in['g_lora_b'], 'L0_attn_g_lora_bias': _L0_attn_in['g_lora_bias'], 'L0_attn_gn_weight': _L0_attn_in['gn_weight'], 'L0_attn_gn_bias': _L0_attn_in['gn_bias'], 'L0_ffn_ln1_g': _L0_ffn_in['ln1_g'], 'L0_ffn_ln1_b': _L0_ffn_in['ln1_b'], 'L0_ffn_w1': _L0_ffn_in['w1'], 'L0_ffn_b1': _L0_ffn_in['b1'], 'L0_ffn_ln2_g': _L0_ffn_in['ln2_g'], 'L0_ffn_ln2_b': _L0_ffn_in['ln2_b'], 'L0_ffn_w2': _L0_ffn_in['w2'], 'L0_ffn_b2': _L0_ffn_in['b2'], 'L1_attn_Wq': _L1_attn_in['Wq'], 'L1_attn_Wk': _L1_attn_in['Wk'], 'L1_attn_Wv': _L1_attn_in['Wv'], 'L1_attn_Wo': _L1_attn_in['Wo'], 'L1_attn_bo': _L1_attn_in['bo'], 'L1_attn_adaptive_threshold': _L1_attn_in['adaptive_threshold'], 'L1_ffn_w_router': _L1_ffn_in['w_router'], 'L1_ffn_gate_up_proj': _L1_ffn_in['gate_up_proj'], 'L1_ffn_down_proj': _L1_ffn_in['down_proj'], 'L1_ffn_w_gate': _L1_ffn_in['w_gate'], 'L1_ffn_w_up': _L1_ffn_in['w_up'], 'L1_ffn_w_down': _L1_ffn_in['w_down']}

def reference(x, cls_tok, L0_tok_W, L0_tok_b, L0_tok_cls_token, L0_tok_pos_embedding, L0_attn_x_r, L0_attn_x_w, L0_attn_x_k, L0_attn_x_v, L0_attn_x_a, L0_attn_x_g, L0_attn_k_k, L0_attn_k_a, L0_attn_r_k, L0_attn_W_r, L0_attn_W_k, L0_attn_W_v, L0_attn_W_o, L0_attn_w_lora_a, L0_attn_w_lora_b, L0_attn_w_lora_bias, L0_attn_a_lora_a, L0_attn_a_lora_b, L0_attn_a_lora_bias, L0_attn_g_lora_a, L0_attn_g_lora_b, L0_attn_g_lora_bias, L0_attn_gn_weight, L0_attn_gn_bias, L0_ffn_ln1_g, L0_ffn_ln1_b, L0_ffn_w1, L0_ffn_b1, L0_ffn_ln2_g, L0_ffn_ln2_b, L0_ffn_w2, L0_ffn_b2, L1_attn_Wq, L1_attn_Wk, L1_attn_Wv, L1_attn_Wo, L1_attn_bo, L1_attn_adaptive_threshold, L1_ffn_w_router, L1_ffn_gate_up_proj, L1_ffn_down_proj, L1_ffn_w_gate, L1_ffn_w_up, L1_ffn_w_down):
    import jax
    import jax.numpy as jnp

    def _L0_tok_ref(x, W, b, cls_token, pos_embedding):
        import jax, jax.numpy as jnp
        import numpy as np
        B, C, H, Wd = (64, 3, 96, 96)
        PH, PW, D = (16, 16, 256)
        PATCH_DIM = C * PH * PW
        N_TOK = H // PH * (Wd // PW)
        Bc = x.shape[0]
        nh, nw = (H // PH, Wd // PW)
        patches = x.reshape(Bc, C, nh, PH, nw, PW)
        patches = patches.transpose(0, 2, 4, 1, 3, 5).reshape(Bc, nh * nw, PATCH_DIM)
        tokens = jnp.einsum('bnp,dp->bnd', patches, W) + b
        cls = jnp.broadcast_to(cls_token, (Bc, 1, D))
        tokens = jnp.concatenate([cls, tokens], axis=1)
        return tokens + pos_embedding

    def _L0_attn_ref(hidden_states, x_r, x_w, x_k, x_v, x_a, x_g, k_k, k_a, r_k, W_r, W_k, W_v, W_o, w_lora_a, w_lora_b, w_lora_bias, a_lora_a, a_lora_b, a_lora_bias, g_lora_a, g_lora_b, g_lora_bias, gn_weight, gn_bias):
        import jax, jax.numpy as jnp
        import numpy as np
        B, T, C, H = (2, 512, 256, 16)
        D = C // H
        RW, RA, RG = (64, 64, 128)
        EPS = 1e-05

        def _rwkv7_scan(r, log_w, k, v, a, b):
            Bn, Tn, Hn, Dn = r.shape

            def step(S, xs):
                r_t, w_t, k_t, v_t, a_t, b_t = xs
                sa = jnp.einsum('bhij,bhj->bhi', S, a_t)
                S = S * jnp.exp(w_t)[:, :, None, :] + sa[..., None] * b_t[:, :, None, :] + v_t[..., None] * k_t[:, :, None, :]
                o_t = jnp.einsum('bhij,bhj->bhi', S, r_t)
                return (S, o_t)
            S0 = jnp.zeros((Bn, Hn, Dn, Dn), r.dtype)
            xs = tuple((jnp.swapaxes(x, 0, 1) for x in (r, log_w, k, v, a, b)))
            _, o = jax.lax.scan(step, S0, xs)
            return jnp.swapaxes(o, 0, 1)
        Bn, Tn, Cn = hidden_states.shape
        shifted = jnp.concatenate([jnp.zeros_like(hidden_states[:, :1]), hidden_states[:, :-1]], axis=1)
        delta = shifted - hidden_states
        xr = hidden_states + delta * x_r
        xw = hidden_states + delta * x_w
        xk = hidden_states + delta * x_k
        xv = hidden_states + delta * x_v
        xa = hidden_states + delta * x_a
        r = xr @ W_r
        log_w = -jax.nn.softplus(-(jnp.tanh(xw @ w_lora_a) @ w_lora_b + w_lora_bias)) - 0.5
        k = xk @ W_k
        v = xv @ W_v
        a = jax.nn.sigmoid(xa @ a_lora_a @ a_lora_b + a_lora_bias)
        g = jax.nn.sigmoid(r @ g_lora_a) @ g_lora_b + g_lora_bias
        kk = (k * k_k).reshape(Bn, Tn, H, D)
        kk = kk / jnp.maximum(jnp.linalg.norm(kk, axis=-1, keepdims=True), 1e-12)
        k = k * (1.0 + (a - 1.0) * k_a)
        rh = r.reshape(Bn, Tn, H, D)
        wh = log_w.reshape(Bn, Tn, H, D)
        kh = k.reshape(Bn, Tn, H, D)
        vh = v.reshape(Bn, Tn, H, D)
        ah = a.reshape(Bn, Tn, H, D)
        o = _rwkv7_scan(rh, wh, kh, vh, -kk, kk * ah)
        mu = o.mean(-1, keepdims=True)
        var = ((o - mu) ** 2).mean(-1, keepdims=True)
        o_flat = ((o - mu) * jax.lax.rsqrt(var + EPS)).reshape(Bn, Tn, C) * gn_weight + gn_bias
        bonus = ((rh * kh * r_k).sum(-1, keepdims=True) * vh).reshape(Bn, Tn, C)
        o_flat = o_flat + bonus
        return o_flat * g @ W_o

    def _L0_ffn_ref(x, ln1_g, ln1_b, w1, b1, ln2_g, ln2_b, w2, b2):
        import jax, jax.numpy as jnp
        import numpy as np
        LN_EPS = 1e-05

        def layer_norm(x, g, b):
            mu = jnp.mean(x, axis=-1, keepdims=True)
            var = jnp.mean(jnp.square(x - mu), axis=-1, keepdims=True)
            return (x - mu) * jax.lax.rsqrt(var + LN_EPS) * g + b

        def ternary_quant(w):
            scale = 1.0 / jnp.clip(jnp.mean(jnp.abs(w)), 1e-05)
            wq = jnp.clip(jnp.round(w * scale), -1.0, 1.0) / scale
            return w + jax.lax.stop_gradient(wq - w)
        h = layer_norm(x, ln1_g, ln1_b)
        h = jnp.einsum('bsd,hd->bsh', h, ternary_quant(w1)) + b1
        h = jax.nn.gelu(h, approximate=False)
        h = layer_norm(h, ln2_g, ln2_b)
        out = jnp.einsum('bsh,dh->bsd', h, ternary_quant(w2)) + b2
        return out

    def _L1_attn_ref(x, Wq, Wk, Wv, Wo, bo, adaptive_threshold):
        import jax, jax.numpy as jnp
        import numpy as np
        HIDDEN = 256
        HEADS = 16
        HEAD_DIM = HIDDEN // HEADS
        SPARSITY_RATIO = 0.5
        B, S, _ = x.shape
        H, D = (HEADS, HEAD_DIM)
        q = (x @ Wq.T).reshape(B, S, H, D).transpose(0, 2, 1, 3)
        k = (x @ Wk.T).reshape(B, S, H, D).transpose(0, 2, 1, 3)
        v = (x @ Wv.T).reshape(B, S, H, D).transpose(0, 2, 1, 3)
        scores = jnp.einsum('bhqd,bhkd->bhqk', q, k) / jnp.sqrt(jnp.asarray(D, x.dtype))
        k_keep = max(1, int(S * (1.0 - SPARSITY_RATIO)))
        topv = jax.lax.top_k(scores, k_keep)[0]
        kth = topv[..., -1:]
        thr = jnp.clip(adaptive_threshold, 0.0, 1.0)
        keep = (scores >= kth) & (scores >= thr)
        neg_inf = jnp.asarray(-jnp.inf, scores.dtype)
        masked = jnp.where(keep, scores, neg_inf)
        attn = jax.nn.softmax(masked, axis=-1)
        out = jnp.einsum('bhqk,bhkd->bhqd', attn, v)
        out = out.transpose(0, 2, 1, 3).reshape(B, S, H * D)
        return out @ Wo.T + bo

    def _L1_ffn_ref(hidden_states, w_router, gate_up_proj, down_proj, w_gate, w_up, w_down):
        import jax, jax.numpy as jnp
        import numpy as np
        E = 16
        H = 256
        F = 512
        TOP_K = 1
        B, S = (2, 256)
        b, s, h = hidden_states.shape
        x = hidden_states.reshape(-1, h)
        logits = x @ w_router.T
        _, top_idx = jax.lax.top_k(logits, TOP_K)
        mask = jax.nn.one_hot(top_idx, E, dtype=logits.dtype).sum(axis=1)
        scores = jax.nn.sigmoid(logits) * mask
        masked_inputs = scores.T[:, :, None] * x[None, :, :]
        gate_up = jnp.einsum('eth,ehf->etf', masked_inputs, gate_up_proj)
        gate, up = jnp.split(gate_up, 2, axis=-1)
        expert_out = jnp.einsum('etf,efh->eth', up * jax.nn.silu(gate), down_proj)
        shared = jax.nn.silu(x @ w_gate.T) * (x @ w_up.T) @ w_down.T
        out = shared + expert_out.sum(axis=0)
        return out.reshape(b, s, h)
    h = _L0_tok_ref(x, L0_tok_W, L0_tok_b, L0_tok_cls_token, L0_tok_pos_embedding)
    h = jnp.concatenate([jnp.broadcast_to(cls_tok, (h.shape[0], 1, h.shape[2])), h], axis=1)
    h = h + _L0_attn_ref(_layernorm(h, axis=-1), L0_attn_x_r, L0_attn_x_w, L0_attn_x_k, L0_attn_x_v, L0_attn_x_a, L0_attn_x_g, L0_attn_k_k, L0_attn_k_a, L0_attn_r_k, L0_attn_W_r, L0_attn_W_k, L0_attn_W_v, L0_attn_W_o, L0_attn_w_lora_a, L0_attn_w_lora_b, L0_attn_w_lora_bias, L0_attn_a_lora_a, L0_attn_a_lora_b, L0_attn_a_lora_bias, L0_attn_g_lora_a, L0_attn_g_lora_b, L0_attn_g_lora_bias, L0_attn_gn_weight, L0_attn_gn_bias)
    h = h + _L0_ffn_ref(_layernorm(h, axis=-1), L0_ffn_ln1_g, L0_ffn_ln1_b, L0_ffn_w1, L0_ffn_b1, L0_ffn_ln2_g, L0_ffn_ln2_b, L0_ffn_w2, L0_ffn_b2)
    h = h + _L1_attn_ref(_layernorm(h, axis=-1), L1_attn_Wq, L1_attn_Wk, L1_attn_Wv, L1_attn_Wo, L1_attn_bo, L1_attn_adaptive_threshold)
    h = h + _L1_ffn_ref(_layernorm(h, axis=-1), L1_ffn_w_router, L1_ffn_gate_up_proj, L1_ffn_down_proj, L1_ffn_w_gate, L1_ffn_w_up, L1_ffn_w_down)
    return h

_drawn_inputs = setup_inputs


def setup_inputs(seed=0):
    import zlib

    import numpy as np

    out = dict(_drawn_inputs(seed))
    spreads = {'L0_attn_a_lora_bias': (0.0, 0.8),
     'L0_attn_g_lora_bias': (0.0, 0.1),
     'L0_attn_gn_weight': (1.0, 0.6),
     'L0_attn_gn_bias': (0.0, 0.632),
     'L0_ffn_ln1_g': (1.0, 0.2),
     'L0_ffn_ln1_b': (0.0, 0.1),
     'L0_ffn_b1': (0.0, 0.1),
     'L0_ffn_ln2_g': (1.0, 0.2),
     'L0_ffn_ln2_b': (0.0, 0.1),
     'L0_ffn_b2': (0.0, 0.1),
     'L1_attn_bo': (0.0, 0.1)}
    factors = {'L0_attn_x_w': 8.0,
     'L0_attn_x_a': 8.0,
     'L0_attn_k_k': 4.566,
     'L0_attn_r_k': 49.18,
     'L0_attn_w_lora_a': 8.0,
     'L0_attn_w_lora_b': 8.0,
     'L0_attn_w_lora_bias': 8.0,
     'L0_attn_a_lora_a': 8.0,
     'L0_attn_a_lora_b': 8.0,
     'L0_attn_g_lora_a': 8.0,
     'L1_ffn_w_router': 6.951,
     'L1_ffn_gate_up_proj': 6.876,
     'L1_ffn_down_proj': 6.843,
     'L1_ffn_w_gate': 2.766,
     'L1_ffn_w_up': 2.74,
     'L1_ffn_w_down': 2.722}
    for name, (base, spread) in spreads.items():
        noise = np.random.default_rng([zlib.crc32(name.encode()), seed]).standard_normal(out[name].shape)
        drawn = base * np.exp(spread * noise) if base else spread * noise
        out[name] = jnp.asarray(drawn.astype(out[name].dtype))
    for name, factor in factors.items():
        out[name] = (out[name] * factor).astype(out[name].dtype)
    return out
```

```python
from contextlib import ExitStack

import concourse.bass as bass
from concourse import mybir

P = 128
B = 16
T = 38
D = 256
NT = 5
NP = NT * P
NTOK = B * T
TPT = P // B
NH, HD = 16, 16
KD = D // P
KP = 768 // P
HID = 1024
KH = HID // P
NE, F = 16, 512
KF = F // P
KEEP = T // 2
C = 96
XTRA = NTOK // (C + 1)
TRASH = (NE + XTRA) * C
RING = 4
EPS = 1e-5
EXP_MINUS_HALF = 0.6065306597126334
NEG = -3.0e38
PA, PW, PB, PK, PV, PR = range(6)
NV = 6
HG = 8
CW = D // HG
ST = 2 * HD * HD
ROW = HG * NV * CW

F32 = mybir.dt.float32
I32 = mybir.dt.int32
ALU = mybir.AluOpType
ACT = mybir.ActivationFunctionType
X = mybir.AxisListType.X

MIX, LN1G, LN1B, B1, LN2G, LN2B, NPV = 0, 10, 12, 14, 22, 30, 38
C_E, C_VALID, C_TROW, C_K, C_HM, C_PADROW, NCST = 0, 16, 21, 26, 32, 40, 45
KK_, KA_, RK_, GNW, GNB = range(5)


class Link:

    def __init__(self, eng, sem):
        self.eng, self.sem, self.n = eng, sem, 0

    def __call__(self, ins):
        self.n += 1
        ins.then_inc(self.sem, 1)
        self.eng.wait_ge(self.sem, self.n)


def pipeline(eng, stages, count, unroll, peel):
    last = max(lag for _, lag in stages)
    assert peel % unroll == 0 and count % unroll == 0 and peel >= last
    for k in range(peel):
        for fn, lag in stages:
            if k >= lag:
                fn(k - lag, (k - lag) % unroll)
    with eng.Fori(peel // unroll, count // unroll) as i:
        for u in range(unroll):
            for fn, lag in stages:
                fn(i * unroll + (u - lag), (u - lag) % unroll)
    for k in range(count, count + last):
        for fn, lag in stages:
            if k - lag < count:
                fn(k - lag, (k - lag) % unroll)


def build(nc, a, out):
    with ExitStack() as ctx:
        def sb(name, shape, dt=F32):
            return ctx.enter_context(nc.sbuf_tensor(name, shape, dt))

        def sem(name):
            return ctx.enter_context(nc.semaphore(name))

        def dram(name, shape):
            return nc.dram_tensor(name, shape, F32, kind="Internal").ap()

        psum = ctx.enter_context(nc.psum_tensor("psum", [P, 8 * 512], F32))

        def ps(bank, lo, hi, rows=P):
            return psum[0:rows, bank * 512 + lo:bank * 512 + hi]

        packed_dram = dram("packed_dram", [NP, ROW])
        o_dram = dram("o_dram", [NP, D])
        v_dram = dram("v_dram", [NP, D])
        xs_dram = dram("xs_dram", [TRASH + P, D])
        ys_dram = dram("ys_dram", [TRASH + P, D])

        ident, tri, ones = sb("ident", [P, P]), sb("tri", [P, P]), sb("ones", [P, P])
        neghalf = sb("neghalf", [P, NH])
        cst = sb("cst", [P, NCST])
        pvec = sb("pvec", [P, NPV])
        rows = sb("rows", [P, 5, D])
        brow = sb("brow", [1, 3, D])
        w4 = sb("w4", [P, 4, KD, D])
        lora_a = sb("lora_a", [P, KD, D])
        wlb, alb, glb = sb("wlb", [65, D]), sb("alb", [65, D]), sb("glb", [P, D])
        w1t = sb("w1t", [P, KD, HID])
        w2t = sb("w2t", [P, KH, D])
        w2g = sb("w2g", [P, KH, D + 1])
        wat = sb("wat", [P, 4, KD, D])
        wsh = sb("wsh", [P, KD, 2 * F])
        wsd = sb("wsd", [P, KF, D])
        wrt = sb("wrt", [P, KD, NE])
        thr, thr5 = sb("thr", [P, 1]), sb("thr5", [P, 5])
        absum = sb("absum", [P, KD + KH])
        tern = sb("tern", [P, 6])
        bc2 = sb("bc2", [P, 2, D])
        row2 = sb("row2", [1, 2, D])

        h_tok = sb("h_tok", [P, NT, D])
        xn_tok = sb("xn_tok", [P, NT, D])
        xnT = sb("xnT", [P, KD, B + NP])
        g_tok = sb("g_tok", [P, NT, D])
        bonus = sb("bonus", [P, NT, D])
        stat, mv = sb("stat", [P, NT, 6]), sb("mv", [P, NT, 2])
        ve, rstd = sb("ve", [P, NT]), sb("rstd", [P, NT])
        r1 = sb("r1", [P, 14976])
        r2 = sb("r2", [P, 10240])

        def carve(region, at, *shape):
            n = 1
            for s in shape:
                n *= s
            v = region[:, at:at + n]
            if len(shape) == 1:
                return v
            names = ["x", "y", "z", "w"][:len(shape)]
            return v.rearrange(f"p ({' '.join(names)}) -> p {' '.join(names)}",
                               **dict(zip(names, shape)))

        pack = carve(r1, 0, NT, HG, NV, CW)
        scan_in = carve(r1, NT * ROW, T * NV * CW)
        wgu = carve(r1, 0, RING, KD, 2 * F)
        wdn = carve(r1, RING * KD * 2 * F, RING, KF, D)
        tern_a, tern_b = carve(r1, 0, 2048), carve(r1, 2048, 2048)
        selT = carve(r1, 4096, NP)
        table = carve(r1, 4096 + NP, D)
        tokw = carve(r1, 4096 + NP + D, KP, D)
        xT = carve(r2, 0, KP, NP)
        state, prod, outer, decayed, kv, carried = [carve(r2, 512 * i, ST) for i in range(6)]
        sr = carve(r2, 3072, 2, ST)
        mix = carve(r2, 4096, 2, 5, KD, P)
        rT, sgT = carve(r2, 4096, KD, NP), carve(r2, 4096 + KD * NP, NP)
        delta = carve(r2, 6656, KD, P)
        lwT, laT = carve(r2, 6912, 2, P), carve(r2, 7168, 2, P)
        kk, am, sqk = carve(r2, 7424, D), carve(r2, 7680, D), carve(r2, 7936, D)
        a_tok, w_tok = carve(r2, 8192, 2, D), carve(r2, 8704, D)
        o_scan = carve(r2, 8960, T * CW)
        hgT, sqT = carve(r2, 0, KH, NP), carve(r2, KH * NP, KH, NP)
        qT, kT = carve(r2, 0, KD, B * T), carve(r2, 1216, KD * B * T)
        qm = carve(r2, 2432, 2, 864)
        wk1, wk2 = carve(r2, 4160, 5, T), carve(r2, 4350, 5, T)
        ex, keep, pm = carve(r2, 4540, 2, 5, T), carve(r2, 4920, 2, 5, T), carve(r2, 5300, 2, 5, T)
        ptS = carve(r2, 5680, 2, NP)
        vS, oS = carve(r2, 6960, 2, D), carve(r2, 7472, 2, D)
        mx = carve(r2, 7984, 2, 5, 24)
        scS = carve(r2, 8224, 2, 5, T)
        shT = carve(r2, 0, KF, NP)
        gshT = carve(r2, 2560, NP)
        xs_tok = carve(r2, 3200, NT, D)
        xsS = carve(r2, 4480, RING, D)
        xsT = carve(r2, 5504, RING, KD, C)
        sgE = carve(r2, 6272, 2, KF * C)
        actE = carve(r2, 7040, 2, KF * C)
        ysS = carve(r2, 7808, 2, D)
        ysum = carve(r2, 8320, NT, D)
        ygat = g_tok

        ss, rn = sb("ss", [P, NH]), sb("rn", [P, NH])
        sa = sb("sa", [P, CW])
        bs = sb("bs", [P, NT, NH])
        gmu, gva, grs = sb("gmu", [P, NT, NH]), sb("gva", [P, NT, NH]), sb("grs", [P, NT, NH])
        fst = sb("fst", [P, NT, 6])
        nb, cthr, rinv = sb("nb", [P, 2, 5]), sb("cthr", [P, 2, 5]), sb("rinv", [P, 2, 5])
        lg, oh, rt1 = sb("lg", [P, NT, NE]), sb("oh", [P, NT, NE]), sb("rt1", [P, NT, NE])
        rt5 = sb("rt5", [P, 8, NT])
        ex16 = sb("ex16", [P, 4, NE])
        xk = sb("xk", [P, XTRA, NE])
        slot = sb("slot", [P, NT], I32)
        ctl = sb("ctl", [P, 8], I32)
        ctlf = sb("ctlf", [P, 8])
        cell = sb("cell", [P, 2])

        l_x, l_emb, l_tern, l_rw, l_cst, l_mid, l_late = [sem(f"l_{n}") for n in
                                                      ("x", "emb", "tern", "rw", "cst", "mid", "late")]
        dve_step, act_step, pool_step, pe_step = [sem(f"{n}_step") for n in ("dve", "act", "pool", "pe")]
        consts_set = sem("consts_set")
        abs_sum, abs_row, abs_one, abs_all = [sem("abs_" + n) for n in ("sum", "row", "one", "all")]
        tern_ready, rows2_mm, rows2_set, bc2_mm, bc2_set = [sem(n) for n in (
            "tern_ready", "rows2_mm", "rows2_set", "bc2_mm", "bc2_set")]
        emb_mm = sem("emb_mm")
        h_ready, ve_ready, rstd_ready, xn_ready, xT_mm, xT_ready = [sem(n) for n in (
            "h_ready", "ve_ready", "rstd_ready", "xn_ready", "xT_mm", "xT_ready")]
        mix_ready, proj_mm, lora_ready, z_mm = [sem(n) for n in ("mix_ready", "proj_mm", "lora_ready", "z_mm")]
        rv_packed, w_packed, a_ready = [sem(n) for n in ("rv_packed", "w_packed", "a_ready")]
        kk_ready, sq_ready, ss_ready, rn_ready, k_packed = [sem(n) for n in (
            "kk_ready", "sq_ready", "ss_ready", "rn_ready", "k_packed")]
        packed_out, scan_loaded = sem("packed_out"), sem("scan_loaded")
        scan_dve, scan_pool, o_mm, o_copied = [sem(n) for n in ("scan_dve", "scan_pool", "o_mm", "o_copied")]
        o_out, o_loaded = sem("o_out"), sem("o_loaded")
        rk_ready, bs_ready, bonus_ready = [sem(n) for n in ("rk_ready", "bs_ready", "bonus_ready")]
        rT_mm, rT_ready, ga_mm, sg_ready, g_mm, g_ready = [sem(n) for n in (
            "rT_mm", "rT_ready", "ga_mm", "sg_ready", "g_mm", "g_ready")]
        cen_ready, gsq_ready, gva_ready, grs_ready, y_ready = [sem(n) for n in (
            "cen_ready", "gsq_ready", "gva_ready", "grs_ready", "y_ready")]
        yT_mm, yT_ready, wo_mm = sem("yT_mm"), sem("yT_ready"), sem("wo_mm")
        f1_mm, f1_ready, f2_mm, fv_ready, frs_ready = [sem(n) for n in (
            "f1_mm", "f1_ready", "f2_mm", "fv_ready", "frs_ready")]
        q_mm, q_ready, v_mm, v_ready, v_out = [sem(n) for n in (
            "q_mm", "q_ready", "v_mm", "v_ready", "v_out")]
        v_loaded = [sem("v_loaded0"), sem("v_loaded1")]
        qm_zero, qm_ready, sc_mm, sc_ready, nb_ready, keep_ready, exp_ready, pm_ready, rinv_ready, pn_ready = [
            sem(n) for n in ("qm_zero", "qm_ready", "sc_mm", "sc_ready", "nb_ready", "keep_ready", "exp_ready",
                             "pm_ready", "rinv_ready", "pn_ready")]
        top_step, sum_ready = sem("top_step"), sem("sum_ready")
        pt_mm, pt_ready, pv_mm, pv_ready, ot_mm, ot_ready, ao_mm = [sem(n) for n in (
            "pt_mm", "pt_ready", "pv_mm", "pv_ready", "ot_mm", "ot_ready", "ao_mm")]
        zero_out = sem("zero_out")
        lg_mm, oh_ready, score_in, score_ready, cnt_mm, slot_ready, ctl_ready = [sem(n) for n in (
            "lg_mm", "oh_ready", "score_in", "score_ready", "cnt_mm", "slot_ready", "ctl_ready")]
        xs_ready, xs_out = sem("xs_ready"), sem("xs_out")
        sh_mm, sh_silu, sh_ready, sd_mm, ysum_ready = [sem(n) for n in (
            "sh_mm", "sh_silu", "sh_ready", "sd_mm", "ysum_ready")]
        w_loaded = [sem(f"w_loaded{i}") for i in range(RING)]
        x_loaded = [sem(f"x_loaded{i}") for i in range(RING)]
        ex_mm, ex_ready, gu_mm, silu_ready, act_ready, y_mm, ys_ready = [sem(n) for n in (
            "ex_mm", "ex_ready", "gu_mm", "silu_ready", "act_ready", "y_mm", "ys_ready")]
        ys_out = [sem("ys_out0"), sem("ys_out1")]
        o_w, o_x, o_xt, o_xc, o_gu, o_silu, o_act, o_y, o_yc, o_st = [sem("over_" + n) for n in (
            "w", "x", "xt", "xc", "gu", "silu", "act", "y", "yc", "st")]
        yg_loaded = [sem(f"yg_loaded{j}") for j in range(NT)]
        res_ready, stored = sem("res_ready"), sem("stored")

        SCAN_DVE, SCAN_POOL = 6, 3
        CHUNKS = [(j, (min(TPT, T - TPT * j)) // 2) for j in range(NT)]

        def tcol(t, v):
            return scan_in[:, bass.ds(t * (NV * CW) + v * CW, CW)].rearrange("p (h j) -> p h j", h=2)

        def along_i(v):
            return v.unsqueeze(2).broadcast_to([P, 2, HD, HD])

        def along_j(v):
            return v.unsqueeze(3).broadcast_to([P, 2, HD, HD])

        def s4(v):
            return v.rearrange("p (h i j) -> p h i j", h=2, i=HD)

        def wgu_src(e):
            return a["gate_up"][e].rearrange("(k p) n -> p k n", p=P)

        def wdn_src(e):
            return a["down"][e].rearrange("(k p) n -> p k n", p=P)

        block = ctx.enter_context(nc.Block())

        @block.sync
        def _(sp):
            sp.dma_start(tokw, a["tokw"].rearrange("p (k n) -> p k n", k=KP)).then_inc(l_emb, 16)
            for k in range(KP):
                sp.dma_start(xT[:, k, 2 * B:NTOK], a["xT"][:, k * 576:(k + 1) * 576]).then_inc(l_x, 16)
            sp.dma_start(selT[0:40], a["sel"]).then_inc(l_emb, 16)
            sp.dma_start(table[0:1], a["cls_tok"]).then_inc(l_emb, 16)
            sp.dma_start(table[1:38], a["pos"]).then_inc(l_emb, 16)
            sp.dma_start(table[38:39], a["tok_b"]).then_inc(l_emb, 16)
            sp.dma_start(table[39:40], a["tok_cls"]).then_inc(l_emb, 16)
            sp.dma_start(ident[:], a["ident"]).then_inc(l_cst, 16)
            sp.dma_start(pvec[:], a["pvec"]).then_inc(l_cst, 16)
            sp.dma_start(lora_a[:], a["lora_a"].rearrange("p (k n) -> p k n", k=KD)).then_inc(l_rw, 16)
            sp.dma_start(w4[:], a["w4"].rearrange("p (w k n) -> p w k n", w=4, k=KD)).then_inc(l_rw, 16)
            sp.dma_start(wlb[0:64], a["wlb"]).then_inc(l_rw, 16)
            sp.dma_start(wlb[64:65], a["wlbias"]).then_inc(l_rw, 16)
            sp.dma_start(alb[0:64], a["alb"]).then_inc(l_rw, 16)
            sp.dma_start(alb[64:65], a["albias"]).then_inc(l_rw, 16)
            sp.dma_start(rows[:], a["rows"].broadcast_to([P, 5 * D]).rearrange("p (r n) -> p r n", r=5)).then_inc(l_rw, 16)
            sp.dma_start(glb[:], a["glb"]).then_inc(l_mid, 16)
            sp.dma_start(cst[:], a["cst"]).then_inc(l_mid, 16)
            sp.dma_start(wat[:], a["wat"].rearrange("p (w k n) -> p w k n", w=4, k=KD)).then_inc(l_mid, 16)
            sp.dma_start(tri[:], a["tri"]).then_inc(l_late, 16)
            sp.dma_start(wsh[:], a["wsh"].rearrange("p (k n) -> p k n", k=KD)).then_inc(l_late, 16)
            sp.dma_start(wsd[:], a["wsd"].rearrange("p (k n) -> p k n", k=KF)).then_inc(l_late, 16)
            sp.dma_start(wrt[:], a["wrt"].rearrange("p (k n) -> p k n", k=KD)).then_inc(l_late, 16)
            sp.dma_start(thr[:], a["thr"].broadcast_to([P, 1])).then_inc(l_late, 16)

            def repack(j):
                steps = CHUNKS[j][1] * 2
                sp.wait_ge(rv_packed, j + 1)
                sp.wait_ge(w_packed, j + 1)
                sp.wait_ge(k_packed, j + 1)
                sp.dma_start(packed_dram[j * P:(j + 1) * P], pack[:, j].rearrange("p h v c -> p (h v c)"))\
                  .then_inc(packed_out, 16)
                sp.wait_ge(packed_out, 16 * (j + 1))
                dst = scan_in[:, j * TPT * NV * CW:(j * TPT + steps) * NV * CW]
                sp.dma_start(dst.rearrange("p (t x) -> p t x", t=steps),
                             packed_dram[j * P:j * P + steps * B].rearrange("(t b) (h x) -> (b h) t x", b=B, h=HG))\
                  .then_inc(scan_loaded, 16)

            def fetch_o(j):
                steps = CHUNKS[j][1] * 2
                sp.wait_ge(o_copied, j * TPT // 2 + steps // 2 + 1)
                src = o_scan[:, j * TPT * CW:(j * TPT + steps) * CW].rearrange("p (t c) -> p t c", t=steps)
                sp.dma_start(o_dram[j * P:j * P + steps * B].rearrange("(t b) (h c) -> (b h) t c", b=B, h=HG), src)\
                  .then_inc(o_out, 16)
                sp.wait_ge(o_out, 16 * (j + 1))
                sp.wait_ge(xT_mm, j + 1)
                sp.dma_start(xn_tok[0:steps * B, j], o_dram[j * P:j * P + steps * B]).then_inc(o_loaded, 16)

            repack(0)
            for buf, first, end in ((xs_dram, 0, TRASH + P), (ys_dram, NE * C, TRASH)):
                for lo in range(first, end, P):
                    hi = min(lo + P, end)
                    sp.dma_start(buf[lo:hi], a["zero"][0:hi - lo]).then_inc(zero_out, 16)
            sp.dma_start(ys_dram[TRASH:TRASH + P], a["zero"]).then_inc(o_st, 16)
            repack(1)
            repack(2)
            repack(3)
            fetch_o(0)
            repack(4)
            for j in range(1, NT):
                fetch_o(j)

            sp.wait_ge(bonus_ready, NT)
            sp.wait_ge(scan_pool, SCAN_POOL * T + 1)
            sp.wait_ge(scan_dve, SCAN_DVE * T + 2)

            def load_w(e, s):
                sp.dma_start(wgu[:, s], wgu_src(e)).then_inc(w_loaded[s], 16)
                sp.dma_start(wdn[:, s], wdn_src(e)).then_inc(w_loaded[s], 16)

            for e in range(RING):
                load_w(e, e)
            for j in range(NT):
                sp.wait_ge(v_ready, j + 1)
                sp.dma_start(v_dram[j * P:(j + 1) * P], g_tok[:, j]).then_inc(v_out, 16)
            sp.wait_ge(v_out, 16 * NT)
            v_img = v_dram[0:NTOK].rearrange("(t b) c -> b t c", b=B)

            def load_v(n, s):
                if not isinstance(n, int) or n >= 2:
                    sp.wait_ge(pv_mm, n - 1)
                sp.dma_start(vS[0:T, s], v_img[n]).then_inc(v_loaded[s], 16)

            pipeline(sp, [(load_v, 0)], B, 2, 2)

            sp.wait_ge(xs_out, 16 * NT)

            def load_x(e, s):
                if not isinstance(e, int) or e >= RING:
                    sp.wait_ge(ex_mm, e - RING + 1)
                sp.dma_start(xsS[0:C, s], xs_dram[bass.ds(e * C, C)]).then_inc(x_loaded[s], 16)

            def load_next(e, s):
                if not isinstance(e, int) or e >= RING:
                    sp.wait_ge(y_mm, e - RING + 1)
                    load_w(e, s)

            def store_y(e, s):
                sp.wait_ge(ys_ready, e + 1)
                sp.dma_start(ys_dram[bass.ds(e * C, C)], ysS[0:C, s % 2]).then_inc(ys_out[s % 2], 16)

            pipeline(sp, [(load_x, 0), (load_next, 0), (store_y, 3)], NE, RING, RING)

            sp.wait_ge(y_mm, NE)
            sp.wait_ge(ctl_ready, 1)
            n_over = sp.value_load(ctl[0:1, XTRA:XTRA + 1], min_val=0, max_val=XTRA)
            with sp.Fori(0, n_over) as k:
                e = sp.value_load(ctl[0:1, bass.ds(k, 1)], min_val=0, max_val=NE - 1)
                sp.wait_ge(o_st, k * 16 + 16)
                sp.dma_start(wgu[:, 0], wgu_src(e)).then_inc(o_w, 16)
                sp.dma_start(wdn[:, 0], wdn_src(e)).then_inc(o_w, 16)
                sp.dma_start(xsS[0:C, 0], xs_dram[bass.ds(k * C + NE * C, C)]).then_inc(o_x, 16)
                sp.wait_ge(o_yc, k + 1)
                sp.dma_start(ys_dram[bass.ds(k * C + NE * C, C)], ysS[0:C, 0]).then_inc(o_st, 16)

            for j in range(NT):
                sp.wait_ge(res_ready, j + 1)
                n = min(P, NTOK - j * P)
                sp.dma_start(out[j * P:j * P + n], xn_tok[0:n, j]).then_inc(stored, 16)
            sp.wait_ge(stored, 16 * NT)

        @block.tensor
        def _(pe):
            mm = nc.tensor.matmul

            def layer(dst, lhs, rhs, chunks, inc=None):
                for k in range(chunks):
                    ins = mm(dst, lhs(k), rhs(k), start=(k == 0), stop=(k == chunks - 1))
                return ins

            def turn(s, j):
                pe.wait_ge(xn_ready, NT * s + j + 1)
                if NT * s + j >= 2:
                    pe.wait_ge(xT_ready, NT * s + j - 1)
                for k in range(KD):
                    ins = nc.tensor.transpose(ps(j % 2, 256 + k * P, 256 + (k + 1) * P),
                                              xn_tok[:, j, k * P:(k + 1) * P], ident[:])
                ins.then_inc(xT_mm, 1)

            pe.wait_ge(consts_set, 1)
            pe.wait_ge(l_cst, 32)
            for i, k0, kn in ((0, 0, KD), (1, KD, KH)):
                pe.wait_ge(abs_sum, i + 1)
                for k in range(kn):
                    ins = mm(ps(4 + 2 * i, k * P, (k + 1) * P, 1), absum[:, k0 + k:k0 + k + 1], ident[:],
                             start=True, stop=True)
                ins.then_inc(abs_row, 1)
            for i in range(2):
                pe.wait_ge(abs_one, i + 1)
                mm(ps(2 + i, 0, 1), ones[0:1, :], tern[0:1, 3 * i:3 * i + 1], start=True, stop=True)\
                    .then_inc(abs_all, 1)

            pe.wait_ge(l_emb, 16 * 6)
            pe.wait_ge(l_x, 16 * KP)
            for j in range(NT):
                if j >= 2:
                    pe.wait_ge(h_ready, j - 1)
                dst = ps(j % 2, 0, D)
                for k in range(KP):
                    mm(dst, xT[:, k, j * P:(j + 1) * P], tokw[:, k], start=(k == 0), stop=False)
                mm(dst, selT[0:40, j * P:(j + 1) * P], table[0:40], start=False, stop=True).then_inc(emb_mm, 1)
            pe.wait_ge(l_cst, 32)
            pe.wait_ge(h_ready, NT)
            for j in range(NT):
                turn(0, j)

            def project(j):
                if j == 0:
                    pe.wait_ge(l_rw, 16 * 7)
                pe.wait_ge(mix_ready, j + 1)
                if j >= 2:
                    pe.wait_ge(k_packed, j - 1)
                    pe.wait_ge(rv_packed, j - 1)
                    pe.wait_ge(lora_ready, j - 1)
                m = mix[:, j % 2]
                layer(ps(2 + j % 2, 0, D), lambda k: m[:, 0, k], lambda k: w4[:, 0, k], KD)
                layer(ps(2 + j % 2, D, 2 * D), lambda k: m[:, 2, k], lambda k: w4[:, 1, k], KD)
                layer(ps(4 + j % 2, 0, D), lambda k: m[:, 3, k], lambda k: w4[:, 2, k], KD)
                layer(ps(4 + j % 2, D, D + P, 64), lambda k: lora_a[:, k, 0:64], lambda k: m[:, 1, k], KD)
                layer(ps(4 + j % 2, D + P, D + 2 * P, 64), lambda k: lora_a[:, k, 64:128], lambda k: m[:, 4, k], KD)\
                    .then_inc(proj_mm, 1)

            def lora_out(j):
                pe.wait_ge(lora_ready, j + 1)
                if j >= 2:
                    pe.wait_ge(a_ready, j - 1)
                ins = mm(ps(6 + j % 2, 0, D), lwT[0:65, j % 2], wlb[:], start=True, stop=True)
                if j == 0:
                    ins.then_inc(o_mm, 1)
                mm(ps(6 + j % 2, D, 2 * D), laT[0:65, j % 2], alb[:], start=True, stop=True).then_inc(z_mm, 1)

            def scan_out(j):
                with pe.Fori(j * TPT // 2, j * TPT // 2 + CHUNKS[j][1]) as q:
                    pe.wait_ge(scan_dve, q * (2 * SCAN_DVE) + (2 * SCAN_DVE + 2))
                    pe.wait_ge(o_copied, q + 1)
                    src = sr.rearrange("p u (x j) -> p j (u x)", j=HD)
                    for jj in range(HD):
                        ins = mm(ps(0, 0, 2 * CW), ident[:], src[:, jj], start=(jj == 0), stop=(jj == HD - 1))
                    ins.then_inc(o_mm, 1)

            def gate():
                for j in range(NT):
                    pe.wait_ge(rv_packed, j + 1)
                    pe.wait_ge(a_ready, min(NT, NT + j))
                    pe.wait_ge(w_packed, NT)
                    if j >= 2:
                        pe.wait_ge(rT_ready, j - 1)
                    for k in range(KD):
                        ins = nc.tensor.transpose(ps(6 + j % 2, k * P, (k + 1) * P),
                                                  g_tok[:, j, k * P:(k + 1) * P], ident[:])
                    ins.then_inc(rT_mm, 1)
                pe.wait_ge(rT_ready, NT)
                pe.wait_ge(lora_ready, NT)
                for lo, hi in ((0, 512), (512, NP)):
                    ins = layer(psum[:, 4 * 512 + lo:4 * 512 + hi], lambda k: lora_a[:, k, P:2 * P],
                                lambda k: rT[:, k, lo:hi], KD)
                ins.then_inc(ga_mm, 1)
                pe.wait_ge(sg_ready, 1)
                pe.wait_ge(l_mid, 48)
                for j in range(NT):
                    if j >= 2:
                        pe.wait_ge(g_ready, j - 1)
                    mm(ps(6 + j % 2, 0, D), sgT[:, j * P:(j + 1) * P], glb[:], start=True, stop=False)
                    mm(ps(6 + j % 2, 0, D), ones[0:1, :], brow[0:1, 0], start=False, stop=True).then_inc(g_mm, 1)

            project(0)
            lora_out(0)
            project(1)
            lora_out(1)
            project(2)
            lora_out(2)
            scan_out(0)
            project(3)
            lora_out(3)
            scan_out(1)
            project(4)
            lora_out(4)
            scan_out(2)
            gate()
            pe.wait_ge(tern_ready, 1)
            pe.wait_ge(g_ready, NT)
            for c, col in ((0, LN2G), (1, LN2B)):
                ins = layer(ps(4 + c, 0, D, 1), lambda k: pvec[:, col + k:col + k + 1], lambda k: w2t[:, k], KH)
            ins.then_inc(rows2_mm, 1)
            pe.wait_ge(rows2_set, 1)
            for c in range(2):
                ins = mm(ps(6, c * D, (c + 1) * D), ones[0:1, :], row2[0:1, c], start=True, stop=True)
            ins.then_inc(bc2_mm, 1)
            scan_out(3)
            scan_out(4)

            for j in range(NT):
                pe.wait_ge(y_ready, j + 1)
                if j >= 2:
                    pe.wait_ge(yT_ready, j - 1)
                for k in range(KD):
                    ins = nc.tensor.transpose(ps(1 + j % 2, 256 + k * P, 256 + (k + 1) * P),
                                              xn_tok[:, j, k * P:(k + 1) * P], ident[:])
                ins.then_inc(yT_mm, 1)
                pe.wait_ge(yT_ready, j + 1)
                if j >= 2:
                    pe.wait_ge(h_ready, NT + j - 1)
                layer(ps(3 + j % 2, 0, D), lambda k: xnT[:, k, B + j * P:B + (j + 1) * P],
                      lambda k: w4[:, 3, k], KD).then_inc(wo_mm, 1)

            for j in range(NT):
                turn(1, j)
            pe.wait_ge(xT_ready, 2 * NT)
            pe.wait_ge(h_ready, 2 * NT)
            for m in range(KH):
                if m >= 3:
                    pe.wait_ge(f1_ready, m - 2)
                base = 2 * (m % 3) * 512
                for lo, hi in ((0, 512), (512, NP)):
                    ins = layer(psum[:, base + lo:base + hi], lambda k: w1t[:, k, m * P:(m + 1) * P],
                                lambda k: xnT[:, k, B + lo:B + hi], KD)
                ins.then_inc(f1_mm, 1)
            pe.wait_ge(f1_ready, KH)
            pe.wait_ge(bc2_set, 1)
            for j in range(NT):
                if j >= 2:
                    pe.wait_ge(h_ready, 2 * NT + j - 1)
                layer(ps(6 + j % 2, 0, D + 1), lambda k: hgT[:, k, j * P:(j + 1) * P], lambda k: w2g[:, k], KH)
                layer(ps(6 + j % 2, 300, 301), lambda k: sqT[:, k, j * P:(j + 1) * P],
                      lambda k: ones[:, 0:1], KH).then_inc(f2_mm, 1)

            for j in range(NT):
                turn(2, j)
            pe.wait_ge(xT_ready, 3 * NT)
            pe.wait_ge(h_ready, 3 * NT)
            for w in range(2):
                for m in range(KD):
                    base = 2 * (1 + w * KD + m if w * KD + m < 3 else 1) * 512
                    if w * KD + m == 3:
                        pe.wait_ge(q_ready, 1)
                    for lo, hi in ((0, 512), (512, NP)):
                        ins = layer(psum[:, base + lo:base + hi], lambda k: wat[:, w, k, m * P:(m + 1) * P],
                                    lambda k: xnT[:, k, B + lo:B + hi], KD)
                    ins.then_inc(q_mm, 1)
            for j in range(NT):
                if j >= 2:
                    pe.wait_ge(v_ready, j - 1)
                layer(ps(j % 2, 0, D), lambda k: xnT[:, k, B + j * P:B + (j + 1) * P],
                      lambda k: wat[:, 2, k], KD).then_inc(v_mm, 1)
            pe.wait_ge(q_ready, 4)
            pe.wait_ge(v_ready, NT)

            def plain(dst):
                mm(dst, ones[0:1, 0:64], ones[0:1, 0:1], start=True, stop=True)

            def scores(n, s):
                pe.wait_ge(qm_ready, n + 1)
                if not isinstance(n, int) or n >= 2:
                    pe.wait_ge(sc_ready, n - 1)
                key = [kT[:, bass.ds(n * T + half * (B * T), T)] for half in range(2)]
                for tile, (at, half) in enumerate(((0, 0), (128, 0), (256, 0), (512, 1), (640, 1))):
                    dst = ps(s, tile * T, (tile + 1) * T)
                    both = tile == 2
                    ins = mm(dst, qm[:, s, at:at + P], key[half], start=True, stop=not both)
                    if both:
                        ins = mm(dst, qm[:, s, 384:512], key[1], start=False, stop=True)
                ins.then_inc(sc_mm, 1)

            def turn_probs(n, s):
                pe.wait_ge(pn_ready, n + 1)
                if not isinstance(n, int) or n >= 2:
                    pe.wait_ge(pt_ready, n - 1)
                plain(ps(2 + 2 * s, 0, 1, 64))
                for tile in range(5):
                    ins = nc.tensor.transpose(ps(2 + 2 * s, tile * P, (tile + 1) * P, T), pm[:, s, tile], ident[:])
                ins.then_inc(pt_mm, 1)

            def values(n, s):
                pe.wait_ge(pt_ready, n + 1)
                pe.wait_ge(v_loaded[s], (n - s) * 8 + 16)
                if not isinstance(n, int) or n >= 2:
                    pe.wait_ge(ot_ready, n - 1)
                plain(ps(6 + s, 0, 1, 64))
                for hh in range(NH):
                    ins = mm(ps(6 + s, hh * HD, (hh + 1) * HD, T), ptS[0:T, s, hh * T:(hh + 1) * T],
                             vS[0:T, s, hh * HD:(hh + 1) * HD], start=True, stop=True)
                ins.then_inc(pv_mm, 1)

            def turn_out(n, s):
                pe.wait_ge(pv_ready, n + 1)
                plain(ps(6 + s, 256, 257, 64))
                for k in range(KD):
                    ins = nc.tensor.transpose(ps(6 + s, 256 + k * T, 256 + (k + 1) * T),
                                              oS[0:T, s, k * P:(k + 1) * P], ident[0:T, 0:T])
                ins.then_inc(ot_mm, 1)

            pipeline(pe, [(scores, 0), (turn_probs, 2), (values, 3), (turn_out, 4)], B, 2, 4)

            pe.wait_ge(ot_ready, B)
            for j in range(NT):
                if j >= 2:
                    pe.wait_ge(h_ready, 3 * NT + j - 1)
                dst = ps(2 + j % 2, 0, D)
                for k in range(KD):
                    mm(dst, xnT[:, k, B + j * P:B + (j + 1) * P], wat[:, 3, k], start=(k == 0), stop=False)
                mm(dst, ones[0:1, :], brow[0:1, 2], start=False, stop=True).then_inc(ao_mm, 1)

            pe.wait_ge(l_late, 16 * 5)
            for j in range(NT):
                turn(3, j)
                pe.wait_ge(xT_ready, 3 * NT + j + 1)
                layer(ps(6, j * NE, (j + 1) * NE), lambda k: xnT[:, k, B + j * P:B + (j + 1) * P],
                      lambda k: wrt[:, k], KD).then_inc(lg_mm, 1)
            pe.wait_ge(oh_ready, 1)
            for j in range(NT):
                dst = ps(3, j * NE, (j + 1) * NE)
                for i in range(j):
                    mm(dst, ones[:], oh[:, i], start=(i == 0), stop=False)
                mm(dst, tri[:], oh[:, j], start=(j == 0), stop=True)
            layer(ps(3, NT * NE, (NT + 1) * NE), lambda k: ones[:], lambda k: oh[:, k], NT).then_inc(cnt_mm, 1)

            for f in range(KF):
                for u in range(2):
                    n = 2 * f + u
                    bnk = (4, 6)[u]
                    if f >= 1:
                        pe.wait_ge(sh_ready, f)
                    for lo, hi in ((0, 512), (512, NP)):
                        ins = layer(psum[:, bnk * 512 + lo:bnk * 512 + hi],
                                    lambda k: wsh[:, k, u * F + f * P:u * F + (f + 1) * P],
                                    lambda k: xnT[:, k, B + lo:B + hi], KD)
                    ins.then_inc(sh_mm, 1)
            pe.wait_ge(sh_ready, KF)
            for j in range(NT):
                if j >= 2:
                    pe.wait_ge(ysum_ready, j - 1)
                layer(ps(4 + j % 2, 0, D), lambda k: shT[:, k, j * P:(j + 1) * P], lambda k: wsd[:, k], KF)\
                    .then_inc(sd_mm, 1)
            pe.wait_ge(ysum_ready, NT)

            def item_T(s, bnk=0):
                for k in range(KD):
                    ins = nc.tensor.transpose(ps(bnk, k * C, (k + 1) * C), xsS[0:C, s, k * P:(k + 1) * P],
                                              ident[0:C, 0:C])
                return ins

            def item_gu(s, u):
                for f in range(2 * KF):
                    ins = layer(ps(2 + 2 * u + f // KF, (f % KF) * C, (f % KF + 1) * C),
                                lambda k: wgu[:, s, k, f * P:(f + 1) * P], lambda k: xsT[:, s, k], KD)
                return ins

            def item_y(s, u):
                return layer(ps(6 + u, 0, D, C), lambda k: actE[:, u, k * C:(k + 1) * C],
                             lambda k: wdn[:, s, k], KF)

            def expert_T(e, s):
                pe.wait_ge(x_loaded[s], (e - s) * (16 // RING) + 16 if not isinstance(e, int) else 16 * (e // RING) + 16)
                if not isinstance(e, int) or e >= 2:
                    pe.wait_ge(ex_ready, e - 1)
                item_T(s, s % 2).then_inc(ex_mm, 1)

            def expert_gu(e, s):
                pe.wait_ge(ex_ready, e + 1)
                pe.wait_ge(w_loaded[s], (e - s) * (32 // RING) + 32 if not isinstance(e, int) else 32 * (e // RING) + 32)
                if not isinstance(e, int) or e >= 2:
                    pe.wait_ge(act_ready, e - 1)
                item_gu(s, s % 2).then_inc(gu_mm, 1)

            def expert_y(e, s):
                pe.wait_ge(act_ready, e + 1)
                if not isinstance(e, int) or e >= 2:
                    pe.wait_ge(ys_ready, e - 1)
                item_y(s, s % 2).then_inc(y_mm, 1)

            pipeline(pe, [(expert_T, 0), (expert_gu, 1), (expert_y, 2)], NE, RING, RING)
            pe.wait_ge(ys_ready, NE)
            n_over = pe.value_load(ctl[0:1, XTRA:XTRA + 1], min_val=0, max_val=XTRA)
            with pe.Fori(0, n_over) as k:
                pe.wait_ge(o_x, k * 16 + 16)
                item_T(0).then_inc(o_xt, 1)
                pe.wait_ge(o_xc, k + 1)
                pe.wait_ge(o_w, k * 32 + 32)
                item_gu(0, 0).then_inc(o_gu, 1)
                pe.wait_ge(o_act, k + 1)
                item_y(0, 0).then_inc(o_y, 1)

        @block.scalar
        def _(act):
            fn = nc.scalar.activation
            step = Link(act, act_step)
            act.dma_start(w1t[:], a["w1t"].rearrange("p (k n) -> p k n", k=KD)).then_inc(l_tern, 16)
            act.dma_start(w2t[:], a["w2t"].rearrange("p (k n) -> p k n", k=KH)).then_inc(l_tern, 16)
            act.dma_start(brow[:], a["brow"].rearrange("o (r n) -> o r n", r=3)).then_inc(l_tern, 16)

            for j in range(NT):
                act.wait_ge(emb_mm, j + 1)
                fn(h_tok[:, j], ps(j % 2, 0, D), ACT.Copy).then_inc(h_ready, 1)

            def turned(s, j):
                act.wait_ge(xT_mm, NT * s + j + 1)
                src = ps(j % 2, 256, 512).rearrange("p (k n) -> p k n", k=KD)
                dst = xnT[:, :, B + j * P:B + (j + 1) * P]
                if s == 1:
                    fn(dst[:, 0], src[:, 0], ACT.Identity, scale=pvec[:, LN1G:LN1G + 1], bias=pvec[:, LN1B:LN1B + 1])
                    fn(dst[:, 1], src[:, 1], ACT.Identity, scale=pvec[:, LN1G + 1:LN1G + 2],
                       bias=pvec[:, LN1B + 1:LN1B + 2]).then_inc(xT_ready, 1)
                else:
                    fn(dst, src, ACT.Copy).then_inc(xT_ready, 1)

            for j in range(NT):
                turned(0, j)

            def lora(j):
                act.wait_ge(proj_mm, j + 1)
                if j >= 2:
                    act.wait_ge(z_mm, j - 1)
                step(fn(lwT[0:64, j % 2], ps(4 + j % 2, D, D + P, 64), ACT.Sigmoid, scale=2.0))
                ins = fn(laT[0:64, j % 2], ps(4 + j % 2, D + P, D + 2 * P, 64), ACT.Copy)
                if j == 0:
                    ins.then_inc(o_copied, 1)
                fn(lwT[0:64, j % 2], lwT[0:64, j % 2], ACT.Copy, scale=2.0, bias=-1.0).then_inc(lora_ready, 1)
                fn(g_tok[:, j], ps(2 + j % 2, 0, D), ACT.Copy)
                fn(pack[:, j, :, PR], ps(2 + j % 2, 0, D).rearrange("p (h c) -> p h c", h=HG), ACT.Copy)
                fn(pack[:, j, :, PV], ps(4 + j % 2, 0, D).rearrange("p (h c) -> p h c", h=HG), ACT.Copy)\
                    .then_inc(rv_packed, 1)

            def gates(j):
                act.wait_ge(z_mm, j + 1)
                if j >= 2:
                    act.wait_ge(k_packed, j - 1)
                if j >= 1:
                    act.wait_ge(w_packed, j)
                fn(a_tok[:, j % 2], ps(6 + j % 2, D, 2 * D), ACT.Sigmoid).then_inc(a_ready, 1)
                step(fn(w_tok, ps(6 + j % 2, 0, D), ACT.Sigmoid))
                fn(pack[:, j, :, PW], w_tok.rearrange("p (h c) -> p h c", h=HG), ACT.Copy, scale=EXP_MINUS_HALF)\
                    .then_inc(w_packed, 1)

            def square_k(j):
                act.wait_ge(kk_ready, j + 1)
                if j >= 1:
                    act.wait_ge(ss_ready, j)
                fn(sqk, kk, ACT.Square).then_inc(sq_ready, 1)

            def scan_copy(j):
                with act.Fori(j * TPT // 2, j * TPT // 2 + CHUNKS[j][1]) as q:
                    act.wait_ge(o_mm, q + 2)
                    fn(o_scan[:, bass.ds(q * (2 * CW), 2 * CW)], ps(0, 0, 2 * CW), ACT.Copy).then_inc(o_copied, 1)

            def gate():
                for j in range(NT):
                    act.wait_ge(rT_mm, j + 1)
                    fn(rT[:, :, j * P:(j + 1) * P], ps(6 + j % 2, 0, 256).rearrange("p (k n) -> p k n", k=KD),
                       ACT.Copy).then_inc(rT_ready, 1)
                act.wait_ge(ga_mm, 1)
                fn(sgT, psum[:, 4 * 512:4 * 512 + NP], ACT.Sigmoid).then_inc(sg_ready, 1)
                for j in range(NT):
                    act.wait_ge(g_mm, j + 1)
                    fn(g_tok[:, j], ps(6 + j % 2, 0, D), ACT.Copy).then_inc(g_ready, 1)

            act.wait_ge(consts_set, 2)
            lora(0)
            gates(0)
            lora(1)
            square_k(0)
            gates(1)
            square_k(1)
            lora(2)
            gates(2)
            scan_copy(0)
            lora(3)
            square_k(2)
            gates(3)
            scan_copy(1)
            lora(4)
            square_k(3)
            gates(4)
            scan_copy(2)
            square_k(4)
            gate()
            act.wait_ge(bc2_mm, 1)
            fn(bc2[:].rearrange("p r n -> p (r n)"), ps(6, 0, 2 * D), ACT.Copy).then_inc(bc2_set, 1)
            scan_copy(3)
            scan_copy(4)

            for j in range(NT):
                act.wait_ge(cen_ready, j + 1)
                fn(mix[:, 0, j], xn_tok[:, j].rearrange("p (a b) -> p a b", a=KD), ACT.Square).then_inc(gsq_ready, 1)
            for j in range(NT):
                act.wait_ge(yT_mm, j + 1)
                fn(xnT[:, :, B + j * P:B + (j + 1) * P],
                   ps(1 + j % 2, 256, 512).rearrange("p (k n) -> p k n", k=KD), ACT.Copy).then_inc(yT_ready, 1)
            for j in range(NT):
                turned(1, j)
            for m in range(KH):
                act.wait_ge(f1_mm, m + 1)
                base = 2 * (m % 3) * 512
                step(fn(hgT[:, m], psum[:, base:base + NP], ACT.Gelu, scale=tern[:, 1:2], bias=pvec[:, B1 + m:B1 + m + 1]))
                fn(sqT[:, m], hgT[:, m], ACT.Square).then_inc(f1_ready, 1)

            for j in range(NT):
                turned(2, j)
            for w in range(2):
                for m in range(KD):
                    base = 2 * (1 + w * KD + m if w * KD + m < 3 else 1) * 512
                    dst = qT[:, m] if w == 0 else kT[:, m * B * T:(m + 1) * B * T]
                    act.wait_ge(q_mm, w * KD + m + 1)
                    fn(dst.rearrange("p (b t) -> p b t", b=B),
                       psum[:, base:base + NTOK].rearrange("p (t b) -> p b t", b=B), ACT.Copy).then_inc(q_ready, 1)
            for j in range(NT):
                act.wait_ge(v_mm, j + 1)
                fn(g_tok[:, j], ps(j % 2, 0, D), ACT.Copy).then_inc(v_ready, 1)

            def copy_scores(n, s):
                act.wait_ge(sc_mm, n + 1)
                if not isinstance(n, int) or n >= 2:
                    act.wait_ge(keep_ready, n - 1)
                    act.wait_ge(exp_ready, n - 1)
                fn(scS[:, s].rearrange("p i k -> p (i k)"), ps(s, 0, 5 * T), ACT.Copy).then_inc(sc_ready, 1)

            def exps(n, s):
                act.wait_ge(nb_ready, n + 1)
                if not isinstance(n, int) or n >= 2:
                    act.wait_ge(pm_ready, n - 1)
                for tile in range(5):
                    ins = fn(ex[:, s, tile], scS[:, s, tile], ACT.Exp, scale=0.25,
                             bias=nb[:, s, tile:tile + 1])
                ins.then_inc(exp_ready, 1)

            def copy_probs(n, s):
                act.wait_ge(pt_mm, n + 1)
                if not isinstance(n, int) or n >= 2:
                    act.wait_ge(pv_mm, n - 1)
                fn(ptS[0:T, s, 0:NTOK], psum[0:T, (2 + 2 * s) * 512:(2 + 2 * s) * 512 + NTOK], ACT.Copy)\
                    .then_inc(pt_ready, 1)

            def copy_o(n, s):
                act.wait_ge(pv_mm, n + 1)
                if not isinstance(n, int) or n >= 2:
                    act.wait_ge(ot_mm, n - 1)
                fn(oS[0:T, s], ps(6 + s, 0, D, T), ACT.Copy).then_inc(pv_ready, 1)

            def copy_oT(n, s):
                act.wait_ge(ot_mm, n + 1)
                for k in range(KD):
                    flat = xnT[:].rearrange("p k n -> p (k n)")
                    dst = flat[:, bass.DynSlice(n + (B + k * (B + NP)), T, step=B)]
                    ins = fn(dst, ps(6 + s, 256 + k * T, 256 + (k + 1) * T), ACT.Copy)
                ins.then_inc(ot_ready, 1)

            pipeline(act, [(copy_scores, 0), (exps, 0), (copy_probs, 2), (copy_o, 3), (copy_oT, 4)], B, 2, 4)

            for j in range(NT):
                turned(3, j)
            act.wait_ge(lg_mm, NT)
            fn(lg[:].rearrange("p j e -> p (j e)"), ps(6, 0, NT * NE), ACT.Copy).then_inc(score_in, 1)
            act.wait_ge(score_in, 2)
            fn(rt5[:, 1], rt5[:, 0], ACT.Sigmoid).then_inc(score_ready, 1)
            act.wait_ge(score_ready, 1)
            act.wait_ge(h_ready, 4 * NT)
            for j in range(NT):
                ins = fn(xs_tok[:, j], xn_tok[:, j], ACT.Copy, scale=rt5[:, 1, j:j + 1])
            ins.then_inc(xs_ready, 1)
            for f in range(KF):
                act.wait_ge(sh_mm, 2 * f + 1)
                if f >= 1:
                    act.wait_ge(sh_ready, f)
                fn(gshT, psum[:, 4 * 512:4 * 512 + NP], ACT.Silu).then_inc(sh_silu, 1)

            def item_xT(s, bnk=0):
                return fn(xsT[:, s], ps(bnk, 0, KD * C).rearrange("p (k n) -> p k n", k=KD), ACT.Copy)

            def expert_xT(e, s):
                act.wait_ge(ex_mm, e + 1)
                if not isinstance(e, int) or e >= RING:
                    act.wait_ge(gu_mm, e - RING + 1)
                item_xT(s, s % 2).then_inc(ex_ready, 1)

            def expert_silu(e, s):
                act.wait_ge(gu_mm, e + 1)
                if not isinstance(e, int) or e >= 2:
                    act.wait_ge(act_ready, e - 1)
                fn(sgE[:, s % 2], ps(2 + 2 * (s % 2), 0, KF * C), ACT.Silu).then_inc(silu_ready, 1)

            def expert_copy(e, s):
                act.wait_ge(y_mm, e + 1)
                if isinstance(e, int):
                    if e >= 2:
                        act.wait_ge(ys_out[s % 2], 16 * (e // 2))
                else:
                    act.wait_ge(ys_out[s % 2], (e - s % 2) * 8)
                fn(ysS[0:C, s % 2], ps(6 + s % 2, 0, D, C), ACT.Copy).then_inc(ys_ready, 1)

            pipeline(act, [(expert_xT, 0), (expert_silu, 1), (expert_copy, 2)], NE, RING, RING)
            act.wait_ge(ys_out[0], 8 * NE)
            n_over = act.value_load(ctl[0:1, XTRA:XTRA + 1], min_val=0, max_val=XTRA)
            with act.Fori(0, n_over) as k:
                act.wait_ge(o_xt, k + 1)
                item_xT(0).then_inc(o_xc, 1)
                act.wait_ge(o_gu, k + 1)
                fn(sgE[:, 0], ps(2, 0, KF * C), ACT.Silu).then_inc(o_silu, 1)
                act.wait_ge(o_y, k + 1)
                fn(ysS[0:C, 0], ps(6, 0, D, C), ACT.Copy).then_inc(o_yc, 1)

        @block.vector
        def _(dve):
            v = nc.vector
            step = Link(dve, dve_step)
            v.memset(ones[:], 1.0).then_inc(consts_set, 1)
            v.memset(xnT[:, :, 0:B], 0.0)
            v.memset(neghalf[:], -0.5)
            v.memset(w2g[:, :, D:D + 1], 1.0)
            v.memset(xT[:, :, 0:2 * B], 0.0)
            v.memset(xT[:, :, NTOK:NP], 0.0)
            v.memset(lwT[64:65], 1.0)
            v.memset(laT[64:65], 1.0).then_inc(consts_set, 1)

            dve.wait_ge(l_tern, 48)
            flat = (w1t[:].rearrange("p k n -> p (k n)"), w2t[:].rearrange("p k n -> p (k n)"))
            for i, k0, kn, wt in ((0, 0, KD, w1t), (1, KD, KH, w2t)):
                v.tensor_reduce(absum[:, k0:k0 + kn], wt[:], X, ALU.add, apply_absolute_value=True)\
                    .then_inc(abs_sum, 1)
            for i, kn in ((0, KD), (1, KH)):
                dve.wait_ge(abs_row, i + 1)
                row = psum[0:1, (4 + 2 * i) * 512:(4 + 2 * i) * 512 + kn * P]
                v.tensor_reduce(tern[0:1, 3 * i:3 * i + 1], row, X, ALU.add).then_inc(abs_one, 1)
            for i in range(2):
                w, c = flat[i], 3 * i
                dve.wait_ge(abs_all, i + 1)
                step(v.tensor_scalar(tern[:, c + 1:c + 2], ps(2 + i, 0, 1), 1.0 / (HID * D), 1e-5, ALU.mult, ALU.max))
                step(v.reciprocal(tern[:, c + 2:c + 3], tern[:, c + 1:c + 2]))
                v.tensor_scalar(tern_a, w, tern[:, c + 2:c + 3], 0.5, ALU.mult, ALU.is_gt)
                step(v.tensor_scalar(tern_b, w, tern[:, c + 2:c + 3], -0.5, ALU.mult, ALU.is_lt))
                step(v.tensor_tensor(w, tern_a, tern_b, ALU.subtract))
            dve.wait_ge(l_cst, 32)
            for k in range(KH):
                ins = v.tensor_scalar(w2g[:, k, 0:D], w2t[:, k], pvec[:, LN2G + k:LN2G + k + 1], None, ALU.mult)
            ins.then_inc(tern_ready, 1)

            def ln_stats(s, j):
                dve.wait_ge(h_ready, NT * s + j + 1)
                step(v.bn_stats(stat[:, j], h_tok[:, j]))
                step(v.bn_aggr(mv[:, j], stat[:, j]))
                if s == 1:
                    v.tensor_scalar(ve[:, j:j + 1], mv[:, j, 1:2], 1.0 + EPS, EPS * EPS, ALU.mult, ALU.add)\
                        .then_inc(ve_ready, 1)
                else:
                    v.tensor_scalar(ve[:, j:j + 1], mv[:, j, 1:2], EPS, None, ALU.add).then_inc(ve_ready, 1)

            def ln_apply(s, j):
                dve.wait_ge(rstd_ready, NT * s + j + 1)
                v.tensor_scalar(xn_tok[:, j], h_tok[:, j], mv[:, j, 0:1], rstd[:, j:j + 1], ALU.subtract, ALU.mult)\
                    .then_inc(xn_ready, 1)

            def layernorm(s, before=None):
                for j in range(NT + 1):
                    if j < NT:
                        if before:
                            before(j)
                        ln_stats(s, j)
                    if j >= 1:
                        ln_apply(s, j - 1)

            layernorm(0)

            def mixes(j):
                dve.wait_ge(xT_ready, j + 1)
                now = xnT[:, :, B + j * P:B + (j + 1) * P]
                if j >= 1:
                    dve.wait_ge(mix_ready, j)
                step(v.tensor_tensor(delta, xnT[:, :, j * P:(j + 1) * P], now, ALU.subtract))
                if j >= 2:
                    dve.wait_ge(proj_mm, j - 1)
                for m in range(5):
                    for k in range(KD):
                        ins = v.scalar_tensor_tensor(mix[:, j % 2, m, k], delta[:, k],
                                                     pvec[:, MIX + 2 * m + k:MIX + 2 * m + k + 1], now[:, k],
                                                     ALU.mult, ALU.add)
                ins.then_inc(mix_ready, 1)

            def hc(x):
                return x.rearrange("p (h c) -> p h c", h=HG)

            def hoc(x):
                return x.rearrange("p (h o c) -> p h o c", h=HG, o=2)

            def keys(j):
                psk = ps(2 + j % 2, D, 2 * D)
                dve.wait_ge(rv_packed, j + 1)
                v.tensor_tensor(kk, psk, rows[:, KK_], ALU.mult).then_inc(kk_ready, 1)
                dve.wait_ge(a_ready, j + 1)
                step(v.scalar_tensor_tensor(am, a_tok[:, j % 2], -1.0, rows[:, KA_], ALU.add, ALU.mult))
                v.scalar_tensor_tensor(pack[:, j, :, PK], hc(am), 1.0, hc(psk), ALU.add, ALU.mult)
                dve.wait_ge(sq_ready, j + 1)
                step(v.tensor_reduce(ss[:], sqk.rearrange("p (h d) -> p h d", h=NH), X, ALU.add))
                v.tensor_scalar(ss[:], ss[:], 1e-24, None, ALU.max).then_inc(ss_ready, 1)
                dve.wait_ge(rn_ready, j + 1)
                step(v.tensor_scalar(rn[:], rn[:], -1.0, None, ALU.mult))
                dst = pack[:, j, :, PA]
                step(v.tensor_tensor(dst.rearrange("p h (o c) -> p h o c", o=2), hoc(kk),
                                     rn[:].rearrange("p (h o) -> p h o", h=HG).unsqueeze(3).broadcast_to([P, HG, 2, HD]),
                                     ALU.mult))
                v.scalar_tensor_tensor(pack[:, j, :, PB], dst, -1.0, hc(a_tok[:, j % 2]), ALU.mult, ALU.mult)\
                    .then_inc(k_packed, 1)

            def scan(j):
                dve.wait_ge(scan_loaded, 16 * (j + 1))
                if j == 0:
                    dve.wait_ge(scan_dve, 2)
                with dve.Fori(j * TPT // 2, j * TPT // 2 + CHUNKS[j][1]) as q:
                    for u in range(2):
                        t = q * 2 + u
                        base = q * (2 * SCAN_DVE) + u * SCAN_DVE
                        dve.wait_ge(scan_dve, base + 1)
                        v.tensor_tensor(s4(prod), s4(state), along_i(tcol(t, PA)), ALU.mult).then_inc(scan_dve, 1)
                        dve.wait_ge(scan_dve, base + 3)
                        v.tensor_reduce(sa[:], prod.rearrange("p (x j) -> p x j", j=HD), X, ALU.add)\
                            .then_inc(scan_dve, 1)
                        v.tensor_tensor(kv[:, 0:256].rearrange("p (i j) -> p i j", i=HD),
                                        tcol(t, PV)[:, 0].unsqueeze(2).broadcast_to([P, HD, HD]),
                                        tcol(t, PK)[:, 0].unsqueeze(1).broadcast_to([P, HD, HD]), ALU.mult)\
                            .then_inc(scan_dve, 1)
                        dve.wait_ge(scan_dve, base + 5)
                        v.tensor_tensor(s4(outer), along_j(sa[:].rearrange("p (h i) -> p h i", h=2)),
                                        along_i(tcol(t, PB)), ALU.mult).then_inc(scan_dve, 1)
                        dve.wait_ge(scan_dve, base + 6)
                        dve.wait_ge(scan_pool, q * (2 * SCAN_POOL) + ((u + 1) * SCAN_POOL + 1))
                        v.tensor_tensor(state, outer, carried, ALU.add).then_inc(scan_dve, 1)
                        dve.wait_ge(scan_dve, base + 7)
                        if u == 0:
                            dve.wait_ge(o_mm, q + 1)
                        v.tensor_tensor(s4(sr[:, u]), s4(state), along_i(tcol(t, PR)), ALU.mult).then_inc(scan_dve, 1)

            dve.wait_ge(l_rw, 16 * 7)
            mixes(0)
            mixes(1)
            keys(0)
            mixes(2)
            keys(1)
            dve.wait_ge(emb_mm, NT)
            for head in range(2):
                v.memset(state[:, head * HD * HD:(head + 1) * HD * HD], 0.0).then_inc(scan_dve, 1)
            scan(0)
            mixes(3)
            keys(2)
            scan(1)
            mixes(4)
            keys(3)
            scan(2)
            keys(4)
            dve.wait_ge(rows2_mm, 1)
            v.tensor_copy(row2[0:1, 0], ps(4, 0, D, 1))
            v.scalar_tensor_tensor(row2[0:1, 1], ps(5, 0, D, 1), tern[0:1, 4:5], brow[0:1, 1], ALU.mult, ALU.add)\
                .then_inc(rows2_set, 1)
            scan(3)
            scan(4)

            for j in range(NT):
                dve.wait_ge(rk_ready, j + 1)
                v.tensor_reduce(bs[:, j], bonus[:, j].rearrange("p (h d) -> p h d", h=NH), X, ALU.add)\
                    .then_inc(bs_ready, 1)

            def heads(x):
                return x.rearrange("p (h d) -> p h d", h=NH)

            def spread(x):
                return x.unsqueeze(2).broadcast_to([P, NH, HD])

            for j in range(NT):
                dve.wait_ge(o_loaded, 16 * (j + 1))
                o = heads(xn_tok[:, j])
                step(v.tensor_reduce(gmu[:, j], o, X, ALU.add))
                v.scalar_tensor_tensor(o, spread(gmu[:, j]), -1.0 / HD, o, ALU.mult, ALU.add).then_inc(cen_ready, 1)
            for j in range(NT):
                dve.wait_ge(gsq_ready, j + 1)
                step(v.tensor_reduce(gva[:, j], mix[:, 0, j].rearrange("p a (h d) -> p (a h) d", d=HD), X, ALU.add))
                v.tensor_scalar(gva[:, j], gva[:, j], 1.0 / HD, EPS, ALU.mult, ALU.add).then_inc(gva_ready, 1)
            for j in range(NT):
                y = xn_tok[:, j]
                dve.wait_ge(grs_ready, j + 1)
                step(v.tensor_tensor(heads(y), heads(y), spread(grs[:, j]), ALU.mult))
                step(v.tensor_tensor(y, y, rows[:, GNW], ALU.mult))
                dve.wait_ge(bonus_ready, j + 1)
                step(v.tensor_tensor(y, y, bonus[:, j], ALU.add))
                dve.wait_ge(g_ready, j + 1)
                v.tensor_tensor(y, y, g_tok[:, j], ALU.mult).then_inc(y_ready, 1)

            def add_to_h(src):
                def add(j):
                    src_ap, s, n = src(j)
                    dve.wait_ge(s, n)
                    v.tensor_tensor(h_tok[:, j], h_tok[:, j], src_ap, ALU.add).then_inc(h_ready, 1)
                return add

            layernorm(1, add_to_h(lambda j: (ps(3 + j % 2, 0, D), wo_mm, j + 1)))

            def ffn_stats(j):
                dve.wait_ge(f2_mm, j + 1)
                b = 6 + j % 2
                v.tensor_scalar(fst[:, j, 0:1], ps(b, D, D + 1), -1.0 / HID, None, ALU.mult)
                step(v.tensor_scalar(fst[:, j, 1:2], ps(b, 300, 301), 1.0 / HID, EPS, ALU.mult, ALU.add))
                step(v.tensor_tensor(fst[:, j, 2:3], fst[:, j, 0:1], fst[:, j, 0:1], ALU.mult))
                v.tensor_tensor(fst[:, j, 3:4], fst[:, j, 1:2], fst[:, j, 2:3], ALU.subtract).then_inc(fv_ready, 1)
                step(v.scalar_tensor_tensor(xn_tok[:, j], bc2[:, 0], fst[:, j, 0:1], ps(b, 0, D), ALU.mult, ALU.add))

            def ffn_apply(j):
                dve.wait_ge(frs_ready, j + 1)
                step(v.tensor_tensor(fst[:, j, 5:6], fst[:, j, 4:5], tern[:, 4:5], ALU.mult))
                step(v.scalar_tensor_tensor(xn_tok[:, j], xn_tok[:, j], fst[:, j, 5:6], bc2[:, 1], ALU.mult, ALU.add))
                v.tensor_tensor(h_tok[:, j], h_tok[:, j], xn_tok[:, j], ALU.add).then_inc(h_ready, 1)

            dve.wait_ge(bc2_set, 1)
            dve.wait_ge(xT_mm, 2 * NT)
            for j in range(NT):
                ffn_stats(j)
                ffn_apply(j)
            layernorm(2)

            dve.wait_ge(l_late, 16 * 5)
            dve.wait_ge(f2_mm, NT)
            v.memset(qm, 0.0).then_inc(qm_zero, 1)
            step(v.tensor_scalar(thr[:], thr[:], 0.0, 1.0, ALU.max, ALU.min))
            step(v.tensor_scalar(thr[:], thr[:], 4.0, None, ALU.mult))
            step(v.tensor_scalar(thr5[:], cst[:, C_PADROW:C_PADROW + 5], thr[:], None, ALU.add))

            def plain():
                v.memset(cell[:, 0:1], 0.0)

            def first(n, k):
                return isinstance(n, int) and n < k

            def keep_mask(n, s):
                v.tensor_tensor(keep[:, s], scS[:, s], cthr[:, s].unsqueeze(2).broadcast_to([P, 5, T]), ALU.is_ge)\
                    .then_inc(keep_ready, 1)

            def sum_probs(n, s):
                dve.wait_ge(pm_ready, n + 1)
                v.tensor_reduce(rinv[:, s], pm[:, s], X, ALU.add).then_inc(sum_ready, 1)

            def invert_sums(n, s):
                dve.wait_ge(sum_ready, n + 1)
                v.reciprocal(rinv[:, s], rinv[:, s]).then_inc(rinv_ready, 1)

            def topk(n, s):
                sc = [scS[:, s, i] for i in range(5)]
                done = lambda c: dve.wait_ge(top_step, n * 6 + c)
                dve.wait_ge(sc_ready, n + 1)
                if first(n, 1):
                    plain()
                else:
                    done(0)
                    keep_mask(n - 1, 1 - s)
                for i in range(5):
                    ins = v.max(mx[:, s, i, 0:8], sc[i])
                ins.then_inc(top_step, 1)
                done(1)
                v.tensor_scalar(nb[:, s], mx[:, s, :, 0], -0.25, None, ALU.mult).then_inc(nb_ready, 1)
                for i in range(5):
                    ins = v.match_replace(wk1[:, i], mx[:, s, i, 0:8], sc[i], NEG)
                ins.then_inc(top_step, 1)
                done(2)
                plain() if first(n, 1) else sum_probs(n - 1, 1 - s)
                for i in range(5):
                    ins = v.max(mx[:, s, i, 8:16], wk1[:, i])
                ins.then_inc(top_step, 1)
                done(3)
                plain() if first(n, 1) else invert_sums(n - 1, 1 - s)
                for i in range(5):
                    ins = v.match_replace(wk2[:, i], mx[:, s, i, 8:16], wk1[:, i], NEG)
                ins.then_inc(top_step, 1)
                done(4)
                plain()
                for i in range(5):
                    ins = v.max(mx[:, s, i, 16:24], wk2[:, i])
                ins.then_inc(top_step, 1)
                done(5)
                v.tensor_tensor(cthr[:, s], mx[:, s, :, KEEP - 1], thr5[:], ALU.max).then_inc(top_step, 1)

            pipeline(dve, [(topk, 0)], B, 2, 2)
            dve.wait_ge(top_step, 6 * B)
            keep_mask(B - 1, 1)
            sum_probs(B - 1, 1)
            invert_sums(B - 1, 1)

            layernorm(3, add_to_h(lambda j: (ps(2 + j % 2, 0, D), ao_mm, j + 1)))

            def wide(x, n=NE):
                return x.unsqueeze(2).broadcast_to([P, NT, n])

            em = cst[:, C_E:C_E + NE].unsqueeze(1).broadcast_to([P, NT, NE])
            dve.wait_ge(score_in, 1)
            step(v.tensor_reduce(rt5[:, 0], lg[:], X, ALU.max))
            step(v.tensor_tensor(rt1[:], lg[:], wide(rt5[:, 0]), ALU.is_equal))
            v.tensor_tensor(rt1[:], rt1[:], em, ALU.mult).then_inc(score_in, 1)
            dve.wait_ge(score_in, 2)
            step(v.tensor_reduce(rt5[:, 2], rt1[:], X, ALU.min))
            step(v.tensor_tensor(oh[:], em, wide(rt5[:, 2]), ALU.is_equal))
            valid = cst[:, C_VALID:C_VALID + NT]
            v.tensor_tensor(oh[:], oh[:], wide(valid), ALU.mult).then_inc(oh_ready, 1)
            dve.wait_ge(cnt_mm, 1)
            dve.wait_ge(oh_ready, 1)
            step(v.tensor_tensor(rt1[:], oh[:], ps(3, 0, NT * NE).rearrange("p (j e) -> p j e", j=NT), ALU.mult))
            step(v.tensor_reduce(rt5[:, 3], rt1[:], X, ALU.add))
            cnt = ps(3, NT * NE, (NT + 1) * NE)
            step(v.tensor_scalar(ex16[:, 0], cnt, float(C), None, ALU.is_gt))
            for m in range(2, XTRA + 1):
                step(v.scalar_tensor_tensor(ex16[:, 0], cnt, float(C * m), ex16[:, 0], ALU.is_gt, ALU.add))
            step(v.tensor_tensor_scan(ex16[:, 1], ones[:, 0:NE], ex16[:, 0], 0.0, ALU.mult, ALU.add))
            step(v.tensor_tensor(ex16[:, 2], ex16[:, 1], ex16[:, 0], ALU.subtract))
            step(v.tensor_tensor(rt1[:], oh[:], ex16[:, 2].unsqueeze(1).broadcast_to([P, NT, NE]), ALU.mult))
            step(v.tensor_reduce(rt5[:, 4], rt1[:], X, ALU.add))
            step(v.tensor_scalar(rt5[:, 4], rt5[:, 4], float(NE - 1), None, ALU.add))
            v.tensor_scalar(rt5[:, 5], rt5[:, 2], float(NE), None, ALU.add)
            step(v.tensor_scalar(rt5[:, 6], rt5[:, 3], float(C), None, ALU.is_lt))
            step(v.tensor_tensor(rt5[:, 5], rt5[:, 5], rt5[:, 4], ALU.subtract))
            step(v.tensor_tensor(rt5[:, 5], rt5[:, 5], rt5[:, 6], ALU.mult))
            step(v.tensor_tensor(rt5[:, 5], rt5[:, 5], rt5[:, 4], ALU.add))
            step(v.scalar_tensor_tensor(rt5[:, 5], rt5[:, 5], float(C), rt5[:, 3], ALU.mult, ALU.add))
            step(v.tensor_tensor(rt5[:, 5], rt5[:, 5], valid, ALU.mult))
            v.tensor_tensor(slot[:], rt5[:, 5], cst[:, C_TROW:C_TROW + NT], ALU.add).then_inc(slot_ready, 1)
            step(v.tensor_tensor(xk[:], ex16[:, 1].unsqueeze(1).broadcast_to([P, XTRA, NE]),
                                 cst[:, C_K:C_K + XTRA].unsqueeze(2).broadcast_to([P, XTRA, NE]), ALU.is_le))
            step(v.tensor_reduce(ctlf[:, 0:XTRA], xk[:], X, ALU.add))
            step(v.tensor_scalar(ctlf[:, 0:XTRA], ctlf[:, 0:XTRA], float(NE - 1), None, ALU.min))
            v.tensor_copy(ctlf[:, XTRA:XTRA + 1], ex16[:, 1, NE - 1:NE])
            step(v.tensor_copy(ctl[:, 0:XTRA], ctlf[:, 0:XTRA]))
            v.tensor_copy(ctl[:, XTRA:XTRA + 1], ctlf[:, XTRA:XTRA + 1]).then_inc(ctl_ready, 1)

            for f in range(KF):
                dve.wait_ge(sh_silu, f + 1)
                dve.wait_ge(sh_mm, 2 * f + 2)
                v.tensor_tensor(shT[:, f], gshT, psum[:, 6 * 512:6 * 512 + NP], ALU.mult).then_inc(sh_ready, 1)
            for j in range(NT):
                dve.wait_ge(sd_mm, j + 1)
                v.tensor_tensor(ysum[:, j], h_tok[:, j], ps(4 + j % 2, 0, D), ALU.add).then_inc(ysum_ready, 1)

            def expert_act(e, s):
                dve.wait_ge(silu_ready, e + 1)
                if not isinstance(e, int) or e >= 2:
                    dve.wait_ge(y_mm, e - 1)
                v.tensor_tensor(actE[:, s % 2], sgE[:, s % 2], ps(3 + 2 * (s % 2), 0, KF * C), ALU.mult)\
                    .then_inc(act_ready, 1)

            pipeline(dve, [(expert_act, 0)], NE, RING, RING)
            dve.wait_ge(y_mm, NE)
            n_over = dve.value_load(ctl[0:1, XTRA:XTRA + 1], min_val=0, max_val=XTRA)
            with dve.Fori(0, n_over) as k:
                dve.wait_ge(o_silu, k + 1)
                v.tensor_tensor(actE[:, 0], sgE[:, 0], ps(3, 0, KF * C), ALU.mult).then_inc(o_act, 1)
            for j in range(NT):
                dve.wait_ge(yg_loaded[j], 16)
                v.tensor_tensor(xn_tok[:, j], ysum[:, j], ygat[:, j], ALU.add).then_inc(res_ready, 1)

        @block.gpsimd
        def _(pool):
            g = nc.gpsimd
            pool.wait_ge(consts_set, 2)
            g.memset(cell[:, 1:2], 0.0).then_inc(scan_pool, 1)

            def ln_pow(s, j):
                pool.wait_ge(ve_ready, NT * s + j + 1)
                g.tensor_tensor(rstd[:, j:j + 1], ve[:, j:j + 1], neghalf[:, 0:1], ALU.pow).then_inc(rstd_ready, 1)

            for j in range(NT):
                ln_pow(0, j)

            def key_pow(j):
                pool.wait_ge(ss_ready, j + 1)
                g.tensor_tensor(rn[:], ss[:], neghalf[:], ALU.pow).then_inc(rn_ready, 1)

            def rk(j):
                pool.wait_ge(k_packed, j + 1)
                pool.wait_ge(rv_packed, j + 1)
                dst = bonus[:, j].rearrange("p (h c) -> p h c", h=HG)
                g.tensor_tensor(dst, pack[:, j, :, PR], pack[:, j, :, PK], ALU.mult).then_inc(pool_step, 1)
                pool.wait_ge(pool_step, j + 1)
                g.tensor_tensor(bonus[:, j], bonus[:, j], rows[:, RK_], ALU.mult).then_inc(rk_ready, 1)

            def scan(j):
                pool.wait_ge(scan_loaded, 16 * (j + 1))
                if j == 0:
                    pool.wait_ge(scan_dve, 2)
                with pool.Fori(j * TPT // 2, j * TPT // 2 + CHUNKS[j][1]) as q:
                    for u in range(2):
                        t = q * 2 + u
                        done = q * (2 * SCAN_POOL) + (u * SCAN_POOL + 1)
                        pool.wait_ge(scan_pool, done)
                        g.tensor_tensor(kv[:, 256:512].rearrange("p (i j) -> p i j", i=HD),
                                        tcol(t, PV)[:, 1].unsqueeze(2).broadcast_to([P, HD, HD]),
                                        tcol(t, PK)[:, 1].unsqueeze(1).broadcast_to([P, HD, HD]), ALU.mult)\
                            .then_inc(scan_pool, 1)
                        pool.wait_ge(scan_dve, q * (2 * SCAN_DVE) + (u * SCAN_DVE + 1))
                        g.tensor_tensor(s4(decayed), s4(state), along_i(tcol(t, PW)), ALU.mult).then_inc(scan_pool, 1)
                        pool.wait_ge(scan_pool, done + 2)
                        pool.wait_ge(scan_dve, q * (2 * SCAN_DVE) + (u * SCAN_DVE + 5))
                        g.tensor_tensor(carried, decayed, kv, ALU.add).then_inc(scan_pool, 1)

            key_pow(0)
            key_pow(1)
            scan(0)
            rk(0)
            key_pow(2)
            scan(1)
            rk(1)
            key_pow(3)
            scan(2)
            rk(2)
            key_pow(4)
            scan(3)
            rk(3)
            scan(4)
            rk(4)
            for j in range(NT):
                pool.wait_ge(bs_ready, j + 1)
                g.tensor_tensor(bonus[:, j].rearrange("p (h o c) -> p h o c", h=HG, o=2),
                                pack[:, j, :, PV].rearrange("p h (o c) -> p h o c", o=2),
                                bs[:, j].rearrange("p (h o) -> p h o", h=HG).unsqueeze(3).broadcast_to([P, HG, 2, HD]),
                                ALU.mult).then_inc(pool_step, 1)
                pool.wait_ge(pool_step, NT + j + 1)
                g.tensor_tensor(bonus[:, j], bonus[:, j], rows[:, GNB], ALU.add).then_inc(bonus_ready, 1)
            for j in range(NT):
                pool.wait_ge(gva_ready, j + 1)
                g.tensor_tensor(grs[:, j], gva[:, j], neghalf[:], ALU.pow).then_inc(grs_ready, 1)
            for j in range(NT):
                ln_pow(1, j)
            for j in range(NT):
                pool.wait_ge(fv_ready, j + 1)
                g.tensor_tensor(fst[:, j, 4:5], fst[:, j, 3:4], neghalf[:, 0:1], ALU.pow).then_inc(frs_ready, 1)
            for j in range(NT):
                ln_pow(2, j)

            pool.wait_ge(qm_zero, 1)
            pool.wait_ge(q_ready, 2)
            pool.wait_ge(l_mid, 48)
            mask = cst[:, C_HM:C_HM + HG].unsqueeze(1).unsqueeze(3).broadcast_to([P, KD, HG, T])

            def mask_q(n, s):
                if not isinstance(n, int) or n >= 2:
                    pool.wait_ge(sc_mm, n - 1)
                src = qT[:, :, bass.ds(n * T, T)].unsqueeze(2).broadcast_to([P, KD, HG, T])
                dst = qm[:, s].rearrange("p (k n) -> p k n", k=KD)[:, :, 0:HG * T]
                g.tensor_tensor(dst.rearrange("p k (h q) -> p k h q", h=HG), src, mask, ALU.mult)\
                    .then_inc(qm_ready, 1)

            def mask_p(n, s):
                pool.wait_ge(exp_ready, n + 1)
                pool.wait_ge(keep_ready, n + 1)
                if not isinstance(n, int) or n >= 2:
                    pool.wait_ge(pt_mm, n - 1)
                g.tensor_tensor(pm[:, s], ex[:, s], keep[:, s], ALU.mult).then_inc(pm_ready, 1)

            def norm_p(n, s):
                pool.wait_ge(rinv_ready, n + 1)
                g.tensor_tensor(pm[:, s], pm[:, s], rinv[:, s].unsqueeze(2).broadcast_to([P, 5, T]), ALU.mult)\
                    .then_inc(pn_ready, 1)

            def probs(n, s):
                mask_p(n, s)
                if not isinstance(n, int) or n + 2 < B:
                    mask_q(n + 2, s)
                norm_p(n, s)

            mask_q(0, 0)
            mask_q(1, 1)
            pipeline(pool, [(probs, 0)], B - 2, 2, 2)
            probs(B - 2, 0)
            probs(B - 1, 1)

            for j in range(NT):
                ln_pow(3, j)
            pool.wait_ge(slot_ready, 1)
            pool.wait_ge(xs_ready, 1)
            n_zero = -(-(TRASH + P) // P) + -(-(TRASH - NE * C) // P)
            pool.wait_ge(zero_out, 16 * n_zero)
            for j in range(NT):
                g.indirect_dma_start(xs_dram, bass.IndirectOffsetOnAxis(slot[:, j:j + 1], 0), xs_tok[:, j], None)\
                    .then_inc(xs_out, 16)
                pool.wait_ge(xs_out, 16 * (j + 1))
            pool.wait_ge(ctl_ready, 1)
            n_over = pool.value_load(ctl[0:1, XTRA:XTRA + 1], min_val=0, max_val=XTRA)
            pool.wait_ge(ys_out[0], 8 * NE)
            pool.wait_ge(ys_out[1], 8 * NE)
            pool.wait_ge(o_st, n_over * 16 + 16)
            g.tensor_tensor(cell[:, 1:2], neghalf[:, 0:1], neghalf[:, 0:1], ALU.add)
            for j in range(NT):
                g.indirect_dma_start(ygat[:, j], None, ys_dram, bass.IndirectOffsetOnAxis(slot[:, j:j + 1], 0))\
                    .then_inc(yg_loaded[j], 16)


def kernel(x, cls_tok, **w):
    import numpy as np
    import concourse.bacc as bacc
    from concourse import mybir as mb
    from concourse.bass_utils import run_bass_kernel_spmd

    def chunks(m):
        k, n = m.shape
        return m.reshape(k // P, P, n).transpose(1, 0, 2).reshape(P, -1)

    def cols(v):
        return v.reshape(-1, P).T

    t0, a0, f0, a1, f1 = "L0_tok_", "L0_attn_", "L0_ffn_", "L1_attn_", "L1_ffn_"
    w = {k: np.asarray(m) for k, m in w.items()}
    x = np.asarray(x)
    patches = x.reshape(B, 3, 6, 16, 6, 16).transpose(1, 3, 5, 2, 4, 0).reshape(768, 36 * B)
    sel = np.zeros((40, NP), np.float32)
    for n in range(NTOK):
        sel[n // B, n] = 1
        if n // B == 1:
            sel[39, n] = 1
        if n // B >= 2:
            sel[38, n] = 1
    cst = np.zeros((P, NCST), np.float32)
    cst[NH * T - 4 * P:, C_PADROW + 4] = NEG
    cst[:, C_E:C_E + NE] = np.arange(NE) - NE
    tok = np.arange(NP).reshape(NT, P).T
    cst[:, C_VALID:C_VALID + NT] = tok < NTOK
    cst[:, C_TROW:C_TROW + NT] = np.where(tok < NTOK, 0, TRASH + tok - NTOK)
    cst[:, C_K:C_K + XTRA] = np.arange(XTRA)
    cst[:, C_HM:C_HM + HG] = np.arange(P)[:, None] // HD == np.arange(HG)
    arrays = {
        "xT": chunks(patches),
        "tokw": chunks(w[t0 + "W"].T),
        "cls_tok": np.asarray(cls_tok).reshape(1, D),
        "pos": w[t0 + "pos_embedding"].reshape(T - 1, D),
        "tok_b": w[t0 + "b"].reshape(1, D),
        "tok_cls": w[t0 + "cls_token"].reshape(1, D),
        "sel": sel,
        "ident": np.eye(P, dtype=np.float32),
        "tri": np.triu(np.ones((P, P), np.float32), 1),
        "cst": cst,
        "zero": np.zeros((P, D), np.float32),
        "pvec": np.concatenate([cols(w[a0 + n]) for n in ("x_r", "x_w", "x_k", "x_v", "x_a")]
                               + [cols(w[f0 + n]) for n in ("ln1_g", "ln1_b", "b1", "ln2_g", "ln2_b")], 1),
        "rows": np.concatenate([w[a0 + n].reshape(-1) for n in ("k_k", "k_a", "r_k", "gn_weight", "gn_bias")])[None],
        "brow": np.concatenate([w[a0 + "g_lora_bias"], w[f0 + "b2"], w[a1 + "bo"]])[None],
        "w4": np.concatenate([chunks(w[a0 + n]) for n in ("W_r", "W_k", "W_v", "W_o")], 1),
        "lora_a": chunks(np.concatenate([w[a0 + n + "_lora_a"] for n in "wag"], 1)),
        "wlb": w[a0 + "w_lora_b"], "wlbias": w[a0 + "w_lora_bias"][None],
        "alb": w[a0 + "a_lora_b"], "albias": w[a0 + "a_lora_bias"][None],
        "glb": w[a0 + "g_lora_b"],
        "w1t": chunks(w[f0 + "w1"].T), "w2t": chunks(w[f0 + "w2"].T),
        "wat": np.concatenate([chunks(w[a1 + n].T) for n in ("Wq", "Wk", "Wv", "Wo")], 1),
        "thr": w[a1 + "adaptive_threshold"].reshape(1, 1),
        "wrt": chunks(w[f1 + "w_router"].T),
        "gate_up": w[f1 + "gate_up_proj"], "down": w[f1 + "down_proj"],
        "wsh": chunks(np.concatenate([w[f1 + "w_gate"].T, w[f1 + "w_up"].T], 1)),
        "wsd": chunks(w[f1 + "w_down"].T),
    }
    arrays = {n: np.ascontiguousarray(m) for n, m in arrays.items()}
    nc = bacc.Bacc("TRN2", target_bir_lowering=False, num_devices=1)
    arrays = {"in_" + n: m for n, m in arrays.items()}
    args = {n[3:]: nc.dram_tensor(n, m.shape, mb.dt.from_np(m.dtype), kind="ExternalInput").ap()
            for n, m in arrays.items()}
    out = nc.dram_tensor("out", [NTOK, D], F32, kind="ExternalOutput").ap()
    build(nc, args, out)
    r = run_bass_kernel_spmd(nc, [arrays], core_ids=[0])
    return r.results[0]["out"].reshape(T, B, D).transpose(1, 0, 2)
```

```python
from contextlib import ExitStack

import concourse.bass as bass
from concourse import mybir

P = 128
B = 16
T = 38
D = 256
NT = 5
NP = NT * P
NTOK = B * T
TPT = P // B
NH, HD = 16, 16
KD = D // P
KP = 768 // P
HID = 1024
KH = HID // P
NE, F = 16, 512
KF = F // P
KEEP = T // 2
C = 80
RING = 4
XTRA = -(-(NTOK // (C + 1)) // RING) * RING
TRASH = (NE + XTRA) * C
EPS = 1e-5
EXP_MINUS_HALF = 0.6065306597126334
NEG = -3.0e38
PA, PW, PB, PK, PV, PR = range(6)
NV = 6
HG = 8
CW = D // HG
ST = 2 * HD * HD
ROW = HG * NV * CW

F32 = mybir.dt.float32
I32 = mybir.dt.int32
ALU = mybir.AluOpType
ACT = mybir.ActivationFunctionType
X = mybir.AxisListType.X

MIX, LN1G, LN1B, B1, LN2G, LN2B, NPV = 0, 10, 12, 14, 22, 30, 38
C_E, C_VALID, C_TROW, C_K, C_HM, C_PADROW, NCST = 0, 16, 21, 26, 34, 42, 47
KK_, KA_, RK_, GNW, GNB = range(5)


class Link:

    def __init__(self, eng, sem):
        self.eng, self.sem, self.n = eng, sem, 0

    def __call__(self, ins):
        self.n += 1
        ins.then_inc(self.sem, 1)
        self.eng.wait_ge(self.sem, self.n)


def pipeline(eng, stages, count, unroll, peel):
    last = max(lag for _, lag in stages)
    assert peel % unroll == 0 and count % unroll == 0 and peel >= last
    for k in range(peel):
        for fn, lag in stages:
            if k >= lag:
                fn(k - lag, (k - lag) % unroll)
    with eng.Fori(peel // unroll, count // unroll) as i:
        for u in range(unroll):
            for fn, lag in stages:
                fn(i * unroll + (u - lag), (u - lag) % unroll)
    for k in range(count, count + last):
        for fn, lag in stages:
            if k - lag < count:
                fn(k - lag, (k - lag) % unroll)


def pipeline_rings(eng, stages, more):
    for k in range(RING):
        for fn, lag in stages:
            if k >= lag:
                fn(k - lag, k - lag)
    with eng.Fori(1, more + NE // RING) as i:
        for u in range(RING):
            for fn, lag in stages:
                fn(i * RING + (u - lag), (u - lag) % RING)
    for k in range(max(lag for _, lag in stages)):
        for fn, lag in stages:
            if k < lag:
                fn(more * RING + (NE + k - lag), (k - lag) % RING)


def build(nc, a, out):
    with ExitStack() as ctx:
        def sb(name, shape, dt=F32):
            return ctx.enter_context(nc.sbuf_tensor(name, shape, dt))

        def sem(name):
            return ctx.enter_context(nc.semaphore(name))

        def dram(name, shape):
            return nc.dram_tensor(name, shape, F32, kind="Internal").ap()

        psum = ctx.enter_context(nc.psum_tensor("psum", [P, 8 * 512], F32))

        def ps(bank, lo, hi, rows=P):
            return psum[0:rows, bank * 512 + lo:bank * 512 + hi]

        packed_dram = dram("packed_dram", [NP, ROW])
        o_dram = dram("o_dram", [NP, D])
        v_dram = dram("v_dram", [NP, D])
        xs_dram = dram("xs_dram", [TRASH + P, D])
        ys_dram = dram("ys_dram", [TRASH + P, D])

        ident, tri, ones = sb("ident", [P, P]), sb("tri", [P, P]), sb("ones", [P, P])
        neghalf = sb("neghalf", [P, NH])
        cst = sb("cst", [P, NCST])
        pvec = sb("pvec", [P, NPV])
        rows = sb("rows", [P, 5, D])
        brow = sb("brow", [1, 3, D])
        w4 = sb("w4", [P, 4, KD, D])
        lora_a = sb("lora_a", [P, KD, D])
        wlb, alb, glb = sb("wlb", [65, D]), sb("alb", [65, D]), sb("glb", [P, D])
        w1t = sb("w1t", [P, KD, HID])
        w2t = sb("w2t", [P, KH, D])
        w2g = sb("w2g", [P, KH, D + 1])
        wat = sb("wat", [P, 4, KD, D])
        wsh = sb("wsh", [P, KD, 2 * F])
        wsd = sb("wsd", [P, KF, D])
        wrt = sb("wrt", [P, KD, NE])
        thr, thr5 = sb("thr", [P, 1]), sb("thr5", [P, 5])
        absum = sb("absum", [P, KD + KH])
        tern = sb("tern", [P, 6])
        bc2 = sb("bc2", [P, 2, D])
        row2 = sb("row2", [1, 2, D])

        h_tok = sb("h_tok", [P, NT, D])
        xn_tok = sb("xn_tok", [P, NT, D])
        xnT = sb("xnT", [P, KD, B + NP])
        g_tok = sb("g_tok", [P, NT, D])
        bonus = sb("bonus", [P, NT, D])
        stat, mv = sb("stat", [P, NT, 6]), sb("mv", [P, NT, 2])
        ve, rstd = sb("ve", [P, NT]), sb("rstd", [P, NT])
        r1 = sb("r1", [P, 14976])
        r2 = sb("r2", [P, 10240])

        def carve(region, at, *shape):
            n = 1
            for s in shape:
                n *= s
            v = region[:, at:at + n]
            if len(shape) == 1:
                return v
            names = ["x", "y", "z", "w"][:len(shape)]
            return v.rearrange(f"p ({' '.join(names)}) -> p {' '.join(names)}",
                               **dict(zip(names, shape)))

        pack = carve(r1, 0, NT, HG, NV, CW)
        scan_in = carve(r1, NT * ROW, T * NV * CW)
        wgu = carve(r1, 0, RING, KD, 2 * F)
        wdn = carve(r1, RING * KD * 2 * F, RING, KF, D)
        selT = carve(r1, 4096, NP)
        table = carve(r1, 4096 + NP, D)
        tokw = carve(r1, 4096 + NP + D, KP, D)
        xT = carve(r2, 0, KP, NP)
        state, prod, outer, decayed, kv, carried = [carve(r2, 512 * i, ST) for i in range(6)]
        sr = sb("sr", [P, 2, 2, ST])
        mix = carve(r2, 4096, 2, 5, KD, P)
        rT, sgT = carve(r2, 4096, KD, NP), carve(r2, 4096 + KD * NP, NP)
        delta = carve(r2, 6656, KD, P)
        lwT, laT = carve(r2, 6912, 2, P), carve(r2, 7168, 2, P)
        kk, am, sqk = carve(r2, 7424, D), carve(r2, 7680, D), carve(r2, 7936, D)
        a_tok, w_tok = carve(r2, 8192, 2, D), carve(r2, 8704, D)
        o_scan = carve(r2, 8960, T * CW)
        gsq = carve(r2, 0, NT, D)
        hgT, sqT = carve(r2, 0, KH, NP), carve(r2, KH * NP, KH, NP)
        qT, kT = carve(r2, 0, KD, B * T), carve(r2, 1216, KD * B * T)
        qm = carve(r2, 2432, 2, 864)
        wk1, wk2 = carve(r2, 4160, 5, T), carve(r2, 4350, 5, T)
        ex, keep, pm = carve(r2, 4540, 2, 5, T), carve(r2, 4920, 2, 5, T), carve(r2, 5300, 2, 5, T)
        ptS = carve(r2, 5680, 2, NP)
        vS, oS = carve(r2, 6960, 2, D), carve(r2, 7472, 2, D)
        mx = carve(r2, 7984, 2, 5, 24)
        scS = carve(r2, 8224, 2, 5, T)
        shT = carve(r2, 0, KF, NP)
        gshT = carve(r2, 2560, NP)
        xs_tok = carve(r2, 3200, NT, D)
        xsS = carve(r2, 4480, RING, D)
        xsT = carve(r2, 5504, RING, KD, C)
        sgE = carve(r2, 6272, 2, KF * C)
        actE = carve(r2, 7040, 2, KF * C)
        ysS = carve(r2, 7808, 2, D)
        ysum = carve(r2, 8320, NT, D)
        ygat = g_tok

        ss, rn = sb("ss", [P, NH]), sb("rn", [P, NH])
        sa = sb("sa", [P, CW])
        bs = sb("bs", [P, NT, NH])
        gmu, gva, grs = sb("gmu", [P, NT, NH]), sb("gva", [P, NT, NH]), sb("grs", [P, NT, NH])
        fst = sb("fst", [P, NT, 6])
        nb, cthr, rinv = sb("nb", [P, 2, 5]), sb("cthr", [P, 2, 5]), sb("rinv", [P, 2, 5])
        lg, oh, rt1 = sb("lg", [P, NT, NE]), sb("oh", [P, NT, NE]), sb("rt1", [P, NT, NE])
        rt5 = sb("rt5", [P, 8, NT])
        ex16 = sb("ex16", [P, 4, NE])
        xk = sb("xk", [P, XTRA, NE])
        slot = sb("slot", [P, NT], I32)
        ctl = sb("ctl", [P, NE + XTRA + 1], I32)
        ctlf = sb("ctlf", [P, NE + XTRA + 1])
        cell = sb("cell", [P, 2])

        l_x = [sem(f"l_x{j}") for j in range(NT)]
        l_emb, l_tern, l_rw, l_cst, l_mid, l_late = [sem(f"l_{n}") for n in
                                                     ("emb", "tern", "rw", "cst", "mid", "late")]
        dve_step, act_step, pool_step, pe_step = [sem(f"{n}_step") for n in ("dve", "act", "pool", "pe")]
        consts_set = sem("consts_set")
        abs_sum, abs_row, abs_one, abs_all = [sem("abs_" + n) for n in ("sum", "row", "one", "all")]
        tern_ready, rows2_mm, rows2_set, bc2_mm, bc2_set = [sem(n) for n in (
            "tern_ready", "rows2_mm", "rows2_set", "bc2_mm", "bc2_set")]
        emb_mm = sem("emb_mm")
        h_ready, ve_ready, rstd_ready, xn_ready, xT_mm, xT_ready = [sem(n) for n in (
            "h_ready", "ve_ready", "rstd_ready", "xn_ready", "xT_mm", "xT_ready")]
        mix_ready, proj_mm, lora_ready, z_mm = [sem(n) for n in ("mix_ready", "proj_mm", "lora_ready", "z_mm")]
        rv_packed, w_packed, a_ready = [sem(n) for n in ("rv_packed", "w_packed", "a_ready")]
        kk_ready, sq_ready, ss_ready, rn_ready, k_packed = [sem(n) for n in (
            "kk_ready", "sq_ready", "ss_ready", "rn_ready", "k_packed")]
        packed_out, scan_loaded = sem("packed_out"), sem("scan_loaded")
        scan_dve, scan_pool, o_mm, o_copied = [sem(n) for n in ("scan_dve", "scan_pool", "o_mm", "o_copied")]
        o_out, o_loaded = sem("o_out"), sem("o_loaded")
        rk_ready, bs_ready, bonus_ready = [sem(n) for n in ("rk_ready", "bs_ready", "bonus_ready")]
        rT_mm, rT_ready, ga_mm, sg_ready, g_mm, g_ready = [sem(n) for n in (
            "rT_mm", "rT_ready", "ga_mm", "sg_ready", "g_mm", "g_ready")]
        cen_ready, gsq_ready, gva_ready, grs_ready, y_ready = [sem(n) for n in (
            "cen_ready", "gsq_ready", "gva_ready", "grs_ready", "y_ready")]
        sqsum_ready = sem("sqsum_ready")
        yT_mm, yT_ready, wo_mm = sem("yT_mm"), sem("yT_ready"), sem("wo_mm")
        f1_mm, f1_ready, f2_mm, fv_ready, frs_ready = [sem(n) for n in (
            "f1_mm", "f1_ready", "f2_mm", "fv_ready", "frs_ready")]
        q_mm, q_ready, v_mm, v_ready, v_out = [sem(n) for n in (
            "q_mm", "q_ready", "v_mm", "v_ready", "v_out")]
        v_loaded = [sem("v_loaded0"), sem("v_loaded1")]
        qm_zero, qm_ready, sc_mm, sc_ready, nb_ready, keep_ready, exp_ready, pm_ready, rinv_ready, pn_ready = [
            sem(n) for n in ("qm_zero", "qm_ready", "sc_mm", "sc_ready", "nb_ready", "keep_ready", "exp_ready",
                             "pm_ready", "rinv_ready", "pn_ready")]
        top_step, sum_ready = sem("top_step"), sem("sum_ready")
        pt_mm, pt_ready, pv_mm, pv_ready, ot_mm, ot_ready, ao_mm = [sem(n) for n in (
            "pt_mm", "pt_ready", "pv_mm", "pv_ready", "ot_mm", "ot_ready", "ao_mm")]
        zero_out = sem("zero_out")
        lg_mm, oh_ready, score_in, score_ready, cnt_mm, slot_ready, ctl_ready = [sem(n) for n in (
            "lg_mm", "oh_ready", "score_in", "score_ready", "cnt_mm", "slot_ready", "ctl_ready")]
        xs_ready = sem("xs_ready")
        xs_out = [sem(f"xs_out{j}") for j in range(NT)]
        sh_mm, sh_silu, sh_ready, sd_mm, ysum_ready = [sem(n) for n in (
            "sh_mm", "sh_silu", "sh_ready", "sd_mm", "ysum_ready")]
        w_loaded = [sem(f"w_loaded{i}") for i in range(RING)]
        x_loaded = [sem(f"x_loaded{i}") for i in range(RING)]
        ex_mm, ex_ready, gu_mm, silu_ready, act_ready, y_mm, ys_ready = [sem(n) for n in (
            "ex_mm", "ex_ready", "gu_mm", "silu_ready", "act_ready", "y_mm", "ys_ready")]
        ys_out = [sem("ys_out0"), sem("ys_out1")]
        yg_loaded = [sem(f"yg_loaded{j}") for j in range(NT)]
        res_ready, stored = sem("res_ready"), sem("stored")

        SCAN_DVE, SCAN_POOL = 6, 3
        CHUNKS = [(j, (min(TPT, T - TPT * j)) // 2) for j in range(NT)]

        def tcol(t, v):
            return scan_in[:, bass.ds(t * (NV * CW) + v * CW, CW)].rearrange("p (h j) -> p h j", h=2)

        def along_i(v):
            return v.unsqueeze(2).broadcast_to([P, 2, HD, HD])

        def along_j(v):
            return v.unsqueeze(3).broadcast_to([P, 2, HD, HD])

        def s4(v):
            return v.rearrange("p (h i j) -> p h i j", h=2, i=HD)

        def wgu_src(e):
            return a["gate_up"][e].rearrange("(k p) n -> p k n", p=P)

        def wdn_src(e):
            return a["down"][e].rearrange("(k p) n -> p k n", p=P)

        block = ctx.enter_context(nc.Block())

        @block.sync
        def _(sp):
            def load_patches(j):
                lo, hi = max(2 * B, j * P), min(NTOK, (j + 1) * P)
                src = a["xT"][:, KP * (lo - 2 * B):KP * (hi - 2 * B)]
                sp.dma_start(xT[:, :, lo:hi], src.rearrange("p (k n) -> p k n", k=KP)).then_inc(l_x[j], 16)

            load_patches(0)
            sp.dma_start(tokw, a["tokw"].rearrange("p (k n) -> p k n", k=KP)).then_inc(l_emb, 16)
            sp.dma_start(selT[0:40], a["sel"]).then_inc(l_emb, 16)
            sp.dma_start(table[0:1], a["cls_tok"]).then_inc(l_emb, 16)
            sp.dma_start(table[1:38], a["pos"]).then_inc(l_emb, 16)
            sp.dma_start(table[38:39], a["tok_b"]).then_inc(l_emb, 16)
            sp.dma_start(table[39:40], a["tok_cls"]).then_inc(l_emb, 16)
            for j in range(1, NT):
                load_patches(j)
            sp.dma_start(ident[:], a["ident"]).then_inc(l_cst, 16)
            sp.dma_start(pvec[:], a["pvec"]).then_inc(l_cst, 16)
            sp.dma_start(lora_a[:], a["lora_a"].rearrange("p (k n) -> p k n", k=KD)).then_inc(l_rw, 16)
            sp.dma_start(w4[:], a["w4"].rearrange("p (w k n) -> p w k n", w=4, k=KD)).then_inc(l_rw, 16)
            sp.dma_start(wlb[0:64], a["wlb"]).then_inc(l_rw, 16)
            sp.dma_start(wlb[64:65], a["wlbias"]).then_inc(l_rw, 16)
            sp.dma_start(alb[0:64], a["alb"]).then_inc(l_rw, 16)
            sp.dma_start(alb[64:65], a["albias"]).then_inc(l_rw, 16)
            sp.dma_start(rows[:], a["rows"].broadcast_to([P, 5 * D]).rearrange("p (r n) -> p r n", r=5)).then_inc(l_rw, 16)
            sp.dma_start(w1t[:], a["w1t"].rearrange("p (k n) -> p k n", k=KD)).then_inc(l_tern, 16)
            sp.dma_start(w2t[:], a["w2t"].rearrange("p (k n) -> p k n", k=KH)).then_inc(l_tern, 16)
            sp.dma_start(brow[:], a["brow"].rearrange("o (r n) -> o r n", r=3)).then_inc(l_tern, 16)
            sp.dma_start(glb[:], a["glb"]).then_inc(l_mid, 16)
            sp.dma_start(cst[:], a["cst"]).then_inc(l_mid, 16)
            sp.dma_start(wat[:], a["wat"].rearrange("p (w k n) -> p w k n", w=4, k=KD)).then_inc(l_mid, 16)
            sp.dma_start(tri[:], a["tri"]).then_inc(l_late, 16)
            sp.dma_start(wsh[:], a["wsh"].rearrange("p (k n) -> p k n", k=KD)).then_inc(l_late, 16)
            sp.dma_start(wsd[:], a["wsd"].rearrange("p (k n) -> p k n", k=KF)).then_inc(l_late, 16)
            sp.dma_start(wrt[:], a["wrt"].rearrange("p (k n) -> p k n", k=KD)).then_inc(l_late, 16)
            sp.dma_start(thr[:], a["thr"].broadcast_to([P, 1])).then_inc(l_late, 16)

            def repack(j):
                steps = CHUNKS[j][1] * 2
                sp.wait_ge(rv_packed, j + 1)
                sp.wait_ge(w_packed, j + 1)
                sp.wait_ge(k_packed, j + 1)
                sp.dma_start(packed_dram[j * P:(j + 1) * P], pack[:, j].rearrange("p h v c -> p (h v c)"))\
                  .then_inc(packed_out, 16)
                sp.wait_ge(packed_out, 16 * (j + 1))
                dst = scan_in[:, j * TPT * NV * CW:(j * TPT + steps) * NV * CW]
                sp.dma_start(dst.rearrange("p (t x) -> p t x", t=steps),
                             packed_dram[j * P:j * P + steps * B].rearrange("(t b) (h x) -> (b h) t x", b=B, h=HG))\
                  .then_inc(scan_loaded, 16)

            def fetch_o(j):
                steps = CHUNKS[j][1] * 2
                sp.wait_ge(o_copied, j * TPT // 2 + steps // 2 + 1)
                src = o_scan[:, j * TPT * CW:(j * TPT + steps) * CW].rearrange("p (t c) -> p t c", t=steps)
                sp.dma_start(o_dram[j * P:j * P + steps * B].rearrange("(t b) (h c) -> (b h) t c", b=B, h=HG), src)\
                  .then_inc(o_out, 16)
                sp.wait_ge(o_out, 16 * (j + 1))
                sp.wait_ge(xT_mm, j + 1)
                sp.dma_start(xn_tok[0:steps * B, j], o_dram[j * P:j * P + steps * B]).then_inc(o_loaded, 16)

            repack(0)
            for buf, first, end in ((xs_dram, 0, TRASH + P), (ys_dram, NE * C, TRASH + P)):
                for lo in range(first, end, P):
                    hi = min(lo + P, end)
                    sp.dma_start(buf[lo:hi], a["zero"][0:hi - lo]).then_inc(zero_out, 16)
            repack(1)
            repack(2)
            repack(3)
            fetch_o(0)
            repack(4)
            for j in range(1, NT):
                fetch_o(j)

            sp.wait_ge(bonus_ready, NT)
            sp.wait_ge(scan_pool, SCAN_POOL * T + 1)
            sp.wait_ge(scan_dve, SCAN_DVE * T + 2)

            def load_w(e, s):
                sp.dma_start(wgu[:, s], wgu_src(e)).then_inc(w_loaded[s], 16)
                sp.dma_start(wdn[:, s], wdn_src(e)).then_inc(w_loaded[s], 16)

            for e in range(RING):
                load_w(e, e)
            for j in range(NT):
                sp.wait_ge(v_ready, j + 1)
                sp.dma_start(v_dram[j * P:(j + 1) * P], g_tok[:, j]).then_inc(v_out, 16)
            sp.wait_ge(v_out, 16 * NT)
            v_img = v_dram[0:NTOK].rearrange("(t b) c -> b t c", b=B)

            def load_v(n, s):
                if not isinstance(n, int) or n >= 2:
                    sp.wait_ge(pv_mm, n - 1)
                sp.dma_start(vS[0:T, s], v_img[n]).then_inc(v_loaded[s], 16)

            pipeline(sp, [(load_v, 0)], B, 2, 2)

            sp.wait_ge(ctl_ready, 1)
            more = sp.value_load(ctl[0:1, NE + XTRA:NE + XTRA + 1], min_val=0, max_val=XTRA // RING)
            for j in range(NT):
                sp.wait_ge(xs_out[j], 16)

            def load_x(e, s):
                if not isinstance(e, int) or e >= RING:
                    sp.wait_ge(ex_mm, e - RING + 1)
                sp.dma_start(xsS[0:C, s], xs_dram[bass.ds(e * C, C)]).then_inc(x_loaded[s], 16)

            def load_next(e, s):
                if not isinstance(e, int) or e >= RING:
                    expert = sp.value_load(ctl[0:1, bass.ds(e, 1)], min_val=0, max_val=NE - 1)
                    sp.wait_ge(y_mm, e - RING + 1)
                    load_w(expert, s)

            def store_y(e, s):
                sp.wait_ge(ys_ready, e + 1)
                sp.dma_start(ys_dram[bass.ds(e * C, C)], ysS[0:C, s % 2]).then_inc(ys_out[s % 2], 16)

            pipeline_rings(sp, [(load_x, 0), (load_next, 0), (store_y, 3)], more)

            for j in range(NT):
                sp.wait_ge(res_ready, j + 1)
                n = min(P, NTOK - j * P)
                sp.dma_start(out[j * P:j * P + n], xn_tok[0:n, j]).then_inc(stored, 16)
            sp.wait_ge(stored, 16 * NT)

        @block.tensor
        def _(pe):
            mm = nc.tensor.matmul

            def layer(dst, lhs, rhs, chunks, inc=None):
                for k in range(chunks):
                    ins = mm(dst, lhs(k), rhs(k), start=(k == 0), stop=(k == chunks - 1))
                return ins

            def turn(s, j):
                pe.wait_ge(xn_ready, NT * s + j + 1)
                if NT * s + j >= 2:
                    pe.wait_ge(xT_ready, NT * s + j - 1)
                for k in range(KD):
                    ins = nc.tensor.transpose(ps(j % 2, 256 + k * P, 256 + (k + 1) * P),
                                              xn_tok[:, j, k * P:(k + 1) * P], ident[:])
                ins.then_inc(xT_mm, 1)

            pe.wait_ge(consts_set, 2)

            def abs_row_of(i, bank, k0, kn):
                pe.wait_ge(abs_sum, i + 1)
                for k in range(kn):
                    ins = mm(ps(bank, k * P, (k + 1) * P, 1), absum[:, k0 + k:k0 + k + 1], ident[:],
                             start=True, stop=True)
                ins.then_inc(abs_row, 1)

            def abs_to_all(i, bank):
                pe.wait_ge(abs_one, i + 1)
                mm(ps(bank, 0, 1), ones[0:1, :], tern[0:1, 3 * i:3 * i + 1], start=True, stop=True)\
                    .then_inc(abs_all, 1)

            pe.wait_ge(l_emb, 16 * 6)
            for j in range(NT):
                pe.wait_ge(l_x[j], 16)
                if j >= 2:
                    pe.wait_ge(h_ready, j - 1)
                dst = ps(j % 2, 0, D)
                for k in range(KP):
                    mm(dst, xT[:, k, j * P:(j + 1) * P], tokw[:, k], start=(k == 0), stop=False)
                mm(dst, selT[0:40, j * P:(j + 1) * P], table[0:40], start=False, stop=True).then_inc(emb_mm, 1)
            pe.wait_ge(l_cst, 32)
            pe.wait_ge(h_ready, NT)
            for j in range(NT):
                turn(0, j)

            def project(j):
                if j == 0:
                    pe.wait_ge(l_rw, 16 * 7)
                pe.wait_ge(mix_ready, j + 1)
                if j >= 2:
                    pe.wait_ge(k_packed, j - 1)
                    pe.wait_ge(rv_packed, j - 1)
                    pe.wait_ge(lora_ready, j - 1)
                m = mix[:, j % 2]
                layer(ps(2 + j % 2, 0, D), lambda k: m[:, 0, k], lambda k: w4[:, 0, k], KD)
                layer(ps(2 + j % 2, D, 2 * D), lambda k: m[:, 2, k], lambda k: w4[:, 1, k], KD)
                layer(ps(4 + j % 2, 0, D), lambda k: m[:, 3, k], lambda k: w4[:, 2, k], KD)
                layer(ps(4 + j % 2, D, D + P, 64), lambda k: lora_a[:, k, 0:64], lambda k: m[:, 1, k], KD)
                layer(ps(4 + j % 2, D + P, D + 2 * P, 64), lambda k: lora_a[:, k, 64:128], lambda k: m[:, 4, k], KD)\
                    .then_inc(proj_mm, 1)

            def lora_out(j):
                pe.wait_ge(lora_ready, j + 1)
                if j >= 2:
                    pe.wait_ge(a_ready, j - 1)
                ins = mm(ps(6 + j % 2, 0, D), lwT[0:65, j % 2], wlb[:], start=True, stop=True)
                if j == 0:
                    ins.then_inc(o_mm, 1)
                mm(ps(6 + j % 2, D, 2 * D), laT[0:65, j % 2], alb[:], start=True, stop=True).then_inc(z_mm, 1)

            def scan_out(j):
                def pair(q, ready, slot):
                    pe.wait_ge(scan_dve, q * (2 * SCAN_DVE) + ready)
                    pe.wait_ge(o_copied, q + 1)
                    src = sr[:, slot].rearrange("p u (x j) -> p j (u x)", j=HD)
                    for jj in range(HD):
                        ins = mm(ps(0, 0, 2 * CW), ident[:], src[:, jj], start=(jj == 0), stop=(jj == HD - 1))
                    ins.then_inc(o_mm, 1)

                lo, n = j * TPT // 2, CHUNKS[j][1]
                with pe.Fori(0, (n - 1) // 2) as i:
                    for slot in range(2):
                        pair(i * 2 + (lo + slot), 2 * SCAN_DVE + 5, slot)
                if n % 2 == 0:
                    pair(lo + n - 2, 2 * SCAN_DVE + 5, 0)
                pair(lo + n - 1, 2 * SCAN_DVE + 2, (n - 1) % 2)

            def gate_turn():
                for j in range(NT):
                    pe.wait_ge(rv_packed, j + 1)
                    pe.wait_ge(a_ready, NT)
                    pe.wait_ge(w_packed, NT)
                    if j >= 2:
                        pe.wait_ge(rT_ready, j - 1)
                    for k in range(KD):
                        ins = nc.tensor.transpose(ps(6 + j % 2, k * P, (k + 1) * P),
                                                  g_tok[:, j, k * P:(k + 1) * P], ident[:])
                    ins.then_inc(rT_mm, 1)

            def gate_hidden():
                pe.wait_ge(rT_ready, NT)
                pe.wait_ge(lora_ready, NT)
                for lo, hi in ((0, 512), (512, NP)):
                    ins = layer(psum[:, 4 * 512 + lo:4 * 512 + hi], lambda k: lora_a[:, k, P:2 * P],
                                lambda k: rT[:, k, lo:hi], KD)
                ins.then_inc(ga_mm, 1)

            def gate():
                pe.wait_ge(sg_ready, 1)
                pe.wait_ge(l_mid, 48)
                for j in range(NT):
                    if j >= 2:
                        pe.wait_ge(g_ready, j - 1)
                    mm(ps(6 + j % 2, 0, D), sgT[:, j * P:(j + 1) * P], glb[:], start=True, stop=False)
                    mm(ps(6 + j % 2, 0, D), ones[0:1, :], brow[0:1, 0], start=False, stop=True).then_inc(g_mm, 1)

            project(0)
            lora_out(0)
            project(1)
            lora_out(1)
            project(2)
            lora_out(2)
            scan_out(0)
            project(3)
            lora_out(3)
            scan_out(1)
            project(4)
            lora_out(4)
            scan_out(2)
            gate_turn()
            scan_out(3)
            gate_hidden()
            scan_out(4)
            pe.wait_ge(k_packed, NT)
            abs_row_of(0, 2, 0, KD)
            abs_to_all(0, 2)
            gate()
            for j in range(NT):
                pe.wait_ge(y_ready, j + 1)
                if j >= 2:
                    pe.wait_ge(yT_ready, j - 1)
                for k in range(KD):
                    ins = nc.tensor.transpose(ps(1 + j % 2, 256 + k * P, 256 + (k + 1) * P),
                                              xn_tok[:, j, k * P:(k + 1) * P], ident[:])
                ins.then_inc(yT_mm, 1)
                pe.wait_ge(yT_ready, j + 1)
                if j >= 2:
                    pe.wait_ge(h_ready, NT + j - 1)
                layer(ps(3 + j % 2, 0, D), lambda k: xnT[:, k, B + j * P:B + (j + 1) * P],
                      lambda k: w4[:, 3, k], KD).then_inc(wo_mm, 1)

            for j in range(NT):
                turn(1, j)
            pe.wait_ge(xT_ready, 2 * NT)
            pe.wait_ge(h_ready, 2 * NT)
            pe.wait_ge(tern_ready, 1)
            for m in range(KH):
                if m == 1:
                    pe.wait_ge(g_ready, NT)
                    abs_row_of(1, 6, KD, KH)
                if m == 2:
                    abs_to_all(1, 6)
                if m == 5:
                    pe.wait_ge(tern_ready, 2)
                    for c, col in ((0, LN2G), (1, LN2B)):
                        ins = layer(ps(6 + c, 0, D, 1), lambda k: pvec[:, col + k:col + k + 1],
                                    lambda k: w2t[:, k], KH)
                    ins.then_inc(rows2_mm, 1)
                if m == 6:
                    pe.wait_ge(rows2_set, 1)
                    for c in range(2):
                        ins = mm(ps(6, c * D, (c + 1) * D), ones[0:1, :], row2[0:1, c], start=True, stop=True)
                    ins.then_inc(bc2_mm, 1)
                if m >= 3:
                    pe.wait_ge(f1_ready, m - 2)
                base = 2 * (m % 3) * 512
                for lo, hi in ((0, 512), (512, NP)):
                    ins = layer(psum[:, base + lo:base + hi], lambda k: w1t[:, k, m * P:(m + 1) * P],
                                lambda k: xnT[:, k, B + lo:B + hi], KD)
                ins.then_inc(f1_mm, 1)
            pe.wait_ge(f1_ready, KH)
            pe.wait_ge(bc2_set, 1)
            pe.wait_ge(sqsum_ready, 1)
            for j in range(NT):
                if j >= 2:
                    pe.wait_ge(h_ready, 2 * NT + j - 1)
                layer(ps(6 + j % 2, 0, D + 1), lambda k: hgT[:, k, j * P:(j + 1) * P], lambda k: w2g[:, k], KH)
                mm(ps(6 + j % 2, 300, 301), sqT[:, 0, j * P:(j + 1) * P], ones[:, 0:1], start=True, stop=True)\
                    .then_inc(f2_mm, 1)

            for j in range(NT):
                turn(2, j)
            pe.wait_ge(xT_ready, 3 * NT)
            pe.wait_ge(h_ready, 3 * NT)
            for w in range(2):
                for m in range(KD):
                    base = 2 * (1 + w * KD + m if w * KD + m < 3 else 1) * 512
                    if w * KD + m == 3:
                        pe.wait_ge(q_ready, 1)
                    for lo, hi in ((0, 512), (512, NP)):
                        ins = layer(psum[:, base + lo:base + hi], lambda k: wat[:, w, k, m * P:(m + 1) * P],
                                    lambda k: xnT[:, k, B + lo:B + hi], KD)
                    ins.then_inc(q_mm, 1)
            for j in range(NT):
                if j >= 2:
                    pe.wait_ge(v_ready, j - 1)
                layer(ps(j % 2, 0, D), lambda k: xnT[:, k, B + j * P:B + (j + 1) * P],
                      lambda k: wat[:, 2, k], KD).then_inc(v_mm, 1)
            pe.wait_ge(q_ready, 4)
            pe.wait_ge(v_ready, NT)

            def plain(dst):
                mm(dst, ones[0:1, 0:64], ones[0:1, 0:1], start=True, stop=True)

            def scores(n, s):
                pe.wait_ge(qm_ready, n + 1)
                if not isinstance(n, int) or n >= 2:
                    pe.wait_ge(sc_ready, n - 1)
                for tile, parts in enumerate((
                        ((0, 0, 64),), ((128, 0, P),), ((256, 0, P), (384, 1, 64)), ((512, 1, P),), ((640, 1, P),))):
                    for i, (at, half, hi) in enumerate(parts):
                        ins = mm(ps(s, tile * T, (tile + 1) * T), qm[0:hi, s, at:at + P],
                                 kT[0:hi, bass.ds(n * T + half * (B * T), T)],
                                 start=(i == 0), stop=(i == len(parts) - 1))
                ins.then_inc(sc_mm, 1)

            def turn_probs(n, s):
                pe.wait_ge(pn_ready, n + 1)
                if not isinstance(n, int) or n >= 2:
                    pe.wait_ge(pt_ready, n - 1)
                plain(ps(2 + 2 * s, 0, 1, 64))
                for tile in range(5):
                    ins = nc.tensor.transpose(ps(2 + 2 * s, tile * P, (tile + 1) * P, T), pm[:, s, tile], ident[:])
                ins.then_inc(pt_mm, 1)

            def values(n, s):
                pe.wait_ge(pt_ready, n + 1)
                pe.wait_ge(v_loaded[s], (n - s) * 8 + 16)
                if not isinstance(n, int) or n >= 2:
                    pe.wait_ge(ot_ready, n - 1)
                plain(ps(6 + s, 0, 1, 64))
                for hh in range(NH):
                    ins = mm(ps(6 + s, hh * HD, (hh + 1) * HD, T), ptS[0:T, s, hh * T:(hh + 1) * T],
                             vS[0:T, s, hh * HD:(hh + 1) * HD], start=True, stop=True)
                ins.then_inc(pv_mm, 1)

            def turn_out(n, s):
                pe.wait_ge(pv_ready, n + 1)
                plain(ps(6 + s, 256, 257, 64))
                for k in range(KD):
                    ins = nc.tensor.transpose(ps(6 + s, 256 + k * T, 256 + (k + 1) * T),
                                              oS[0:T, s, k * P:(k + 1) * P], ident[0:T, 0:T])
                ins.then_inc(ot_mm, 1)

            pipeline(pe, [(scores, 0), (turn_probs, 2), (values, 3), (turn_out, 4)], B, 2, 4)

            pe.wait_ge(ot_ready, B)
            for j in range(NT):
                if j >= 2:
                    pe.wait_ge(h_ready, 3 * NT + j - 1)
                dst = ps(2 + j % 2, 0, D)
                for k in range(KD):
                    mm(dst, xnT[:, k, B + j * P:B + (j + 1) * P], wat[:, 3, k], start=(k == 0), stop=False)
                mm(dst, ones[0:1, :], brow[0:1, 2], start=False, stop=True).then_inc(ao_mm, 1)

            pe.wait_ge(l_late, 16 * 5)
            for j in range(NT):
                turn(3, j)
                pe.wait_ge(xT_ready, 3 * NT + j + 1)
                layer(ps(7, j * NE, (j + 1) * NE), lambda k: xnT[:, k, B + j * P:B + (j + 1) * P],
                      lambda k: wrt[:, k], KD).then_inc(lg_mm, 1)
            for f in range(KF):
                if f == 1:
                    pe.wait_ge(oh_ready, 1)
                    for j in range(NT):
                        dst = ps(3, j * NE, (j + 1) * NE)
                        for i in range(j):
                            mm(dst, ones[:], oh[:, i], start=(i == 0), stop=False)
                        mm(dst, tri[:], oh[:, j], start=(j == 0), stop=True)
                    layer(ps(3, NT * NE, (NT + 1) * NE), lambda k: ones[:], lambda k: oh[:, k], NT).then_inc(cnt_mm, 1)
                for u in range(2):
                    n = 2 * f + u
                    bnk = (4, 6)[u]
                    if n == 1:
                        pe.wait_ge(score_in, 1)
                    if f >= 1:
                        pe.wait_ge(sh_ready, f)
                    for lo, hi in ((0, 512), (512, NP)):
                        ins = layer(psum[:, bnk * 512 + lo:bnk * 512 + hi],
                                    lambda k: wsh[:, k, u * F + f * P:u * F + (f + 1) * P],
                                    lambda k: xnT[:, k, B + lo:B + hi], KD)
                    ins.then_inc(sh_mm, 1)
            pe.wait_ge(sh_ready, KF)

            def item_T(s, bnk=0):
                for k in range(KD):
                    ins = nc.tensor.transpose(ps(bnk, k * C, (k + 1) * C), xsS[0:C, s, k * P:(k + 1) * P],
                                              ident[0:C, 0:C])
                return ins

            def item_gu(s, u):
                for f in range(2 * KF):
                    ins = layer(ps(2 + 2 * u + f // KF, (f % KF) * C, (f % KF + 1) * C),
                                lambda k: wgu[:, s, k, f * P:(f + 1) * P], lambda k: xsT[:, s, k], KD)
                return ins

            def item_y(s, u):
                return layer(ps(6 + u, 0, D, C), lambda k: actE[:, u, k * C:(k + 1) * C],
                             lambda k: wdn[:, s, k], KF)

            def expert_T(e, s):
                pe.wait_ge(x_loaded[s], (e - s) * (16 // RING) + 16 if not isinstance(e, int) else 16 * (e // RING) + 16)
                if not isinstance(e, int) or e >= 2:
                    pe.wait_ge(ex_ready, e - 1)
                item_T(s, s % 2).then_inc(ex_mm, 1)

            def expert_gu(e, s):
                pe.wait_ge(ex_ready, e + 1)
                pe.wait_ge(w_loaded[s], (e - s) * (32 // RING) + 32 if not isinstance(e, int) else 32 * (e // RING) + 32)
                if not isinstance(e, int) or e >= 2:
                    pe.wait_ge(act_ready, e - 1)
                item_gu(s, s % 2).then_inc(gu_mm, 1)

            def expert_y(e, s):
                pe.wait_ge(act_ready, e + 1)
                if not isinstance(e, int) or e >= 2:
                    pe.wait_ge(ys_ready, e - 1)
                item_y(s, s % 2).then_inc(y_mm, 1)

            pe.wait_ge(ctl_ready, 1)
            more = pe.value_load(ctl[0:1, NE + XTRA:NE + XTRA + 1], min_val=0, max_val=XTRA // RING)
            pipeline_rings(pe, [(expert_T, 0), (expert_gu, 1), (expert_y, 2)], more)

            for j in range(NT):
                if j >= 2:
                    pe.wait_ge(ysum_ready, j - 1)
                layer(ps(4 + j % 2, 0, D), lambda k: shT[:, k, j * P:(j + 1) * P], lambda k: wsd[:, k], KF)\
                    .then_inc(sd_mm, 1)

        @block.scalar
        def _(act):
            fn = nc.scalar.activation
            step = Link(act, act_step)

            for j in range(NT):
                act.wait_ge(emb_mm, j + 1)
                fn(h_tok[:, j], ps(j % 2, 0, D), ACT.Copy).then_inc(h_ready, 1)

            def turned(s, j):
                act.wait_ge(xT_mm, NT * s + j + 1)
                src = ps(j % 2, 256, 512).rearrange("p (k n) -> p k n", k=KD)
                dst = xnT[:, :, B + j * P:B + (j + 1) * P]
                if s == 1:
                    fn(dst[:, 0], src[:, 0], ACT.Identity, scale=pvec[:, LN1G:LN1G + 1], bias=pvec[:, LN1B:LN1B + 1])
                    fn(dst[:, 1], src[:, 1], ACT.Identity, scale=pvec[:, LN1G + 1:LN1G + 2],
                       bias=pvec[:, LN1B + 1:LN1B + 2]).then_inc(xT_ready, 1)
                else:
                    fn(dst, src, ACT.Copy).then_inc(xT_ready, 1)

            for j in range(NT):
                turned(0, j)

            def lora(j):
                act.wait_ge(proj_mm, j + 1)
                if j >= 2:
                    act.wait_ge(z_mm, j - 1)
                step(fn(lwT[0:64, j % 2], ps(4 + j % 2, D, D + P, 64), ACT.Sigmoid, scale=2.0))
                ins = fn(laT[0:64, j % 2], ps(4 + j % 2, D + P, D + 2 * P, 64), ACT.Copy)
                if j == 0:
                    ins.then_inc(o_copied, 1)
                fn(lwT[0:64, j % 2], lwT[0:64, j % 2], ACT.Copy, scale=2.0, bias=-1.0).then_inc(lora_ready, 1)
                fn(g_tok[:, j], ps(2 + j % 2, 0, D), ACT.Copy)
                fn(pack[:, j, :, PR], ps(2 + j % 2, 0, D).rearrange("p (h c) -> p h c", h=HG), ACT.Copy)
                fn(pack[:, j, :, PV], ps(4 + j % 2, 0, D).rearrange("p (h c) -> p h c", h=HG), ACT.Copy)\
                    .then_inc(rv_packed, 1)

            def gates(j):
                act.wait_ge(z_mm, j + 1)
                if j >= 2:
                    act.wait_ge(k_packed, j - 1)
                if j >= 1:
                    act.wait_ge(w_packed, j)
                fn(a_tok[:, j % 2], ps(6 + j % 2, D, 2 * D), ACT.Sigmoid).then_inc(a_ready, 1)
                step(fn(w_tok, ps(6 + j % 2, 0, D), ACT.Sigmoid))
                fn(pack[:, j, :, PW], w_tok.rearrange("p (h c) -> p h c", h=HG), ACT.Copy, scale=EXP_MINUS_HALF)\
                    .then_inc(w_packed, 1)

            def square_k(j):
                act.wait_ge(kk_ready, j + 1)
                if j >= 1:
                    act.wait_ge(ss_ready, j)
                fn(sqk, kk, ACT.Square).then_inc(sq_ready, 1)

            def scan_copy(j, between=None):
                def pair(q):
                    act.wait_ge(o_mm, q + 2)
                    fn(o_scan[:, bass.ds(q * (2 * CW), 2 * CW)], ps(0, 0, 2 * CW), ACT.Copy).then_inc(o_copied, 1)

                end = j * TPT // 2 + CHUNKS[j][1]
                with act.Fori(j * TPT // 2, end - 1) as q:
                    pair(q)
                if between is not None:
                    square_k(between)
                pair(end - 1)

            def gate_turned():
                for j in range(NT):
                    act.wait_ge(rT_mm, j + 1)
                    fn(rT[:, :, j * P:(j + 1) * P], ps(6 + j % 2, 0, 256).rearrange("p (k n) -> p k n", k=KD),
                       ACT.Copy).then_inc(rT_ready, 1)

            def gate_sigmoid():
                act.wait_ge(ga_mm, 1)
                fn(sgT, psum[:, 4 * 512:4 * 512 + NP], ACT.Sigmoid).then_inc(sg_ready, 1)

            def gate():
                for j in range(NT):
                    act.wait_ge(g_mm, j + 1)
                    fn(g_tok[:, j], ps(6 + j % 2, 0, D), ACT.Copy).then_inc(g_ready, 1)

            act.wait_ge(consts_set, 2)
            lora(0)
            gates(0)
            square_k(0)
            lora(1)
            gates(1)
            square_k(1)
            lora(2)
            gates(2)
            scan_copy(0, 2)
            lora(3)
            gates(3)
            scan_copy(1, 3)
            lora(4)
            gates(4)
            scan_copy(2, 4)
            gate_turned()
            scan_copy(3)
            gate_sigmoid()
            scan_copy(4)
            gate()

            for j in range(NT):
                act.wait_ge(cen_ready, j + 1)
                fn(gsq[:, j], xn_tok[:, j], ACT.Square).then_inc(gsq_ready, 1)
            act.wait_ge(gva_ready, NT)
            fn(grs[:], gva[:], ACT.Sqrt).then_inc(grs_ready, 1)
            for j in range(NT):
                act.wait_ge(yT_mm, j + 1)
                fn(xnT[:, :, B + j * P:B + (j + 1) * P],
                   ps(1 + j % 2, 256, 512).rearrange("p (k n) -> p k n", k=KD), ACT.Copy).then_inc(yT_ready, 1)
            for j in range(NT):
                turned(1, j)
            for m in range(KH):
                act.wait_ge(f1_mm, m + 1)
                base = 2 * (m % 3) * 512
                step(fn(hgT[:, m], psum[:, base:base + NP], ACT.Gelu, scale=tern[:, 1:2], bias=pvec[:, B1 + m:B1 + m + 1]))
                fn(sqT[:, m], hgT[:, m], ACT.Square).then_inc(f1_ready, 1)
            act.wait_ge(bc2_mm, 1)
            fn(bc2[:].rearrange("p r n -> p (r n)"), ps(6, 0, 2 * D), ACT.Copy).then_inc(bc2_set, 1)

            for j in range(NT):
                turned(2, j)
            for w in range(2):
                for m in range(KD):
                    base = 2 * (1 + w * KD + m if w * KD + m < 3 else 1) * 512
                    dst = qT[:, m] if w == 0 else kT[:, m * B * T:(m + 1) * B * T]
                    act.wait_ge(q_mm, w * KD + m + 1)
                    fn(dst.rearrange("p (b t) -> p b t", b=B),
                       psum[:, base:base + NTOK].rearrange("p (t b) -> p b t", b=B), ACT.Copy).then_inc(q_ready, 1)
            for j in range(NT):
                act.wait_ge(v_mm, j + 1)
                fn(g_tok[:, j], ps(j % 2, 0, D), ACT.Copy).then_inc(v_ready, 1)

            def copy_scores(n, s):
                act.wait_ge(sc_mm, n + 1)
                if not isinstance(n, int) or n >= 2:
                    act.wait_ge(keep_ready, n - 1)
                    act.wait_ge(exp_ready, n - 1)
                fn(scS[:, s].rearrange("p i k -> p (i k)"), ps(s, 0, 5 * T), ACT.Copy).then_inc(sc_ready, 1)

            def exps(n, s):
                act.wait_ge(nb_ready, n + 1)
                if not isinstance(n, int) or n >= 2:
                    act.wait_ge(pm_ready, n - 1)
                for tile in range(5):
                    ins = fn(ex[:, s, tile], scS[:, s, tile], ACT.Exp, scale=0.25,
                             bias=nb[:, s, tile:tile + 1])
                ins.then_inc(exp_ready, 1)

            def copy_probs(n, s):
                act.wait_ge(pt_mm, n + 1)
                if not isinstance(n, int) or n >= 2:
                    act.wait_ge(pv_mm, n - 1)
                fn(ptS[0:T, s, 0:NTOK], psum[0:T, (2 + 2 * s) * 512:(2 + 2 * s) * 512 + NTOK], ACT.Copy)\
                    .then_inc(pt_ready, 1)

            def copy_o(n, s):
                act.wait_ge(pv_mm, n + 1)
                if not isinstance(n, int) or n >= 2:
                    act.wait_ge(ot_mm, n - 1)
                fn(oS[0:T, s], ps(6 + s, 0, D, T), ACT.Copy).then_inc(pv_ready, 1)

            def copy_oT(n, s):
                act.wait_ge(ot_mm, n + 1)
                for k in range(KD):
                    flat = xnT[:].rearrange("p k n -> p (k n)")
                    dst = flat[:, bass.DynSlice(n + (B + k * (B + NP)), T, step=B)]
                    ins = fn(dst, ps(6 + s, 256 + k * T, 256 + (k + 1) * T), ACT.Copy)
                ins.then_inc(ot_ready, 1)

            pipeline(act, [(copy_scores, 0), (exps, 0), (copy_probs, 2), (copy_o, 3), (copy_oT, 4)], B, 2, 4)

            for j in range(NT):
                turned(3, j)
            act.wait_ge(lg_mm, NT)
            fn(lg[:].rearrange("p j e -> p (j e)"), ps(7, 0, NT * NE), ACT.Copy).then_inc(score_in, 1)
            act.wait_ge(score_in, 2)
            fn(rt5[:, 1], rt5[:, 0], ACT.Sigmoid).then_inc(score_ready, 1)
            act.wait_ge(score_ready, 1)
            act.wait_ge(h_ready, 4 * NT)
            for j in range(NT):
                ins = fn(xs_tok[:, j], xn_tok[:, j], ACT.Copy, scale=rt5[:, 1, j:j + 1])
            ins.then_inc(xs_ready, 1)
            for f in range(KF):
                act.wait_ge(sh_mm, 2 * f + 1)
                if f >= 1:
                    act.wait_ge(sh_ready, f)
                fn(gshT, psum[:, 4 * 512:4 * 512 + NP], ACT.Silu).then_inc(sh_silu, 1)

            def item_xT(s, bnk=0):
                return fn(xsT[:, s], ps(bnk, 0, KD * C).rearrange("p (k n) -> p k n", k=KD), ACT.Copy)

            def expert_xT(e, s):
                act.wait_ge(ex_mm, e + 1)
                if not isinstance(e, int) or e >= RING:
                    act.wait_ge(gu_mm, e - RING + 1)
                item_xT(s, s % 2).then_inc(ex_ready, 1)

            def expert_silu(e, s):
                act.wait_ge(gu_mm, e + 1)
                if not isinstance(e, int) or e >= 2:
                    act.wait_ge(act_ready, e - 1)
                fn(sgE[:, s % 2], ps(2 + 2 * (s % 2), 0, KF * C), ACT.Silu).then_inc(silu_ready, 1)

            def expert_copy(e, s):
                act.wait_ge(y_mm, e + 1)
                if isinstance(e, int):
                    if e >= 2:
                        act.wait_ge(ys_out[s % 2], 16 * (e // 2))
                else:
                    act.wait_ge(ys_out[s % 2], (e - s % 2) * 8)
                fn(ysS[0:C, s % 2], ps(6 + s % 2, 0, D, C), ACT.Copy).then_inc(ys_ready, 1)

            act.wait_ge(ctl_ready, 1)
            more = act.value_load(ctl[0:1, NE + XTRA:NE + XTRA + 1], min_val=0, max_val=XTRA // RING)
            pipeline_rings(act, [(expert_xT, 0), (expert_silu, 1), (expert_copy, 2)], more)

        @block.vector
        def _(dve):
            v = nc.vector
            step = Link(dve, dve_step)
            v.memset(ones[:], 1.0).then_inc(consts_set, 1)
            v.memset(xnT[:, :, 0:B], 0.0)
            v.memset(neghalf[:], -0.5)
            v.memset(w2g[:, :, D:D + 1], 1.0)
            v.memset(xT[:, :, 0:2 * B], 0.0)
            v.memset(xT[:, :, NTOK:NP], 0.0)
            v.memset(lwT[64:65], 1.0)
            v.memset(laT[64:65], 1.0).then_inc(consts_set, 1)

            def ternary(i, wt, k0, kn, bank):
                w, below, c = wt[:].rearrange("p k n -> p (k n)"), sr[:].rearrange("p s u x -> p (s u x)"), 3 * i
                v.tensor_reduce(absum[:, k0:k0 + kn], wt[:], X, ALU.add, apply_absolute_value=True)\
                    .then_inc(abs_sum, 1)
                dve.wait_ge(abs_row, i + 1)
                v.tensor_reduce(tern[0:1, c:c + 1], psum[0:1, bank * 512:bank * 512 + kn * P], X, ALU.add)\
                    .then_inc(abs_one, 1)
                dve.wait_ge(abs_all, i + 1)
                step(v.tensor_scalar(tern[:, c + 1:c + 2], ps(bank, 0, 1), 1.0 / (HID * D), 1e-5, ALU.mult, ALU.max))
                step(v.reciprocal(tern[:, c + 2:c + 3], tern[:, c + 1:c + 2]))
                dve.wait_ge(o_mm, T // 2 + 1)
                step(v.tensor_scalar(below, w, tern[:, c + 2:c + 3], -0.5, ALU.mult, ALU.is_lt))
                step(v.tensor_scalar(w, w, tern[:, c + 2:c + 3], 0.5, ALU.mult, ALU.is_gt))
                return v.tensor_tensor(w, w, below, ALU.subtract)

            def ln_stats(s, j):
                dve.wait_ge(h_ready, NT * s + j + 1)
                step(v.bn_stats(stat[:, j], h_tok[:, j]))
                step(v.bn_aggr(mv[:, j], stat[:, j]))
                if s == 1:
                    v.tensor_scalar(ve[:, j:j + 1], mv[:, j, 1:2], 1.0 + EPS, EPS * EPS, ALU.mult, ALU.add)\
                        .then_inc(ve_ready, 1)
                else:
                    v.tensor_scalar(ve[:, j:j + 1], mv[:, j, 1:2], EPS, None, ALU.add).then_inc(ve_ready, 1)

            def ln_apply(s, j):
                dve.wait_ge(rstd_ready, NT * s + j + 1)
                v.tensor_scalar(xn_tok[:, j], h_tok[:, j], mv[:, j, 0:1], rstd[:, j:j + 1], ALU.subtract, ALU.mult)\
                    .then_inc(xn_ready, 1)

            def layernorm(s, before=None):
                for j in range(NT + 1):
                    if j < NT:
                        if before:
                            before(j)
                        ln_stats(s, j)
                    if j >= 1:
                        ln_apply(s, j - 1)

            layernorm(0)

            def mixes(j):
                dve.wait_ge(xT_ready, j + 1)
                now = xnT[:, :, B + j * P:B + (j + 1) * P]
                if j >= 1:
                    dve.wait_ge(mix_ready, j)
                step(v.tensor_tensor(delta, xnT[:, :, j * P:(j + 1) * P], now, ALU.subtract))
                if j >= 2:
                    dve.wait_ge(proj_mm, j - 1)
                for m in range(5):
                    for k in range(KD):
                        ins = v.scalar_tensor_tensor(mix[:, j % 2, m, k], delta[:, k],
                                                     pvec[:, MIX + 2 * m + k:MIX + 2 * m + k + 1], now[:, k],
                                                     ALU.mult, ALU.add)
                ins.then_inc(mix_ready, 1)

            def hc(x):
                return x.rearrange("p (h c) -> p h c", h=HG)

            def hoc(x):
                return x.rearrange("p (h o c) -> p h o c", h=HG, o=2)

            def keys(j):
                psk = ps(2 + j % 2, D, 2 * D)
                dve.wait_ge(rv_packed, j + 1)
                v.tensor_tensor(kk, psk, rows[:, KK_], ALU.mult).then_inc(kk_ready, 1)
                dve.wait_ge(a_ready, j + 1)
                step(v.scalar_tensor_tensor(am, a_tok[:, j % 2], -1.0, rows[:, KA_], ALU.add, ALU.mult))
                v.scalar_tensor_tensor(pack[:, j, :, PK], hc(am), 1.0, hc(psk), ALU.add, ALU.mult)

            def keys_norm(j):
                dve.wait_ge(sq_ready, j + 1)
                step(v.tensor_reduce(ss[:], sqk.rearrange("p (h d) -> p h d", h=NH), X, ALU.add))
                v.tensor_scalar(ss[:], ss[:], 1e-24, None, ALU.max).then_inc(ss_ready, 1)
                dve.wait_ge(rn_ready, j + 1)
                step(v.tensor_scalar(rn[:], rn[:], -1.0, None, ALU.mult))
                dst = pack[:, j, :, PA]
                step(v.tensor_tensor(dst.rearrange("p h (o c) -> p h o c", o=2), hoc(kk),
                                     rn[:].rearrange("p (h o) -> p h o", h=HG).unsqueeze(3).broadcast_to([P, HG, 2, HD]),
                                     ALU.mult))
                v.scalar_tensor_tensor(pack[:, j, :, PB], dst, -1.0, hc(a_tok[:, j % 2]), ALU.mult, ALU.mult)\
                    .then_inc(k_packed, 1)

            def scan(j):
                dve.wait_ge(scan_loaded, 16 * (j + 1))
                if j == 0:
                    dve.wait_ge(scan_dve, 2)

                def times_r(t, u, pair):
                    v.tensor_tensor(s4(sr[:, pair, u]), s4(state), along_i(tcol(t, PR)), ALU.mult).then_inc(scan_dve, 1)

                def step_of(q, u, lead, pair):
                    t = q * 2 + u
                    at = q * (2 * SCAN_DVE)
                    now = u * SCAN_DVE + 2
                    dve.wait_ge(scan_dve, at + (now - 1))
                    v.tensor_tensor(s4(prod), s4(state), along_i(tcol(t, PA)), ALU.mult).then_inc(scan_dve, 1)
                    v.tensor_tensor(kv[:, 0:256].rearrange("p (i j) -> p i j", i=HD),
                                    tcol(t, PV)[:, 0].unsqueeze(2).broadcast_to([P, HD, HD]),
                                    tcol(t, PK)[:, 0].unsqueeze(1).broadcast_to([P, HD, HD]), ALU.mult)\
                        .then_inc(scan_dve, 1)
                    dve.wait_ge(scan_dve, at + (now + lead))
                    v.tensor_reduce(sa[:], prod.rearrange("p (x j) -> p x j", j=HD), X, ALU.add)\
                        .then_inc(scan_dve, 1)
                    if not lead:
                        if u == 1 and not (isinstance(q, int) and q < 1):
                            dve.wait_ge(o_mm, q)
                        times_r(t - 1, 1 - u, pair if u == 1 else 1 - pair)
                    dve.wait_ge(scan_dve, at + (now + 2 + lead))
                    v.tensor_tensor(s4(outer), along_j(sa[:].rearrange("p (h i) -> p h i", h=2)),
                                    along_i(tcol(t, PB)), ALU.mult).then_inc(scan_dve, 1)
                    dve.wait_ge(scan_dve, at + (now + 4))
                    dve.wait_ge(scan_pool, q * (2 * SCAN_POOL) + ((u + 1) * SCAN_POOL + 1))
                    v.tensor_tensor(state, outer, carried, ALU.add).then_inc(scan_dve, 1)

                lo, n = j * TPT // 2, CHUNKS[j][1]
                step_of(lo, 0, 1, 0)
                step_of(lo, 1, 0, 0)
                with dve.Fori(0, (n - 1) // 2) as i:
                    for u in range(4):
                        step_of(i * 2 + (lo + 1 + u // 2), u % 2, 0, (1 + u // 2) % 2)
                if n % 2 == 0:
                    for u in range(2):
                        step_of(lo + n - 1, u, 0, 1)
                dve.wait_ge(scan_dve, (lo + n) * 2 * SCAN_DVE + 1)
                times_r((lo + n) * 2 - 1, 1, (n - 1) % 2)

            dve.wait_ge(l_rw, 16 * 7)
            mixes(0)
            mixes(1)
            keys(0)
            mixes(2)
            keys_norm(0)
            keys(1)
            keys_norm(1)
            dve.wait_ge(emb_mm, NT)
            for head in range(2):
                v.memset(state[:, head * HD * HD:(head + 1) * HD * HD], 0.0).then_inc(scan_dve, 1)
            scan(0)
            keys(2)
            mixes(3)
            keys_norm(2)
            scan(1)
            keys(3)
            mixes(4)
            keys_norm(3)
            scan(2)
            keys(4)
            keys_norm(4)
            scan(3)
            scan(4)
            for j in range(NT):
                dve.wait_ge(rk_ready, j + 1)
                v.tensor_reduce(bs[:, j], bonus[:, j].rearrange("p (h d) -> p h d", h=NH), X, ALU.add)\
                    .then_inc(bs_ready, 1)

            dve.wait_ge(l_tern, 48)
            ternary(0, w1t, 0, KD, 2).then_inc(tern_ready, 1)

            def heads(x):
                return x.rearrange("p (h d) -> p h d", h=NH)

            def spread(x):
                return x.unsqueeze(2).broadcast_to([P, NH, HD])

            for j in range(NT):
                dve.wait_ge(o_loaded, 16 * (j + 1))
                o = heads(xn_tok[:, j])
                step(v.tensor_reduce(gmu[:, j], o, X, ALU.add))
                v.scalar_tensor_tensor(o, spread(gmu[:, j]), -1.0 / HD, o, ALU.mult, ALU.add).then_inc(cen_ready, 1)
            for j in range(NT):
                dve.wait_ge(gsq_ready, j + 1)
                step(v.tensor_reduce(gva[:, j], gsq[:, j].rearrange("p (h d) -> p h d", h=NH), X, ALU.add))
                v.tensor_scalar(gva[:, j], gva[:, j], 1.0 / HD, EPS, ALU.mult, ALU.add).then_inc(gva_ready, 1)
            dve.wait_ge(grs_ready, 1)
            step(v.reciprocal(grs[:], grs[:]))
            for j in range(NT):
                y = xn_tok[:, j]
                step(v.tensor_tensor(heads(y), heads(y), spread(grs[:, j]), ALU.mult))
                step(v.tensor_tensor(y, y, rows[:, GNW], ALU.mult))
                dve.wait_ge(bonus_ready, j + 1)
                step(v.tensor_tensor(y, y, bonus[:, j], ALU.add))
                dve.wait_ge(g_ready, j + 1)
                v.tensor_tensor(y, y, g_tok[:, j], ALU.mult).then_inc(y_ready, 1)

            def add_to_h(src):
                def add(j):
                    src_ap, s, n = src(j)
                    dve.wait_ge(s, n)
                    v.tensor_tensor(h_tok[:, j], h_tok[:, j], src_ap, ALU.add).then_inc(h_ready, 1)
                return add

            layernorm(1, add_to_h(lambda j: (ps(3 + j % 2, 0, D), wo_mm, j + 1)))

            step(ternary(1, w2t, KD, KH, 6))
            for k in range(KH):
                ins = v.tensor_scalar(w2g[:, k, 0:D], w2t[:, k], pvec[:, LN2G + k:LN2G + k + 1], None, ALU.mult)
            ins.then_inc(tern_ready, 1)
            for m in range(1, KH):
                if m == 6:
                    dve.wait_ge(rows2_mm, 1)
                    v.tensor_copy(row2[0:1, 0], ps(6, 0, D, 1))
                    v.scalar_tensor_tensor(row2[0:1, 1], ps(7, 0, D, 1), tern[0:1, 4:5], brow[0:1, 1],
                                           ALU.mult, ALU.add).then_inc(rows2_set, 1)
                dve.wait_ge(f1_ready, m + 1)
                ins = v.tensor_tensor(sqT[:, 0], sqT[:, 0], sqT[:, m], ALU.add)
                if m < KH - 1:
                    step(ins)
            ins.then_inc(sqsum_ready, 1)

            def ffn_stats(j):
                dve.wait_ge(f2_mm, j + 1)
                b = 6 + j % 2
                v.tensor_scalar(fst[:, j, 0:1], ps(b, D, D + 1), -1.0 / HID, None, ALU.mult)
                step(v.tensor_scalar(fst[:, j, 1:2], ps(b, 300, 301), 1.0 / HID, EPS, ALU.mult, ALU.add))
                step(v.tensor_tensor(fst[:, j, 2:3], fst[:, j, 0:1], fst[:, j, 0:1], ALU.mult))
                v.tensor_tensor(fst[:, j, 3:4], fst[:, j, 1:2], fst[:, j, 2:3], ALU.subtract).then_inc(fv_ready, 1)
                step(v.scalar_tensor_tensor(xn_tok[:, j], bc2[:, 0], fst[:, j, 0:1], ps(b, 0, D), ALU.mult, ALU.add))

            def ffn_apply(j):
                dve.wait_ge(frs_ready, j + 1)
                step(v.tensor_tensor(fst[:, j, 5:6], fst[:, j, 4:5], tern[:, 4:5], ALU.mult))
                step(v.scalar_tensor_tensor(xn_tok[:, j], xn_tok[:, j], fst[:, j, 5:6], bc2[:, 1], ALU.mult, ALU.add))
                v.tensor_tensor(h_tok[:, j], h_tok[:, j], xn_tok[:, j], ALU.add).then_inc(h_ready, 1)

            dve.wait_ge(bc2_set, 1)
            dve.wait_ge(xT_mm, 2 * NT)
            for j in range(NT):
                ffn_stats(j)
                ffn_apply(j)
            layernorm(2)

            dve.wait_ge(l_late, 16 * 5)
            dve.wait_ge(f2_mm, NT)
            v.memset(qm, 0.0).then_inc(qm_zero, 1)
            step(v.tensor_scalar(thr[:], thr[:], 0.0, 1.0, ALU.max, ALU.min))
            step(v.tensor_scalar(thr[:], thr[:], 4.0, None, ALU.mult))
            step(v.tensor_scalar(thr5[:], cst[:, C_PADROW:C_PADROW + 5], thr[:], None, ALU.add))

            def plain():
                v.memset(cell[:, 0:1], 0.0)

            def first(n, k):
                return isinstance(n, int) and n < k

            def keep_mask(n, s):
                v.tensor_tensor(keep[:, s], scS[:, s], cthr[:, s].unsqueeze(2).broadcast_to([P, 5, T]), ALU.is_ge)\
                    .then_inc(keep_ready, 1)

            def sum_probs(n, s):
                dve.wait_ge(pm_ready, n + 1)
                v.tensor_reduce(rinv[:, s], pm[:, s], X, ALU.add).then_inc(sum_ready, 1)

            def invert_sums(n, s):
                dve.wait_ge(sum_ready, n + 1)
                v.reciprocal(rinv[:, s], rinv[:, s]).then_inc(rinv_ready, 1)

            def topk(n, s):
                sc = [scS[:, s, i] for i in range(5)]
                done = lambda c: dve.wait_ge(top_step, n * 6 + c)
                dve.wait_ge(sc_ready, n + 1)
                if first(n, 1):
                    plain()
                else:
                    done(0)
                    keep_mask(n - 1, 1 - s)
                for i in range(5):
                    ins = v.max(mx[:, s, i, 0:8], sc[i])
                ins.then_inc(top_step, 1)
                done(1)
                v.tensor_scalar(nb[:, s], mx[:, s, :, 0], -0.25, None, ALU.mult).then_inc(nb_ready, 1)
                for i in range(5):
                    ins = v.match_replace(wk1[:, i], mx[:, s, i, 0:8], sc[i], NEG)
                ins.then_inc(top_step, 1)
                done(2)
                plain() if first(n, 1) else sum_probs(n - 1, 1 - s)
                for i in range(5):
                    ins = v.max(mx[:, s, i, 8:16], wk1[:, i])
                ins.then_inc(top_step, 1)
                done(3)
                plain() if first(n, 1) else invert_sums(n - 1, 1 - s)
                for i in range(5):
                    ins = v.match_replace(wk2[:, i], mx[:, s, i, 8:16], wk1[:, i], NEG)
                ins.then_inc(top_step, 1)
                done(4)
                plain()
                for i in range(5):
                    ins = v.max(mx[:, s, i, 16:24], wk2[:, i])
                ins.then_inc(top_step, 1)
                done(5)
                v.tensor_tensor(cthr[:, s], mx[:, s, :, KEEP - 1], thr5[:], ALU.max).then_inc(top_step, 1)

            pipeline(dve, [(topk, 0)], B, 2, 2)
            dve.wait_ge(top_step, 6 * B)
            keep_mask(B - 1, 1)
            sum_probs(B - 1, 1)
            invert_sums(B - 1, 1)

            layernorm(3, add_to_h(lambda j: (ps(2 + j % 2, 0, D), ao_mm, j + 1)))

            def wide(x, n=NE):
                return x.unsqueeze(2).broadcast_to([P, NT, n])

            em = cst[:, C_E:C_E + NE].unsqueeze(1).broadcast_to([P, NT, NE])
            dve.wait_ge(score_in, 1)
            step(v.tensor_reduce(rt5[:, 0], lg[:], X, ALU.max))
            step(v.tensor_tensor(rt1[:], lg[:], wide(rt5[:, 0]), ALU.is_equal))
            v.tensor_tensor(rt1[:], rt1[:], em, ALU.mult).then_inc(score_in, 1)
            dve.wait_ge(score_in, 2)
            step(v.tensor_reduce(rt5[:, 2], rt1[:], X, ALU.min))
            step(v.tensor_tensor(oh[:], em, wide(rt5[:, 2]), ALU.is_equal))
            valid = cst[:, C_VALID:C_VALID + NT]
            v.tensor_tensor(oh[:], oh[:], wide(valid), ALU.mult).then_inc(oh_ready, 1)

            def shared_act(f):
                dve.wait_ge(sh_silu, f + 1)
                dve.wait_ge(sh_mm, 2 * f + 2)
                v.tensor_tensor(shT[:, f], gshT, psum[:, 6 * 512:6 * 512 + NP], ALU.mult).then_inc(sh_ready, 1)

            shared_act(0)
            dve.wait_ge(cnt_mm, 1)
            dve.wait_ge(oh_ready, 1)
            step(v.tensor_tensor(rt1[:], oh[:], ps(3, 0, NT * NE).rearrange("p (j e) -> p j e", j=NT), ALU.mult))
            step(v.tensor_reduce(rt5[:, 3], rt1[:], X, ALU.add))
            cnt = ps(3, NT * NE, (NT + 1) * NE)
            step(v.tensor_scalar(ex16[:, 0], cnt, float(C), None, ALU.is_gt))
            for m in range(2, XTRA + 1):
                step(v.scalar_tensor_tensor(ex16[:, 0], cnt, float(C * m), ex16[:, 0], ALU.is_gt, ALU.add))
            step(v.tensor_tensor_scan(ex16[:, 1], ones[:, 0:NE], ex16[:, 0], 0.0, ALU.mult, ALU.add))
            step(v.tensor_tensor(ex16[:, 2], ex16[:, 1], ex16[:, 0], ALU.subtract))
            step(v.tensor_tensor(rt1[:], oh[:], ex16[:, 2].unsqueeze(1).broadcast_to([P, NT, NE]), ALU.mult))
            step(v.tensor_reduce(rt5[:, 4], rt1[:], X, ALU.add))
            step(v.tensor_scalar(rt5[:, 4], rt5[:, 4], float(NE - 1), None, ALU.add))
            v.tensor_scalar(rt5[:, 5], rt5[:, 2], float(NE), None, ALU.add)
            step(v.tensor_scalar(rt5[:, 6], rt5[:, 3], float(C), None, ALU.is_lt))
            step(v.tensor_tensor(rt5[:, 5], rt5[:, 5], rt5[:, 4], ALU.subtract))
            step(v.tensor_tensor(rt5[:, 5], rt5[:, 5], rt5[:, 6], ALU.mult))
            step(v.tensor_tensor(rt5[:, 5], rt5[:, 5], rt5[:, 4], ALU.add))
            step(v.scalar_tensor_tensor(rt5[:, 5], rt5[:, 5], float(C), rt5[:, 3], ALU.mult, ALU.add))
            step(v.tensor_tensor(rt5[:, 5], rt5[:, 5], valid, ALU.mult))
            v.tensor_tensor(slot[:], rt5[:, 5], cst[:, C_TROW:C_TROW + NT], ALU.add).then_inc(slot_ready, 1)
            v.tensor_scalar(ctlf[:, 0:NE], cst[:, C_E:C_E + NE], float(NE), None, ALU.add)
            step(v.tensor_tensor(xk[:], ex16[:, 1].unsqueeze(1).broadcast_to([P, XTRA, NE]),
                                 cst[:, C_K:C_K + XTRA].unsqueeze(2).broadcast_to([P, XTRA, NE]), ALU.is_le))
            step(v.tensor_reduce(ctlf[:, NE:NE + XTRA], xk[:], X, ALU.add))
            step(v.tensor_scalar(ctlf[:, NE:NE + XTRA], ctlf[:, NE:NE + XTRA], float(NE - 1), None, ALU.min))
            total, rings = ex16[:, 1, NE - 1:NE], ctlf[:, NE + XTRA:NE + XTRA + 1]
            step(v.tensor_scalar(rings, total, 0.0, None, ALU.is_gt))
            for m in range(RING, XTRA, RING):
                step(v.scalar_tensor_tensor(rings, total, float(m), rings, ALU.is_gt, ALU.add))
            v.tensor_copy(ctl[:], ctlf[:]).then_inc(ctl_ready, 1)

            for f in range(1, KF):
                shared_act(f)

            def expert_act(e, s):
                dve.wait_ge(silu_ready, e + 1)
                if not isinstance(e, int) or e >= 2:
                    dve.wait_ge(y_mm, e - 1)
                v.tensor_tensor(actE[:, s % 2], sgE[:, s % 2], ps(3 + 2 * (s % 2), 0, KF * C), ALU.mult)\
                    .then_inc(act_ready, 1)

            dve.wait_ge(ctl_ready, 1)
            more = dve.value_load(ctl[0:1, NE + XTRA:NE + XTRA + 1], min_val=0, max_val=XTRA // RING)
            pipeline_rings(dve, [(expert_act, 0)], more)
            for j in range(NT):
                dve.wait_ge(sd_mm, j + 1)
                v.tensor_tensor(ysum[:, j], h_tok[:, j], ps(4 + j % 2, 0, D), ALU.add).then_inc(ysum_ready, 1)
            dve.wait_ge(ysum_ready, NT)
            for j in range(NT):
                dve.wait_ge(yg_loaded[j], 16)
                v.tensor_tensor(xn_tok[:, j], ysum[:, j], ygat[:, j], ALU.add).then_inc(res_ready, 1)

        @block.gpsimd
        def _(pool):
            g = nc.gpsimd
            pool.wait_ge(consts_set, 2)
            g.memset(cell[:, 1:2], 0.0).then_inc(scan_pool, 1)

            def ln_pow(s, j):
                pool.wait_ge(ve_ready, NT * s + j + 1)
                g.tensor_tensor(rstd[:, j:j + 1], ve[:, j:j + 1], neghalf[:, 0:1], ALU.pow).then_inc(rstd_ready, 1)

            for j in range(NT):
                ln_pow(0, j)

            def key_pow(j):
                pool.wait_ge(ss_ready, j + 1)
                g.tensor_tensor(rn[:], ss[:], neghalf[:], ALU.pow).then_inc(rn_ready, 1)

            def rk(j):
                pool.wait_ge(k_packed, j + 1)
                pool.wait_ge(rv_packed, j + 1)
                dst = bonus[:, j].rearrange("p (h c) -> p h c", h=HG)
                g.tensor_tensor(dst, pack[:, j, :, PR], pack[:, j, :, PK], ALU.mult).then_inc(pool_step, 1)
                pool.wait_ge(pool_step, j + 1)
                g.tensor_tensor(bonus[:, j], bonus[:, j], rows[:, RK_], ALU.mult).then_inc(rk_ready, 1)

            def scan(j):
                pool.wait_ge(scan_loaded, 16 * (j + 1))
                if j == 0:
                    pool.wait_ge(scan_dve, 2)

                def step_of(q, u, lead):
                    t = q * 2 + u
                    done = q * (2 * SCAN_POOL) + (u * SCAN_POOL + 1)
                    now = u * SCAN_DVE + 2
                    pool.wait_ge(scan_pool, done)
                    g.tensor_tensor(kv[:, 256:512].rearrange("p (i j) -> p i j", i=HD),
                                    tcol(t, PV)[:, 1].unsqueeze(2).broadcast_to([P, HD, HD]),
                                    tcol(t, PK)[:, 1].unsqueeze(1).broadcast_to([P, HD, HD]), ALU.mult)\
                        .then_inc(scan_pool, 1)
                    pool.wait_ge(scan_dve, q * (2 * SCAN_DVE) + (now - 1))
                    g.tensor_tensor(s4(decayed), s4(state), along_i(tcol(t, PW)), ALU.mult).then_inc(scan_pool, 1)
                    pool.wait_ge(scan_pool, done + 2)
                    pool.wait_ge(scan_dve, q * (2 * SCAN_DVE) + (now + 1 + lead))
                    g.tensor_tensor(carried, decayed, kv, ALU.add).then_inc(scan_pool, 1)

                lo, n = j * TPT // 2, CHUNKS[j][1]
                step_of(lo, 0, 1)
                step_of(lo, 1, 0)
                with pool.Fori(lo + 1, lo + n) as q:
                    for u in range(2):
                        step_of(q, u, 0)

            key_pow(0)
            key_pow(1)
            scan(0)
            rk(0)
            key_pow(2)
            scan(1)
            rk(1)
            key_pow(3)
            scan(2)
            rk(2)
            key_pow(4)
            scan(3)
            rk(3)
            scan(4)
            rk(4)
            for j in range(NT):
                pool.wait_ge(bs_ready, j + 1)
                g.tensor_tensor(bonus[:, j].rearrange("p (h o c) -> p h o c", h=HG, o=2),
                                pack[:, j, :, PV].rearrange("p h (o c) -> p h o c", o=2),
                                bs[:, j].rearrange("p (h o) -> p h o", h=HG).unsqueeze(3).broadcast_to([P, HG, 2, HD]),
                                ALU.mult).then_inc(pool_step, 1)
                pool.wait_ge(pool_step, NT + j + 1)
                g.tensor_tensor(bonus[:, j], bonus[:, j], rows[:, GNB], ALU.add).then_inc(bonus_ready, 1)
            for j in range(NT):
                ln_pow(1, j)
            for j in range(NT):
                pool.wait_ge(fv_ready, j + 1)
                g.tensor_tensor(fst[:, j, 4:5], fst[:, j, 3:4], neghalf[:, 0:1], ALU.pow).then_inc(frs_ready, 1)
            for j in range(NT):
                ln_pow(2, j)

            pool.wait_ge(qm_zero, 1)
            pool.wait_ge(q_ready, 2)
            pool.wait_ge(l_mid, 48)
            mask = cst[:, C_HM:C_HM + HG].unsqueeze(1).unsqueeze(3).broadcast_to([P, KD, HG, T])

            def mask_q(n, s):
                if not isinstance(n, int) or n >= 2:
                    pool.wait_ge(sc_mm, n - 1)
                src = qT[:, :, bass.ds(n * T, T)].unsqueeze(2).broadcast_to([P, KD, HG, T])
                dst = qm[:, s].rearrange("p (k n) -> p k n", k=KD)[:, :, 0:HG * T]
                g.tensor_tensor(dst.rearrange("p k (h q) -> p k h q", h=HG), src, mask, ALU.mult)\
                    .then_inc(qm_ready, 1)

            def mask_p(n, s):
                pool.wait_ge(exp_ready, n + 1)
                pool.wait_ge(keep_ready, n + 1)
                if not isinstance(n, int) or n >= 2:
                    pool.wait_ge(pt_mm, n - 1)
                g.tensor_tensor(pm[:, s], ex[:, s], keep[:, s], ALU.mult).then_inc(pm_ready, 1)

            def norm_p(n, s):
                pool.wait_ge(rinv_ready, n + 1)
                g.tensor_tensor(pm[:, s], pm[:, s], rinv[:, s].unsqueeze(2).broadcast_to([P, 5, T]), ALU.mult)\
                    .then_inc(pn_ready, 1)

            def probs(n, s):
                mask_p(n, s)
                if not isinstance(n, int) or n + 2 < B:
                    mask_q(n + 2, s)
                norm_p(n, s)

            mask_q(0, 0)
            mask_q(1, 1)
            pipeline(pool, [(probs, 0)], B - 2, 2, 2)
            probs(B - 2, 0)
            probs(B - 1, 1)

            for j in range(NT):
                ln_pow(3, j)
            pool.wait_ge(slot_ready, 1)
            pool.wait_ge(xs_ready, 1)
            n_zero = -(-(TRASH + P) // P) + -(-(TRASH + P - NE * C) // P)
            pool.wait_ge(zero_out, 16 * n_zero)
            for j in range(NT):
                g.indirect_dma_start(xs_dram, bass.IndirectOffsetOnAxis(slot[:, j:j + 1], 0), xs_tok[:, j], None)\
                    .then_inc(xs_out[j], 16)
            pool.wait_ge(ctl_ready, 1)
            more = pool.value_load(ctl[0:1, NE + XTRA:NE + XTRA + 1], min_val=0, max_val=XTRA // RING)
            for half in range(2):
                pool.wait_ge(ys_out[half], more * (8 * RING) + 8 * NE)
            g.tensor_tensor(cell[:, 1:2], neghalf[:, 0:1], neghalf[:, 0:1], ALU.add)
            for j in range(NT):
                g.indirect_dma_start(ygat[:, j], None, ys_dram, bass.IndirectOffsetOnAxis(slot[:, j:j + 1], 0))\
                    .then_inc(yg_loaded[j], 16)


def kernel(x, cls_tok, **w):
    import numpy as np
    import concourse.bacc as bacc
    from concourse import mybir as mb
    from concourse.bass_utils import run_bass_kernel_spmd

    def chunks(m):
        k, n = m.shape
        return m.reshape(k // P, P, n).transpose(1, 0, 2).reshape(P, -1)

    def cols(v):
        return v.reshape(-1, P).T

    t0, a0, f0, a1, f1 = "L0_tok_", "L0_attn_", "L0_ffn_", "L1_attn_", "L1_ffn_"
    w = {k: np.asarray(m) for k, m in w.items()}
    x = np.asarray(x)
    patches = x.reshape(B, 3, 6, 16, 6, 16).transpose(1, 3, 5, 2, 4, 0).reshape(768, 36 * B)
    sel = np.zeros((40, NP), np.float32)
    for n in range(NTOK):
        sel[n // B, n] = 1
        if n // B == 1:
            sel[39, n] = 1
        if n // B >= 2:
            sel[38, n] = 1
    cst = np.zeros((P, NCST), np.float32)
    cst[NH * T - 4 * P:, C_PADROW + 4] = NEG
    cst[:, C_E:C_E + NE] = np.arange(NE) - NE
    tok = np.arange(NP).reshape(NT, P).T
    cst[:, C_VALID:C_VALID + NT] = tok < NTOK
    cst[:, C_TROW:C_TROW + NT] = np.where(tok < NTOK, 0, TRASH + tok - NTOK)
    cst[:, C_K:C_K + XTRA] = np.arange(XTRA)
    cst[:, C_HM:C_HM + HG] = np.arange(P)[:, None] // HD == np.arange(HG)
    arrays = {
        "xT": np.concatenate([chunks(patches[:, max(2 * B, j * P) - 2 * B:min(NTOK, (j + 1) * P) - 2 * B])
                              for j in range(NT)], 1),
        "tokw": chunks(w[t0 + "W"].T),
        "cls_tok": np.asarray(cls_tok).reshape(1, D),
        "pos": w[t0 + "pos_embedding"].reshape(T - 1, D),
        "tok_b": w[t0 + "b"].reshape(1, D),
        "tok_cls": w[t0 + "cls_token"].reshape(1, D),
        "sel": sel,
        "ident": np.eye(P, dtype=np.float32),
        "tri": np.triu(np.ones((P, P), np.float32), 1),
        "cst": cst,
        "zero": np.zeros((P, D), np.float32),
        "pvec": np.concatenate([cols(w[a0 + n]) for n in ("x_r", "x_w", "x_k", "x_v", "x_a")]
                               + [cols(w[f0 + n]) for n in ("ln1_g", "ln1_b", "b1", "ln2_g", "ln2_b")], 1),
        "rows": np.concatenate([w[a0 + n].reshape(-1) for n in ("k_k", "k_a", "r_k", "gn_weight", "gn_bias")])[None],
        "brow": np.concatenate([w[a0 + "g_lora_bias"], w[f0 + "b2"], w[a1 + "bo"]])[None],
        "w4": np.concatenate([chunks(w[a0 + n]) for n in ("W_r", "W_k", "W_v", "W_o")], 1),
        "lora_a": chunks(np.concatenate([w[a0 + n + "_lora_a"] for n in "wag"], 1)),
        "wlb": w[a0 + "w_lora_b"], "wlbias": w[a0 + "w_lora_bias"][None],
        "alb": w[a0 + "a_lora_b"], "albias": w[a0 + "a_lora_bias"][None],
        "glb": w[a0 + "g_lora_b"],
        "w1t": chunks(w[f0 + "w1"].T), "w2t": chunks(w[f0 + "w2"].T),
        "wat": np.concatenate([chunks(w[a1 + n].T) for n in ("Wq", "Wk", "Wv", "Wo")], 1),
        "thr": w[a1 + "adaptive_threshold"].reshape(1, 1),
        "wrt": chunks(w[f1 + "w_router"].T),
        "gate_up": w[f1 + "gate_up_proj"], "down": w[f1 + "down_proj"],
        "wsh": chunks(np.concatenate([w[f1 + "w_gate"].T, w[f1 + "w_up"].T], 1)),
        "wsd": chunks(w[f1 + "w_down"].T),
    }
    arrays = {n: np.ascontiguousarray(m) for n, m in arrays.items()}
    nc = bacc.Bacc("TRN2", target_bir_lowering=False, num_devices=1)
    arrays = {"in_" + n: m for n, m in arrays.items()}
    args = {n[3:]: nc.dram_tensor(n, m.shape, mb.dt.from_np(m.dtype), kind="ExternalInput").ap()
            for n, m in arrays.items()}
    out = nc.dram_tensor("out", [NTOK, D], F32, kind="ExternalOutput").ap()
    build(nc, args, out)
    r = run_bass_kernel_spmd(nc, [arrays], core_ids=[0])
    return r.results[0]["out"].reshape(T, B, D).transpose(1, 0, 2)
```

```python
from contextlib import ExitStack

import concourse.bass as bass
from concourse import mybir

P = 128
B = 16
T = 38
D = 256
NT = 5
NP = NT * P
NTOK = B * T
TPT = P // B
GT = 4
NH, HD = 16, 16
KD = D // P
KP = 768 // P
HID = 1024
KH = HID // P
NE, F = 16, 512
KF = F // P
KEEP = T // 2
C = 80
RING = 8
XRING = 4
XTRA = -(-(NTOK // (C + 1)) // RING) * RING
TRASH = (NE + XTRA) * C
EPS = 1e-5
EXP_MINUS_HALF = 0.6065306597126334
NEG = -3.0e38
PA, PW, PB, PK, PV, PR = range(6)
NV = 6
HG = 8
CW = D // HG
ST = 2 * HD * HD
ROW = HG * NV * CW

F32 = mybir.dt.float32
I32 = mybir.dt.int32
ALU = mybir.AluOpType
ACT = mybir.ActivationFunctionType
X = mybir.AxisListType.X

MIX, LN1G, LN1B, B1, LN2G, LN2B, NPV = 0, 10, 12, 14, 22, 30, 38
C_E, C_VALID, C_TROW, C_K, C_HM, C_PADROW, NCST = 0, 16, 21, 26, 34, 42, 47
KK_, KA_, RK_, GNW, GNB = range(5)


class Link:

    def __init__(self, eng, sem):
        self.eng, self.sem, self.n = eng, sem, 0

    def __call__(self, ins):
        self.n += 1
        ins.then_inc(self.sem, 1)
        self.eng.wait_ge(self.sem, self.n)


def past(n, k):
    return not isinstance(n, int) or n >= k


def pipeline(eng, stages, count, unroll, peel):
    last = max(lag for _, lag in stages)
    assert peel % unroll == 0 and count % unroll == 0 and peel >= last
    for k in range(peel):
        for fn, lag in stages:
            if k >= lag:
                fn(k - lag, (k - lag) % unroll)
    with eng.Fori(peel // unroll, count // unroll) as i:
        for u in range(unroll):
            for fn, lag in stages:
                fn(i * unroll + (u - lag), (u - lag) % unroll)
    for k in range(count, count + last):
        for fn, lag in stages:
            if k - lag < count:
                fn(k - lag, (k - lag) % unroll)


def pipeline_rings(eng, stages, more):
    for k in range(RING):
        for fn, lag in stages:
            if k >= lag:
                fn(k - lag, k - lag)
    with eng.Fori(1, more + NE // RING) as i:
        for u in range(RING):
            for fn, lag in stages:
                fn(i * RING + (u - lag), (u - lag) % RING)
    for k in range(max(lag for _, lag in stages)):
        for fn, lag in stages:
            if k < lag:
                fn(more * RING + (NE + k - lag), (k - lag) % RING)


def scan_groups(j, group):
    for g in range(j * TPT // GT, min((j + 1) * TPT, T + GT - 1) // GT):
        group(g, min(GT, T - g * GT))


def build(nc, a, out):
    with ExitStack() as ctx:
        def sb(name, shape, dt=F32):
            return ctx.enter_context(nc.sbuf_tensor(name, shape, dt))

        def sem(name):
            return ctx.enter_context(nc.semaphore(name))

        def dram(name, shape):
            return nc.dram_tensor(name, shape, F32, kind="Internal").ap()

        psum = ctx.enter_context(nc.psum_tensor("psum", [P, 8 * 512], F32))

        def ps(bank, lo, hi, rows=P):
            return psum[0:rows, bank * 512 + lo:bank * 512 + hi]

        packed_dram = dram("packed_dram", [NP, ROW])
        o_dram = dram("o_dram", [NP, D])
        v_dram = dram("v_dram", [NP, D])
        xs_dram = dram("xs_dram", [TRASH + P, D])
        ys_dram = dram("ys_dram", [TRASH + P, D])

        ident, tri, ones = sb("ident", [P, P]), sb("tri", [P, P]), sb("ones", [P, P])
        neghalf = sb("neghalf", [P, NH])
        cst = sb("cst", [P, NCST])
        pvec = sb("pvec", [P, NPV])
        rows = sb("rows", [P, 5, D])
        brow = sb("brow", [1, 3, D])
        w4 = sb("w4", [P, 4, KD, D])
        lora_a = sb("lora_a", [P, KD, D])
        wlb, alb, glb = sb("wlb", [65, D]), sb("alb", [65, D]), sb("glb", [P, D])
        w1t = sb("w1t", [P, KD, HID])
        w2t = sb("w2t", [P, KH, D])
        wat = sb("wat", [P, 4, KD, D])
        wsh = sb("wsh", [P, KD, 2 * F])
        wsd = sb("wsd", [P, KF, D])
        wrt = sb("wrt", [P, KD, NE])
        thr, thr5 = sb("thr", [P, 1]), sb("thr5", [P, 5])
        absum = sb("absum", [P, KD + KH])
        tern = sb("tern", [P, 6])
        bc2 = sb("bc2", [P, 2, D])
        row2 = sb("row2", [1, 2, D])

        h_tok = sb("h_tok", [P, NT, D])
        xn_tok = sb("xn_tok", [P, NT, D])
        xnT = sb("xnT", [P, KD, B + NP])
        g_tok = sb("g_tok", [P, NT, D])
        bonus = sb("bonus", [P, NT, D])
        stat, mv = sb("stat", [P, NT, 6]), sb("mv", [P, NT, 2])
        ve, rstd = sb("ve", [P, NT]), sb("rstd", [P, NT])
        r1 = sb("r1", [P, 14976])
        r2 = sb("r2", [P, 10240])

        def carve(region, at, *shape):
            n = 1
            for s in shape:
                n *= s
            v = region[:, at:at + n]
            if len(shape) == 1:
                return v
            names = ["x", "y", "z", "w"][:len(shape)]
            return v.rearrange(f"p ({' '.join(names)}) -> p {' '.join(names)}",
                               **dict(zip(names, shape)))

        pack = carve(r1, 0, NT, HG, NV, CW)
        scan_in = carve(r1, NT * ROW, T * NV * CW)
        EARLY, GU, DN = 4, KD * 2 * F, KF * D
        w2g_at = EARLY * (GU + DN)
        w2g = carve(r1, w2g_at, KH, D + 1)
        selT = carve(r1, 4096, NP)
        table = carve(r1, 4096 + NP, D)
        tokw = carve(r1, 4096 + NP + D, KP, D)
        xT = carve(r2, 0, KP, NP)
        state, prod, outer, decayed, kv, carried = [carve(r2, 512 * i, ST) for i in range(6)]
        sr = sb("sr", [P, 2, GT, ST])
        mix = carve(r2, 4096, 2, 5, KD, P)
        rT, sgT = carve(r2, 4096, KD, NP), carve(r2, 4096 + KD * NP, NP)
        delta = carve(r2, 6656, KD, P)
        lwT, laT = carve(r2, 6912, 2, P), carve(r2, 7168, 2, P)
        kk, am, sqk = carve(r2, 7424, D), carve(r2, 7680, D), carve(r2, 7936, D)
        a_tok, w_tok = carve(r2, 8192, 2, D), carve(r2, 8704, D)
        o_scan = carve(r2, 8960, T * CW)
        gsq = carve(r2, 0, NT, D)
        hgT, sqT = carve(r2, 0, KH, NP), carve(r2, KH * NP, KH, NP)
        qT, kT = carve(r2, 0, KD, B * T), carve(r2, 1216, KD * B * T)
        qm = carve(r2, 2432, 2, 864)
        without8, without16 = carve(r2, 4160, 5, T), carve(r2, 4350, 5, T)
        ex, keep, pm = carve(r2, 4540, 2, 5, T), carve(r2, 4920, 2, 5, T), carve(r2, 5300, 2, 5, T)
        ptS = carve(r2, 5680, 2, NP)
        vS, oS = carve(r2, 6960, 2, D), carve(r2, 7472, 2, D)
        mx = carve(r2, 7984, 2, 5, 24)
        scS = carve(r2, 8224, 2, 5, T)
        shT = carve(r2, 0, KF, NP)
        gshT = carve(r2, 2560, NP)
        xs_tok = carve(r2, 3200, NT, D)
        xsS = carve(r2, 4480, XRING, D)
        xsT = carve(r2, 5504, XRING, KD, C)
        sgE = carve(r2, 6272, 2, KF * C)
        actE = carve(r2, 7040, 2, KF * C)
        ysS = carve(r2, 7808, 2, D)
        ysum = carve(r2, 8320, NT, D)
        ygat = g_tok

        ss, rn = sb("ss", [P, NH]), sb("rn", [P, NH])
        sa = sb("sa", [P, CW])
        bs = sb("bs", [P, NT, NH])
        gmu, gva, grs = sb("gmu", [P, NT, NH]), sb("gva", [P, NT, NH]), sb("grs", [P, NT, NH])
        fst = sb("fst", [P, NT, 6])
        nb, cthr, rinv = sb("nb", [P, 2, 5]), sb("cthr", [P, 2, 5]), sb("rinv", [P, 2, 5])
        lg, oh, rt1 = sb("lg", [P, NT, NE]), sb("oh", [P, NT, NE]), sb("rt1", [P, NT, NE])
        rt5 = sb("rt5", [P, 8, NT])
        ex16 = sb("ex16", [P, 4, NE])
        xk = sb("xk", [P, XTRA, NE])
        slot = sb("slot", [P, NT], I32)
        ctl = sb("ctl", [P, NE + XTRA + 1], I32)
        ctlf = sb("ctlf", [P, NE + XTRA + 1])
        cell = sb("cell", [P, 3])

        l_x = [sem(f"l_x{j}") for j in range(NT)]
        l_emb, l_tern, l_rw, l_cst, l_mid, l_late = [sem(f"l_{n}") for n in
                                                     ("emb", "tern", "rw", "cst", "mid", "late")]
        dve_step, act_step, pool_step = [sem(f"{n}_step") for n in ("dve", "act", "pool")]
        consts_set = sem("consts_set")
        abs_sum, abs_row, abs_one, abs_all = [sem("abs_" + n) for n in ("sum", "row", "one", "all")]
        tern_ready, rows2_mm, rows2_set, bc2_mm, bc2_set = [sem(n) for n in (
            "tern_ready", "rows2_mm", "rows2_set", "bc2_mm", "bc2_set")]
        emb_mm = sem("emb_mm")
        h_ready, ve_ready, rstd_ready, xn_ready, xT_mm, xT_ready = [sem(n) for n in (
            "h_ready", "ve_ready", "rstd_ready", "xn_ready", "xT_mm", "xT_ready")]
        mix_ready, proj_mm, lora_ready, z_mm = [sem(n) for n in ("mix_ready", "proj_mm", "lora_ready", "z_mm")]
        rv_packed, w_packed, a_ready = [sem(n) for n in ("rv_packed", "w_packed", "a_ready")]
        kk_ready, sq_ready, ss_ready, rn_ready, k_packed = [sem(n) for n in (
            "kk_ready", "sq_ready", "ss_ready", "rn_ready", "k_packed")]
        packed_out, scan_loaded = sem("packed_out"), sem("scan_loaded")
        LOADED = 16 * TPT
        scan_dve, scan_pool, o_mm, o_copied = [sem(n) for n in ("scan_dve", "scan_pool", "o_mm", "o_copied")]
        o_out, o_loaded = sem("o_out"), sem("o_loaded")
        rk_ready, bs_ready, bonus_ready = [sem(n) for n in ("rk_ready", "bs_ready", "bonus_ready")]
        rT_mm, rT_ready, ga_mm, sg_ready, g_mm, g_ready = [sem(n) for n in (
            "rT_mm", "rT_ready", "ga_mm", "sg_ready", "g_mm", "g_ready")]
        cen_ready, gsq_ready, gva_ready, grs_ready, y_ready = [sem(n) for n in (
            "cen_ready", "gsq_ready", "gva_ready", "grs_ready", "y_ready")]
        sqsum_ready = sem("sqsum_ready")
        yT_mm, yT_ready, wo_mm = sem("yT_mm"), sem("yT_ready"), sem("wo_mm")
        f1_mm, f1_ready, f2_mm, fv_ready, frs_ready = [sem(n) for n in (
            "f1_mm", "f1_ready", "f2_mm", "fv_ready", "frs_ready")]
        q_mm, q_ready, v_mm, v_ready, v_out = [sem(n) for n in (
            "q_mm", "q_ready", "v_mm", "v_ready", "v_out")]
        v_loaded = [sem("v_loaded0"), sem("v_loaded1")]
        qm_zero, qm_ready, sc_mm, sc_ready, nb_ready, keep_ready, exp_ready, pm_ready, rinv_ready, pn_ready = [
            sem(n) for n in ("qm_zero", "qm_ready", "sc_mm", "sc_ready", "nb_ready", "keep_ready", "exp_ready",
                             "pm_ready", "rinv_ready", "pn_ready")]
        top_step, sum_ready = sem("top_step"), sem("sum_ready")
        pt_mm, pt_ready, pv_mm, pv_ready, ot_mm, ot_ready, ao_mm = [sem(n) for n in (
            "pt_mm", "pt_ready", "pv_mm", "pv_ready", "ot_mm", "ot_ready", "ao_mm")]
        zero_out = sem("zero_out")
        lg_mm, oh_ready, score_in, score_ready, cnt_mm, slot_ready, ctl_ready = [sem(n) for n in (
            "lg_mm", "oh_ready", "score_in", "score_ready", "cnt_mm", "slot_ready", "ctl_ready")]
        xs_ready = sem("xs_ready")
        xs_out = [sem(f"xs_out{j}") for j in range(NT)]
        sh_mm, sh_silu, sh_ready, sd_mm, ysum_ready = [sem(n) for n in (
            "sh_mm", "sh_silu", "sh_ready", "sd_mm", "ysum_ready")]
        w_loaded = [sem(f"w_loaded{i}") for i in range(RING)]
        x_loaded = [sem(f"x_loaded{i}") for i in range(RING)]
        ex_mm, ex_ready, gu_mm, silu_ready, act_ready, y_mm, ys_ready = [sem(n) for n in (
            "ex_mm", "ex_ready", "gu_mm", "silu_ready", "act_ready", "y_mm", "ys_ready")]
        ys_out = [sem("ys_out0"), sem("ys_out1")]
        yg_loaded = [sem(f"yg_loaded{j}") for j in range(NT)]
        res_ready, stored = sem("res_ready"), sem("stored")

        SCAN_DVE, SCAN_POOL = 6, 3
        GROUPS = -(-T // GT)
        STEPS = [min(TPT, T - TPT * j) for j in range(NT)]

        sr_flat = sr[:].rearrange("p s u x -> p (s u x)")

        def flat(w):
            return w[:].rearrange("p a b -> p (a b)")

        wgu = [carve(r1, i * GU, KD, 2 * F) for i in range(EARLY)] + [
            w.rearrange("p (k n) -> p k n", k=KD) for w in (
                flat(w1t), flat(w2t), w4[:].rearrange("p w k n -> p (w k n)"), sr_flat[:, 0:GU])]
        wdn = [carve(r1, EARLY * GU + i * DN, KF, D) for i in range(EARLY)] + [
            w.rearrange("p (k n) -> p k n", k=KF) for w in (
                sr_flat[:, GU:GU + DN], sr_flat[:, GU + DN:GU + 2 * DN],
                r1[:, w2g_at:w2g_at + DN], r1[:, w2g_at + DN:w2g_at + 2 * DN])]

        def tcol(t, v):
            return scan_in[:, bass.ds(t * (NV * CW) + v * CW, CW)].rearrange("p (h j) -> p h j", h=2)

        def along_i(v):
            return v.unsqueeze(2).broadcast_to([P, 2, HD, HD])

        def along_j(v):
            return v.unsqueeze(3).broadcast_to([P, 2, HD, HD])

        def s4(v):
            return v.rearrange("p (h i j) -> p h i j", h=2, i=HD)

        def wgu_src(e):
            return a["gate_up"][e].rearrange("(k p) n -> p k n", p=P)

        def wdn_src(e):
            return a["down"][e].rearrange("(k p) n -> p k n", p=P)

        block = ctx.enter_context(nc.Block())

        @block.sync
        def _(sp):
            def load_patches(j):
                lo, hi = max(2 * B, j * P), min(NTOK, (j + 1) * P)
                src = a["xT"][:, KP * (lo - 2 * B):KP * (hi - 2 * B)]
                sp.dma_start(xT[:, :, lo:hi], src.rearrange("p (k n) -> p k n", k=KP)).then_inc(l_x[j], 16)

            load_patches(0)
            sp.dma_start(tokw, a["tokw"].rearrange("p (k n) -> p k n", k=KP)).then_inc(l_emb, 16)
            sp.dma_start(selT[0:40], a["sel"]).then_inc(l_emb, 16)
            sp.dma_start(table[0:1], a["cls_tok"]).then_inc(l_emb, 16)
            sp.dma_start(table[1:38], a["pos"]).then_inc(l_emb, 16)
            sp.dma_start(table[38:39], a["tok_b"]).then_inc(l_emb, 16)
            sp.dma_start(table[39:40], a["tok_cls"]).then_inc(l_emb, 16)
            for j in range(1, NT):
                load_patches(j)
            sp.dma_start(ident[:], a["ident"]).then_inc(l_cst, 16)
            sp.dma_start(pvec[:], a["pvec"]).then_inc(l_cst, 16)
            sp.dma_start(lora_a[:], a["lora_a"].rearrange("p (k n) -> p k n", k=KD)).then_inc(l_rw, 16)
            sp.dma_start(w4[:], a["w4"].rearrange("p (w k n) -> p w k n", w=4, k=KD)).then_inc(l_rw, 16)
            sp.dma_start(wlb[0:64], a["wlb"]).then_inc(l_rw, 16)
            sp.dma_start(wlb[64:65], a["wlbias"]).then_inc(l_rw, 16)
            sp.dma_start(alb[0:64], a["alb"]).then_inc(l_rw, 16)
            sp.dma_start(alb[64:65], a["albias"]).then_inc(l_rw, 16)
            sp.dma_start(rows[:], a["rows"].broadcast_to([P, 5 * D]).rearrange("p (r n) -> p r n", r=5)).then_inc(l_rw, 16)
            sp.dma_start(w1t[:], a["w1t"].rearrange("p (k n) -> p k n", k=KD)).then_inc(l_tern, 16)
            sp.dma_start(w2t[:], a["w2t"].rearrange("p (k n) -> p k n", k=KH)).then_inc(l_tern, 16)
            sp.dma_start(brow[:], a["brow"].rearrange("o (r n) -> o r n", r=3)).then_inc(l_tern, 16)
            sp.dma_start(glb[:], a["glb"]).then_inc(l_mid, 16)
            sp.dma_start(cst[:], a["cst"]).then_inc(l_mid, 16)
            sp.dma_start(wat[:], a["wat"].rearrange("p (w k n) -> p w k n", w=4, k=KD)).then_inc(l_mid, 16)
            sp.dma_start(tri[:], a["tri"]).then_inc(l_late, 16)
            sp.dma_start(wsh[:], a["wsh"].rearrange("p (k n) -> p k n", k=KD)).then_inc(l_late, 16)
            sp.dma_start(wsd[:], a["wsd"].rearrange("p (k n) -> p k n", k=KF)).then_inc(l_late, 16)
            sp.dma_start(wrt[:], a["wrt"].rearrange("p (k n) -> p k n", k=KD)).then_inc(l_late, 16)
            sp.dma_start(thr[:], a["thr"].broadcast_to([P, 1])).then_inc(l_late, 16)

            def repack(j):
                steps = STEPS[j]
                sp.wait_ge(rv_packed, j + 1)
                sp.wait_ge(w_packed, j + 1)
                sp.wait_ge(k_packed, j + 1)
                if j == 0:
                    for t in range(steps):
                        dst = scan_in[:, t * NV * CW:(t + 1) * NV * CW]
                        src = pack[t * B:(t + 1) * B, j].rearrange("p h v c -> p h (v c)")
                        sp.dma_start(dst, src).then_inc(scan_loaded, 16)
                    return
                sp.dma_start(packed_dram[j * P:(j + 1) * P], pack[:, j].rearrange("p h v c -> p (h v c)"))\
                  .then_inc(packed_out, 16)
                sp.wait_ge(packed_out, 16 * j)
                dst = scan_in[:, j * TPT * NV * CW:(j * TPT + steps) * NV * CW]
                sp.dma_start(dst.rearrange("p (t x) -> p t x", t=steps),
                             packed_dram[j * P:j * P + steps * B].rearrange("(t b) (h x) -> (b h) t x", b=B, h=HG))\
                  .then_inc(scan_loaded, 16)

            def fetch_o(j):
                steps = STEPS[j]
                sp.wait_ge(o_copied, -(-(j * TPT + steps) // GT) + 1)
                src = o_scan[:, j * TPT * CW:(j * TPT + steps) * CW].rearrange("p (t c) -> p t c", t=steps)
                sp.dma_start(o_dram[j * P:j * P + steps * B].rearrange("(t b) (h c) -> (b h) t c", b=B, h=HG), src)\
                  .then_inc(o_out, 16)
                sp.wait_ge(o_out, 16 * (j + 1))
                sp.wait_ge(xT_mm, j + 1)
                sp.dma_start(xn_tok[0:steps * B, j], o_dram[j * P:j * P + steps * B]).then_inc(o_loaded, 16)

            repack(0)
            for buf, first, end in ((xs_dram, 0, TRASH + P), (ys_dram, NE * C, TRASH + P)):
                for lo in range(first, end, P):
                    hi = min(lo + P, end)
                    sp.dma_start(buf[lo:hi], a["zero"][0:hi - lo]).then_inc(zero_out, 16)
            repack(1)
            repack(2)
            repack(3)
            fetch_o(0)
            repack(4)
            for j in range(1, NT):
                fetch_o(j)

            sp.wait_ge(bonus_ready, NT)
            sp.wait_ge(scan_pool, SCAN_POOL * T + 1)
            sp.wait_ge(scan_dve, SCAN_DVE * T + 2)

            def load_w(e, s):
                sp.dma_start(wgu[s], wgu_src(e)).then_inc(w_loaded[s], 16)
                sp.dma_start(wdn[s], wdn_src(e)).then_inc(w_loaded[s], 16)

            for e in range(EARLY):
                load_w(e, e)
            sp.wait_ge(f2_mm, NT)
            for e in range(EARLY, RING):
                load_w(e, e)
            for j in range(NT):
                sp.wait_ge(v_ready, j + 1)
                sp.dma_start(v_dram[j * P:(j + 1) * P], g_tok[:, j]).then_inc(v_out, 16)
            sp.wait_ge(v_out, 16 * NT)
            v_img = v_dram[0:NTOK].rearrange("(t b) c -> b t c", b=B)

            def load_v(n, s):
                if past(n, 2):
                    sp.wait_ge(pv_mm, n - 1)
                sp.dma_start(vS[0:T, s], v_img[n]).then_inc(v_loaded[s], 16)

            pipeline(sp, [(load_v, 0)], B, 2, 2)

            sp.wait_ge(ctl_ready, 1)
            more = sp.value_load(ctl[0:1, NE + XTRA:NE + XTRA + 1], min_val=0, max_val=XTRA // RING)
            for j in range(NT):
                sp.wait_ge(xs_out[j], 16)

            def load_x(e, s):
                if past(e, XRING):
                    sp.wait_ge(ex_mm, e - XRING + 1)
                sp.dma_start(xsS[0:C, s % XRING], xs_dram[bass.ds(e * C, C)]).then_inc(x_loaded[s], 16)

            def load_next(e, s):
                if past(e, RING):
                    expert = sp.value_load(ctl[0:1, bass.ds(e, 1)], min_val=0, max_val=NE - 1)
                    sp.wait_ge(y_mm, e - RING + 1)
                    load_w(expert, s)

            def store_y(e, s):
                sp.wait_ge(ys_ready, e + 1)
                sp.dma_start(ys_dram[bass.ds(e * C, C)], ysS[0:C, s % 2]).then_inc(ys_out[s % 2], 16)

            pipeline_rings(sp, [(load_x, 0), (load_next, 0), (store_y, 3)], more)

            for j in range(NT):
                sp.wait_ge(res_ready, j + 1)
                n = min(P, NTOK - j * P)
                sp.dma_start(out[j * P:j * P + n], xn_tok[0:n, j]).then_inc(stored, 16)
            sp.wait_ge(stored, 16 * NT)

        @block.tensor
        def _(pe):
            mm = nc.tensor.matmul

            def layer(dst, lhs, rhs, chunks, inc=None):
                for k in range(chunks):
                    ins = mm(dst, lhs(k), rhs(k), start=(k == 0), stop=(k == chunks - 1))
                return ins

            def turn(s, j):
                pe.wait_ge(xn_ready, NT * s + j + 1)
                if NT * s + j >= 2:
                    pe.wait_ge(xT_ready, NT * s + j - 1)
                for k in range(KD):
                    ins = nc.tensor.transpose(ps(j % 2, 256 + k * P, 256 + (k + 1) * P),
                                              xn_tok[:, j, k * P:(k + 1) * P], ident[:])
                ins.then_inc(xT_mm, 1)

            pe.wait_ge(consts_set, 2)

            def abs_row_of(i, bank, k0, kn):
                pe.wait_ge(abs_sum, i + 1)
                for k in range(kn):
                    ins = mm(ps(bank, k * P, (k + 1) * P, 1), absum[:, k0 + k:k0 + k + 1], ident[:],
                             start=True, stop=True)
                ins.then_inc(abs_row, 1)

            def abs_to_all(i, bank):
                pe.wait_ge(abs_one, i + 1)
                mm(ps(bank, 0, 1), ones[0:1, :], tern[0:1, 3 * i:3 * i + 1], start=True, stop=True)\
                    .then_inc(abs_all, 1)

            pe.wait_ge(l_emb, 16 * 6)
            for j in range(NT):
                pe.wait_ge(l_x[j], 16)
                if j >= 2:
                    pe.wait_ge(h_ready, j - 1)
                dst = ps(j % 2, 0, D)
                for k in range(KP):
                    mm(dst, xT[:, k, j * P:(j + 1) * P], tokw[:, k], start=(k == 0), stop=False)
                mm(dst, selT[0:40, j * P:(j + 1) * P], table[0:40], start=False, stop=True).then_inc(emb_mm, 1)
            pe.wait_ge(l_cst, 32)
            pe.wait_ge(h_ready, NT)
            for j in range(NT):
                turn(0, j)

            def project(j):
                if j == 0:
                    pe.wait_ge(l_rw, 16 * 7)
                pe.wait_ge(mix_ready, j + 1)
                if j >= 2:
                    pe.wait_ge(k_packed, j - 1)
                    pe.wait_ge(rv_packed, j - 1)
                    pe.wait_ge(lora_ready, j - 1)
                m = mix[:, j % 2]
                layer(ps(2 + j % 2, 0, D), lambda k: m[:, 0, k], lambda k: w4[:, 0, k], KD)
                layer(ps(2 + j % 2, D, 2 * D), lambda k: m[:, 2, k], lambda k: w4[:, 1, k], KD)
                layer(ps(4 + j % 2, 0, D), lambda k: m[:, 3, k], lambda k: w4[:, 2, k], KD)
                layer(ps(4 + j % 2, D, D + P, 64), lambda k: lora_a[:, k, 0:64], lambda k: m[:, 1, k], KD)
                layer(ps(4 + j % 2, D + P, D + 2 * P, 64), lambda k: lora_a[:, k, 64:128], lambda k: m[:, 4, k], KD)\
                    .then_inc(proj_mm, 1)

            def lora_out(j):
                pe.wait_ge(lora_ready, j + 1)
                if j >= 2:
                    pe.wait_ge(a_ready, j - 1)
                ins = mm(ps(6 + j % 2, 0, D), lwT[0:65, j % 2], wlb[:], start=True, stop=True)
                if j < 2:
                    ins.then_inc(o_mm, 1)
                mm(ps(6 + j % 2, D, 2 * D), laT[0:65, j % 2], alb[:], start=True, stop=True).then_inc(z_mm, 1)

            def scan_out(j):
                def group(g, steps):
                    pe.wait_ge(scan_dve, g * (GT * SCAN_DVE) + (steps * SCAN_DVE + 2))
                    pe.wait_ge(o_copied, g + 1)
                    src = sr_flat[:, bass.ds((g - j * TPT // GT) * (GT * ST), steps * ST)]
                    src = src.rearrange("p (x j) -> p j x", j=HD)
                    for jj in range(HD):
                        ins = mm(ps(0, 0, steps * CW), ident[:], src[:, jj], start=(jj == 0), stop=(jj == HD - 1))
                    ins.then_inc(o_mm, 1)

                scan_groups(j, group)

            def gate_turn():
                for j in range(NT):
                    pe.wait_ge(rv_packed, j + 1)
                    pe.wait_ge(a_ready, NT)
                    pe.wait_ge(w_packed, NT)
                    if j >= 2:
                        pe.wait_ge(rT_ready, j - 1)
                    for k in range(KD):
                        ins = nc.tensor.transpose(ps(6 + j % 2, k * P, (k + 1) * P),
                                                  g_tok[:, j, k * P:(k + 1) * P], ident[:])
                    ins.then_inc(rT_mm, 1)

            def gate_hidden():
                pe.wait_ge(rT_ready, NT)
                pe.wait_ge(lora_ready, NT)
                for lo, hi in ((0, 512), (512, NP)):
                    ins = layer(psum[:, 4 * 512 + lo:4 * 512 + hi], lambda k: lora_a[:, k, P:2 * P],
                                lambda k: rT[:, k, lo:hi], KD)
                ins.then_inc(ga_mm, 1)

            def gate():
                pe.wait_ge(sg_ready, 1)
                pe.wait_ge(l_mid, 48)
                for j in range(NT):
                    if j >= 2:
                        pe.wait_ge(g_ready, j - 1)
                    mm(ps(6 + j % 2, 0, D), sgT[:, j * P:(j + 1) * P], glb[:], start=True, stop=False)
                    mm(ps(6 + j % 2, 0, D), ones[0:1, :], brow[0:1, 0], start=False, stop=True).then_inc(g_mm, 1)

            project(0)
            pe.wait_ge(xT_ready, NT)
            abs_row_of(0, 1, 0, KD)
            lora_out(0)
            project(1)
            lora_out(1)
            abs_to_all(0, 1)
            project(2)
            lora_out(2)
            scan_out(0)
            project(3)
            lora_out(3)
            scan_out(1)
            project(4)
            lora_out(4)
            scan_out(2)
            gate_turn()
            scan_out(3)
            gate_hidden()
            scan_out(4)
            gate()
            for j in range(NT):
                pe.wait_ge(y_ready, j + 1)
                if j >= 2:
                    pe.wait_ge(yT_ready, j - 1)
                for k in range(KD):
                    ins = nc.tensor.transpose(ps(1 + j % 2, 256 + k * P, 256 + (k + 1) * P),
                                              xn_tok[:, j, k * P:(k + 1) * P], ident[:])
                ins.then_inc(yT_mm, 1)
                pe.wait_ge(yT_ready, j + 1)
                if j >= 2:
                    pe.wait_ge(h_ready, NT + j - 1)
                layer(ps(3 + j % 2, 0, D), lambda k: xnT[:, k, B + j * P:B + (j + 1) * P],
                      lambda k: w4[:, 3, k], KD).then_inc(wo_mm, 1)

            for j in range(NT):
                turn(1, j)
            pe.wait_ge(xT_ready, 2 * NT)
            pe.wait_ge(h_ready, 2 * NT)
            pe.wait_ge(tern_ready, 1)
            for m in range(KH):
                if m == 1:
                    pe.wait_ge(g_ready, NT)
                    abs_row_of(1, 6, KD, KH)
                if m == 2:
                    abs_to_all(1, 6)
                if m == 5:
                    pe.wait_ge(tern_ready, 2)
                    for c, col in ((0, LN2G), (1, LN2B)):
                        ins = layer(ps(6 + c, 0, D, 1), lambda k: pvec[:, col + k:col + k + 1],
                                    lambda k: w2t[:, k], KH)
                    ins.then_inc(rows2_mm, 1)
                if m >= 3:
                    pe.wait_ge(f1_ready, m - 2)
                base = 2 * (m % 3) * 512
                for lo, hi in ((0, 512), (512, NP)):
                    ins = layer(psum[:, base + lo:base + hi], lambda k: w1t[:, k, m * P:(m + 1) * P],
                                lambda k: xnT[:, k, B + lo:B + hi], KD)
                ins.then_inc(f1_mm, 1)
            pe.wait_ge(rows2_set, 1)
            pe.wait_ge(f1_ready, KH - 2)
            for c in range(2):
                ins = mm(ps(4, c * D, (c + 1) * D), ones[0:1, :], row2[0:1, c], start=True, stop=True)
            ins.then_inc(bc2_mm, 1)
            pe.wait_ge(f1_ready, KH)
            for j in range(NT):
                if j >= 2:
                    pe.wait_ge(h_ready, 2 * NT + j - 1)
                layer(ps(6 + j % 2, 0, D + 1), lambda k: hgT[:, k, j * P:(j + 1) * P], lambda k: w2g[:, k], KH)
                pe.wait_ge(sqsum_ready, 1)
                mm(ps(6 + j % 2, 300, 301), sqT[:, 0, j * P:(j + 1) * P], ones[:, 0:1], start=True, stop=True)\
                    .then_inc(f2_mm, 1)

            for j in range(NT):
                turn(2, j)
            pe.wait_ge(xT_ready, 3 * NT)
            pe.wait_ge(h_ready, 3 * NT)
            for w in range(2):
                for m in range(KD):
                    base = 2 * (1 + w * KD + m if w * KD + m < 3 else 1) * 512
                    if w * KD + m == 3:
                        pe.wait_ge(q_ready, 1)
                    for lo, hi in ((0, 512), (512, NP)):
                        ins = layer(psum[:, base + lo:base + hi], lambda k: wat[:, w, k, m * P:(m + 1) * P],
                                    lambda k: xnT[:, k, B + lo:B + hi], KD)
                    ins.then_inc(q_mm, 1)
            pe.wait_ge(q_ready, 4)

            def project_v():
                for j in range(NT):
                    if j >= 2:
                        pe.wait_ge(v_ready, j - 1)
                    layer(ps(6 + j % 2, 0, D), lambda k: xnT[:, k, B + j * P:B + (j + 1) * P],
                          lambda k: wat[:, 2, k], KD).then_inc(v_mm, 1)

            def scores(n, s):
                pe.wait_ge(qm_ready, n + 1)
                if past(n, 2):
                    pe.wait_ge(sc_ready, n - 1)
                for tile, parts in enumerate((
                        ((0, 0, 64),), ((128, 0, P),), ((256, 0, P), (384, 1, 64)), ((512, 1, P),), ((640, 1, P),))):
                    for i, (at, half, hi) in enumerate(parts):
                        ins = mm(ps(s, tile * T, (tile + 1) * T), qm[0:hi, s, at:at + P],
                                 kT[0:hi, half * B * T + n * T:half * B * T + (n + 1) * T],
                                 start=(i == 0), stop=(i == len(parts) - 1))
                ins.then_inc(sc_mm, 1)

            def turn_probs(n, s):
                pe.wait_ge(pn_ready, n + 1)
                if past(n, 2):
                    pe.wait_ge(pt_ready, n - 1)
                for tile in range(5):
                    ins = nc.tensor.transpose(ps(2 + 2 * s, tile * P, (tile + 1) * P, T), pm[:, s, tile], ident[:])
                ins.then_inc(pt_mm, 1)

            def values(n, s):
                pe.wait_ge(pt_ready, n + 1)
                pe.wait_ge(v_loaded[s], (n - s) * 8 + 16)
                if past(n, 2):
                    pe.wait_ge(ot_ready, n - 1)
                for hh in range(NH):
                    ins = mm(ps(6 + s, hh * HD, (hh + 1) * HD, T), ptS[0:T, s, hh * T:(hh + 1) * T],
                             vS[0:T, s, hh * HD:(hh + 1) * HD], start=True, stop=True)
                ins.then_inc(pv_mm, 1)

            def turn_out(n, s):
                pe.wait_ge(pv_ready, n + 1)
                for k in range(KD):
                    ins = nc.tensor.transpose(ps(6 + s, 256 + k * T, 256 + (k + 1) * T),
                                              oS[0:T, s, k * P:(k + 1) * P], ident[0:T, 0:T])
                ins.then_inc(ot_mm, 1)

            for k in range(B + 4):
                for fn, lag in ((scores, 0), (turn_probs, 2), (values, 3), (turn_out, 4)):
                    if 0 <= k - lag < B:
                        fn(k - lag, (k - lag) % 2)
                if k == 1:
                    project_v()

            pe.wait_ge(ot_ready, B)
            for j in range(NT):
                if j >= 2:
                    pe.wait_ge(h_ready, 3 * NT + j - 1)
                dst = ps(2 + j % 2, 0, D)
                for k in range(KD):
                    mm(dst, xnT[:, k, B + j * P:B + (j + 1) * P], wat[:, 3, k], start=(k == 0), stop=False)
                mm(dst, ones[0:1, :], brow[0:1, 2], start=False, stop=True).then_inc(ao_mm, 1)

            pe.wait_ge(l_late, 16 * 5)
            for j in range(NT):
                turn(3, j)
                pe.wait_ge(xT_ready, 3 * NT + j + 1)
                layer(ps(7, j * NE, (j + 1) * NE), lambda k: xnT[:, k, B + j * P:B + (j + 1) * P],
                      lambda k: wrt[:, k], KD).then_inc(lg_mm, 1)
            for f in range(KF):
                if f == 1:
                    pe.wait_ge(oh_ready, 1)
                    for j in range(NT):
                        dst = ps(3, j * NE, (j + 1) * NE)
                        for i in range(j):
                            mm(dst, ones[:], oh[:, i], start=(i == 0), stop=False)
                        mm(dst, tri[:], oh[:, j], start=(j == 0), stop=True)
                    layer(ps(3, NT * NE, (NT + 1) * NE), lambda k: ones[:], lambda k: oh[:, k], NT).then_inc(cnt_mm, 1)
                for u in range(2):
                    n = 2 * f + u
                    bnk = (4, 6)[u]
                    if n == 1:
                        pe.wait_ge(score_in, 1)
                    if f >= 1:
                        pe.wait_ge(sh_ready if u else sh_silu, f)
                    for lo, hi in ((0, 512), (512, NP)):
                        ins = layer(psum[:, bnk * 512 + lo:bnk * 512 + hi],
                                    lambda k: wsh[:, k, u * F + f * P:u * F + (f + 1) * P],
                                    lambda k: xnT[:, k, B + lo:B + hi], KD)
                    ins.then_inc(sh_mm, 1)
            def item_T(s, bnk=0):
                for k in range(KD):
                    ins = nc.tensor.transpose(ps(bnk, k * C, (k + 1) * C), xsS[0:C, s % XRING, k * P:(k + 1) * P],
                                              ident[0:C, 0:C])
                return ins

            def item_gu(s, u):
                for f in range(2 * KF):
                    ins = layer(ps(2 + 2 * u + f // KF, (f % KF) * C, (f % KF + 1) * C),
                                lambda k: wgu[s][:, k, f * P:(f + 1) * P], lambda k: xsT[:, s % XRING, k], KD)
                return ins

            def item_y(s, u):
                return layer(ps(6 + u, 0, D, C), lambda k: actE[:, u, k * C:(k + 1) * C],
                             lambda k: wdn[s][:, k], KF)

            def expert_T(e, s):
                pe.wait_ge(x_loaded[s], (e - s) * (16 // RING) + 16)
                if past(e, 2):
                    pe.wait_ge(ex_ready, e - 1)
                item_T(s, s % 2).then_inc(ex_mm, 1)

            def expert_gu(e, s):
                if isinstance(e, int) and e == 1:
                    pe.wait_ge(sh_ready, KF)
                pe.wait_ge(ex_ready, e + 1)
                pe.wait_ge(w_loaded[s], (e - s) * (32 // RING) + 32)
                if past(e, 2):
                    pe.wait_ge(act_ready, e - 1)
                item_gu(s, s % 2).then_inc(gu_mm, 1)

            def expert_y(e, s):
                pe.wait_ge(act_ready, e + 1)
                if past(e, 2):
                    pe.wait_ge(ys_ready, e - 1)
                item_y(s, s % 2).then_inc(y_mm, 1)

            pe.wait_ge(ctl_ready, 1)
            more = pe.value_load(ctl[0:1, NE + XTRA:NE + XTRA + 1], min_val=0, max_val=XTRA // RING)
            pipeline_rings(pe, [(expert_T, 0), (expert_gu, 1), (expert_y, 2)], more)

            for j in range(NT):
                if j >= 2:
                    pe.wait_ge(ysum_ready, j - 1)
                layer(ps(4 + j % 2, 0, D), lambda k: shT[:, k, j * P:(j + 1) * P], lambda k: wsd[:, k], KF)\
                    .then_inc(sd_mm, 1)

        @block.scalar
        def _(act):
            fn = nc.scalar.activation
            step = Link(act, act_step)

            def load_table(func):
                step(fn(cell[:, 2:3], ones[:, 0:1], func))

            act.wait_ge(consts_set, 2)
            load_table(ACT.Sigmoid)

            for j in range(NT):
                act.wait_ge(emb_mm, j + 1)
                fn(h_tok[:, j], ps(j % 2, 0, D), ACT.Copy).then_inc(h_ready, 1)

            def turned(s, j):
                act.wait_ge(xT_mm, NT * s + j + 1)
                src = ps(j % 2, 256, 512).rearrange("p (k n) -> p k n", k=KD)
                dst = xnT[:, :, B + j * P:B + (j + 1) * P]
                if s == 1:
                    fn(dst[:, 0], src[:, 0], ACT.Identity, scale=pvec[:, LN1G:LN1G + 1], bias=pvec[:, LN1B:LN1B + 1])
                    fn(dst[:, 1], src[:, 1], ACT.Identity, scale=pvec[:, LN1G + 1:LN1G + 2],
                       bias=pvec[:, LN1B + 1:LN1B + 2]).then_inc(xT_ready, 1)
                else:
                    fn(dst, src, ACT.Copy).then_inc(xT_ready, 1)

            for j in range(NT):
                turned(0, j)

            def lora(j):
                act.wait_ge(proj_mm, j + 1)
                if j >= 2:
                    act.wait_ge(z_mm, j - 1)
                step(fn(lwT[0:64, j % 2], ps(4 + j % 2, D, D + P, 64), ACT.Sigmoid, scale=2.0))
                ins = fn(laT[0:64, j % 2], ps(4 + j % 2, D + P, D + 2 * P, 64), ACT.Copy)
                if j == 0:
                    ins.then_inc(o_copied, 1)
                fn(lwT[0:64, j % 2], lwT[0:64, j % 2], ACT.Copy, scale=2.0, bias=-1.0).then_inc(lora_ready, 1)
                fn(g_tok[:, j], ps(2 + j % 2, 0, D), ACT.Copy)
                fn(pack[:, j, :, PR], ps(2 + j % 2, 0, D).rearrange("p (h c) -> p h c", h=HG), ACT.Copy)
                fn(pack[:, j, :, PV], ps(4 + j % 2, 0, D).rearrange("p (h c) -> p h c", h=HG), ACT.Copy)\
                    .then_inc(rv_packed, 1)

            def gates(j):
                act.wait_ge(z_mm, j + 1)
                if j >= 2:
                    act.wait_ge(k_packed, j - 1)
                if j >= 1:
                    act.wait_ge(w_packed, j)
                fn(a_tok[:, j % 2], ps(6 + j % 2, D, 2 * D), ACT.Sigmoid).then_inc(a_ready, 1)
                step(fn(w_tok, ps(6 + j % 2, 0, D), ACT.Sigmoid))
                fn(pack[:, j, :, PW], w_tok.rearrange("p (h c) -> p h c", h=HG), ACT.Copy, scale=EXP_MINUS_HALF)\
                    .then_inc(w_packed, 1)

            def square_k(j):
                act.wait_ge(kk_ready, j + 1)
                if j >= 1:
                    act.wait_ge(ss_ready, j)
                fn(sqk, kk, ACT.Square).then_inc(sq_ready, 1)

            def scan_copy(j, between=None):
                def group(g, steps):
                    act.wait_ge(o_mm, g + 3)
                    fn(o_scan[:, bass.ds(g * (GT * CW), steps * CW)], ps(0, 0, steps * CW), ACT.Copy)\
                        .then_inc(o_copied, 1)

                last = (j + 1) * TPT // GT - 1

                def copy(g, steps):
                    if between is not None and g == last:
                        square_k(between)
                    group(g, steps)

                scan_groups(j, copy)

            def gate_turned():
                for j in range(NT):
                    act.wait_ge(rT_mm, j + 1)
                    fn(rT[:, :, j * P:(j + 1) * P], ps(6 + j % 2, 0, 256).rearrange("p (k n) -> p k n", k=KD),
                       ACT.Copy).then_inc(rT_ready, 1)

            def gate_sigmoid():
                act.wait_ge(ga_mm, 1)
                fn(sgT, psum[:, 4 * 512:4 * 512 + NP], ACT.Sigmoid).then_inc(sg_ready, 1)

            def gate():
                for j in range(NT):
                    act.wait_ge(g_mm, j + 1)
                    fn(g_tok[:, j], ps(6 + j % 2, 0, D), ACT.Copy).then_inc(g_ready, 1)

            act.wait_ge(consts_set, 2)
            lora(0)
            gates(0)
            square_k(0)
            lora(1)
            gates(1)
            square_k(1)
            lora(2)
            gates(2)
            scan_copy(0, 2)
            lora(3)
            gates(3)
            scan_copy(1, 3)
            lora(4)
            gates(4)
            scan_copy(2, 4)
            gate_turned()
            scan_copy(3)
            gate_sigmoid()
            scan_copy(4)
            gate()

            for j in range(NT):
                act.wait_ge(cen_ready, j + 1)
                fn(gsq[:, j], xn_tok[:, j], ACT.Square).then_inc(gsq_ready, 1)
            load_table(ACT.Sqrt)
            act.wait_ge(gva_ready, NT)
            fn(grs[:], gva[:], ACT.Sqrt).then_inc(grs_ready, 1)
            for j in range(NT):
                act.wait_ge(yT_mm, j + 1)
                fn(xnT[:, :, B + j * P:B + (j + 1) * P],
                   ps(1 + j % 2, 256, 512).rearrange("p (k n) -> p k n", k=KD), ACT.Copy).then_inc(yT_ready, 1)
            load_table(ACT.Gelu)
            for j in range(NT):
                turned(1, j)
            for m in range(KH):
                act.wait_ge(f1_mm, m + 1)
                base = 2 * (m % 3) * 512
                step(fn(hgT[:, m], psum[:, base:base + NP], ACT.Gelu, scale=tern[:, 1:2], bias=pvec[:, B1 + m:B1 + m + 1]))
                fn(sqT[:, m], hgT[:, m], ACT.Square).then_inc(f1_ready, 1)
            act.wait_ge(bc2_mm, 1)
            fn(bc2[:].rearrange("p r n -> p (r n)"), ps(4, 0, 2 * D), ACT.Copy).then_inc(bc2_set, 1)

            for j in range(NT):
                turned(2, j)
            for w in range(2):
                for m in range(KD):
                    base = 2 * (1 + w * KD + m if w * KD + m < 3 else 1) * 512
                    dst = qT[:, m] if w == 0 else kT[:, m * B * T:(m + 1) * B * T]
                    act.wait_ge(q_mm, w * KD + m + 1)
                    fn(dst.rearrange("p (b t) -> p b t", b=B),
                       psum[:, base:base + NTOK].rearrange("p (t b) -> p b t", b=B), ACT.Copy).then_inc(q_ready, 1)
            load_table(ACT.Exp)

            def copy_scores(n, s):
                act.wait_ge(sc_mm, n + 1)
                if past(n, 2):
                    act.wait_ge(keep_ready, n - 1)
                    act.wait_ge(exp_ready, n - 1)
                fn(scS[:, s].rearrange("p i k -> p (i k)"), ps(s, 0, 5 * T), ACT.Copy).then_inc(sc_ready, 1)

            def exps(n, s):
                act.wait_ge(nb_ready, n + 1)
                if past(n, 2):
                    act.wait_ge(pm_ready, n - 1)
                for tile in range(5):
                    ins = fn(ex[:, s, tile], scS[:, s, tile], ACT.Exp, scale=0.25,
                             bias=nb[:, s, tile:tile + 1])
                ins.then_inc(exp_ready, 1)
                if isinstance(n, int) and n == 0:
                    for j in range(NT):
                        act.wait_ge(v_mm, j + 1)
                        fn(g_tok[:, j], ps(6 + j % 2, 0, D), ACT.Copy).then_inc(v_ready, 1)

            def copy_probs(n, s):
                act.wait_ge(pt_mm, n + 1)
                if past(n, 2):
                    act.wait_ge(pv_mm, n - 1)
                fn(ptS[0:T, s, 0:NTOK], psum[0:T, (2 + 2 * s) * 512:(2 + 2 * s) * 512 + NTOK], ACT.Copy)\
                    .then_inc(pt_ready, 1)

            def copy_o(n, s):
                act.wait_ge(pv_mm, n + 1)
                if past(n, 2):
                    act.wait_ge(ot_mm, n - 1)
                fn(oS[0:T, s], ps(6 + s, 0, D, T), ACT.Copy).then_inc(pv_ready, 1)

            def copy_oT(n, s):
                act.wait_ge(ot_mm, n + 1)
                for k in range(KD):
                    flat = xnT[:].rearrange("p k n -> p (k n)")
                    dst = flat[:, bass.DynSlice(n + (B + k * (B + NP)), T, step=B)]
                    ins = fn(dst, ps(6 + s, 256 + k * T, 256 + (k + 1) * T), ACT.Copy)
                ins.then_inc(ot_ready, 1)

            pipeline(act, [(copy_scores, 0), (exps, 0), (copy_probs, 2), (copy_o, 3), (copy_oT, 4)], B, 2, 4)

            load_table(ACT.Sigmoid)
            for j in range(NT):
                turned(3, j)
            act.wait_ge(lg_mm, NT)
            fn(lg[:].rearrange("p j e -> p (j e)"), ps(7, 0, NT * NE), ACT.Copy).then_inc(score_in, 1)
            act.wait_ge(score_in, 2)
            fn(rt5[:, 1], rt5[:, 0], ACT.Sigmoid).then_inc(score_ready, 1)
            act.wait_ge(score_ready, 1)
            act.wait_ge(h_ready, 4 * NT)
            for j in range(NT):
                ins = fn(xs_tok[:, j], xn_tok[:, j], ACT.Copy, scale=rt5[:, 1, j:j + 1])
            ins.then_inc(xs_ready, 1)
            for f in range(KF):
                act.wait_ge(sh_mm, 2 * f + 1)
                if f >= 1:
                    act.wait_ge(sh_ready, f)
                fn(gshT, psum[:, 4 * 512:4 * 512 + NP], ACT.Silu).then_inc(sh_silu, 1)

            def item_xT(s, bnk=0):
                return fn(xsT[:, s % XRING], ps(bnk, 0, KD * C).rearrange("p (k n) -> p k n", k=KD), ACT.Copy)

            def expert_xT(e, s):
                act.wait_ge(ex_mm, e + 1)
                if past(e, XRING):
                    act.wait_ge(gu_mm, e - XRING + 1)
                item_xT(s, s % 2).then_inc(ex_ready, 1)

            def expert_silu(e, s):
                act.wait_ge(gu_mm, e + 1)
                if past(e, 2):
                    act.wait_ge(act_ready, e - 1)
                fn(sgE[:, s % 2], ps(2 + 2 * (s % 2), 0, KF * C), ACT.Silu).then_inc(silu_ready, 1)

            def expert_copy(e, s):
                act.wait_ge(y_mm, e + 1)
                if past(e, 2):
                    act.wait_ge(ys_out[s % 2], (e - s % 2) * 8)
                fn(ysS[0:C, s % 2], ps(6 + s % 2, 0, D, C), ACT.Copy).then_inc(ys_ready, 1)

            act.wait_ge(ctl_ready, 1)
            more = act.value_load(ctl[0:1, NE + XTRA:NE + XTRA + 1], min_val=0, max_val=XTRA // RING)
            pipeline_rings(act, [(expert_xT, 0), (expert_silu, 1), (expert_copy, 2)], more)

        @block.vector
        def _(dve):
            v = nc.vector
            step = Link(dve, dve_step)
            v.memset(ones[:], 1.0).then_inc(consts_set, 1)
            v.memset(xnT[:, :, 0:B], 0.0)
            v.memset(neghalf[:], -0.5)
            v.memset(xT[:, :, 0:2 * B], 0.0)
            v.memset(xT[:, :, NTOK:NP], 0.0)
            v.memset(lwT[64:65], 1.0)
            v.memset(laT[64:65], 1.0).then_inc(consts_set, 1)

            def abs_sums(i, wt, k0, kn):
                v.tensor_reduce(absum[:, k0:k0 + kn], wt[:], X, ALU.add, apply_absolute_value=True)\
                    .then_inc(abs_sum, 1)

            def abs_total(i, kn, bank):
                dve.wait_ge(abs_row, i + 1)
                v.tensor_reduce(tern[0:1, 3 * i:3 * i + 1], psum[0:1, bank * 512:bank * 512 + kn * P], X, ALU.add)\
                    .then_inc(abs_one, 1)

            def signs(i, wt, bank):
                w, below, c = flat(wt), sr_flat[:, 0:HID * KD], 3 * i
                dve.wait_ge(abs_all, i + 1)
                step(v.tensor_scalar(tern[:, c + 1:c + 2], ps(bank, 0, 1), 1.0 / (HID * D), 1e-5, ALU.mult, ALU.max))
                step(v.reciprocal(tern[:, c + 2:c + 3], tern[:, c + 1:c + 2]))
                if i == 1:
                    dve.wait_ge(o_mm, GROUPS + 2)
                step(v.tensor_scalar(below, w, tern[:, c + 2:c + 3], -0.5, ALU.mult, ALU.is_lt))
                step(v.tensor_scalar(w, w, tern[:, c + 2:c + 3], 0.5, ALU.mult, ALU.is_gt))
                return v.tensor_tensor(w, w, below, ALU.subtract)

            def ln_stats(s, j):
                dve.wait_ge(h_ready, NT * s + j + 1)
                step(v.bn_stats(stat[:, j], h_tok[:, j]))
                step(v.bn_aggr(mv[:, j], stat[:, j]))
                if s == 1:
                    v.tensor_scalar(ve[:, j:j + 1], mv[:, j, 1:2], 1.0 + EPS, EPS * EPS, ALU.mult, ALU.add)\
                        .then_inc(ve_ready, 1)
                else:
                    v.tensor_scalar(ve[:, j:j + 1], mv[:, j, 1:2], EPS, None, ALU.add).then_inc(ve_ready, 1)

            def ln_apply(s, j):
                dve.wait_ge(rstd_ready, NT * s + j + 1)
                v.tensor_scalar(xn_tok[:, j], h_tok[:, j], mv[:, j, 0:1], rstd[:, j:j + 1], ALU.subtract, ALU.mult)\
                    .then_inc(xn_ready, 1)

            def layernorm(s, before=None):
                for j in range(NT + 1):
                    if j < NT:
                        if before:
                            before(j)
                        ln_stats(s, j)
                    if j >= 1:
                        ln_apply(s, j - 1)

            layernorm(0)

            def mixes(j):
                dve.wait_ge(xT_ready, j + 1)
                now = xnT[:, :, B + j * P:B + (j + 1) * P]
                if j >= 1:
                    dve.wait_ge(mix_ready, j)
                step(v.tensor_tensor(delta, xnT[:, :, j * P:(j + 1) * P], now, ALU.subtract))
                if j >= 2:
                    dve.wait_ge(proj_mm, j - 1)
                for m in range(5):
                    for k in range(KD):
                        ins = v.scalar_tensor_tensor(mix[:, j % 2, m, k], delta[:, k],
                                                     pvec[:, MIX + 2 * m + k:MIX + 2 * m + k + 1], now[:, k],
                                                     ALU.mult, ALU.add)
                ins.then_inc(mix_ready, 1)

            def hc(x):
                return x.rearrange("p (h c) -> p h c", h=HG)

            def hoc(x):
                return x.rearrange("p (h o c) -> p h o c", h=HG, o=2)

            def keys(j):
                psk = ps(2 + j % 2, D, 2 * D)
                dve.wait_ge(rv_packed, j + 1)
                v.tensor_tensor(kk, psk, rows[:, KK_], ALU.mult).then_inc(kk_ready, 1)
                dve.wait_ge(a_ready, j + 1)
                step(v.scalar_tensor_tensor(am, a_tok[:, j % 2], -1.0, rows[:, KA_], ALU.add, ALU.mult))
                v.scalar_tensor_tensor(pack[:, j, :, PK], hc(am), 1.0, hc(psk), ALU.add, ALU.mult)

            def keys_sum(j):
                dve.wait_ge(sq_ready, j + 1)
                step(v.tensor_reduce(ss[:], sqk.rearrange("p (h d) -> p h d", h=NH), X, ALU.add))
                v.tensor_scalar(ss[:], ss[:], 1e-24, None, ALU.max).then_inc(ss_ready, 1)

            def keys_norm(j):
                dve.wait_ge(rn_ready, j + 1)
                step(v.tensor_scalar(rn[:], rn[:], -1.0, None, ALU.mult))
                dst = pack[:, j, :, PA]
                step(v.tensor_tensor(dst.rearrange("p h (o c) -> p h o c", o=2), hoc(kk),
                                     rn[:].rearrange("p (h o) -> p h o", h=HG).unsqueeze(3).broadcast_to([P, HG, 2, HD]),
                                     ALU.mult))
                v.scalar_tensor_tensor(pack[:, j, :, PB], dst, -1.0, hc(a_tok[:, j % 2]), ALU.mult, ALU.mult)\
                    .then_inc(k_packed, 1)

            def scan(j):
                if j == 0:
                    dve.wait_ge(scan_dve, 2)
                dve.wait_ge(scan_loaded, LOADED + 16 * j)

                def times_r(g, u):
                    dst = sr_flat[:, bass.ds((g - j * TPT // GT) * (GT * ST) + u * ST, ST)]
                    v.tensor_tensor(s4(dst), s4(state), along_i(tcol(g * GT + u, PR)), ALU.mult).then_inc(scan_dve, 1)

                def group(g, steps):
                    for u in range(steps):
                        t, at, now, lead = g * GT + u, g * (GT * SCAN_DVE), u * SCAN_DVE + 2, int(u == 0)
                        dve.wait_ge(scan_dve, at + (now - 1))
                        v.tensor_tensor(s4(prod), s4(state), along_i(tcol(t, PA)), ALU.mult).then_inc(scan_dve, 1)
                        v.tensor_tensor(kv[:, 0:256].rearrange("p (i j) -> p i j", i=HD),
                                        tcol(t, PV)[:, 0].unsqueeze(2).broadcast_to([P, HD, HD]),
                                        tcol(t, PK)[:, 0].unsqueeze(1).broadcast_to([P, HD, HD]), ALU.mult)\
                            .then_inc(scan_dve, 1)
                        dve.wait_ge(scan_dve, at + (now + lead))
                        v.tensor_reduce(sa[:], prod.rearrange("p (x j) -> p x j", j=HD), X, ALU.add)\
                            .then_inc(scan_dve, 1)
                        if u >= 1:
                            if u == 1:
                                dve.wait_ge(o_mm, g + 1)
                            times_r(g, u - 1)
                        dve.wait_ge(scan_dve, at + (now + 2 + lead))
                        v.tensor_tensor(s4(outer), along_j(sa[:].rearrange("p (h i) -> p h i", h=2)),
                                        along_i(tcol(t, PB)), ALU.mult).then_inc(scan_dve, 1)
                        dve.wait_ge(scan_dve, at + (now + 4))
                        dve.wait_ge(scan_pool, g * (GT * SCAN_POOL) + ((u + 1) * SCAN_POOL + 1))
                        v.tensor_tensor(state, outer, carried, ALU.add).then_inc(scan_dve, 1)
                    dve.wait_ge(scan_dve, g * (GT * SCAN_DVE) + (steps * SCAN_DVE + 1))
                    times_r(g, steps - 1)

                scan_groups(j, group)

            dve.wait_ge(l_rw, 16 * 7)
            mixes(0)
            mixes(1)
            dve.wait_ge(l_tern, 48)
            abs_sums(0, w1t, 0, KD)
            keys(0)
            keys_sum(0)
            abs_total(0, KD, 1)
            mixes(2)
            keys_norm(0)
            keys(1)
            keys_sum(1)
            signs(0, w1t, 1).then_inc(tern_ready, 1)
            keys_norm(1)
            dve.wait_ge(emb_mm, NT)
            for head in range(2):
                v.memset(state[:, head * HD * HD:(head + 1) * HD * HD], 0.0).then_inc(scan_dve, 1)
            scan(0)
            keys(2)
            keys_sum(2)
            mixes(3)
            keys_norm(2)
            scan(1)
            keys(3)
            keys_sum(3)
            mixes(4)
            keys_norm(3)
            scan(2)
            keys(4)
            keys_sum(4)
            keys_norm(4)
            scan(3)
            scan(4)
            for j in range(NT):
                dve.wait_ge(rk_ready, j + 1)
                v.tensor_reduce(bs[:, j], bonus[:, j].rearrange("p (h d) -> p h d", h=NH), X, ALU.add)\
                    .then_inc(bs_ready, 1)

            def heads(x):
                return x.rearrange("p (h d) -> p h d", h=NH)

            def spread(x):
                return x.unsqueeze(2).broadcast_to([P, NH, HD])

            for j in range(NT):
                dve.wait_ge(o_loaded, 16 * (j + 1))
                o = heads(xn_tok[:, j])
                step(v.tensor_reduce(gmu[:, j], o, X, ALU.add))
                v.scalar_tensor_tensor(o, spread(gmu[:, j]), -1.0 / HD, o, ALU.mult, ALU.add).then_inc(cen_ready, 1)
            for j in range(NT):
                dve.wait_ge(gsq_ready, j + 1)
                step(v.tensor_reduce(gva[:, j], gsq[:, j].rearrange("p (h d) -> p h d", h=NH), X, ALU.add))
                v.tensor_scalar(gva[:, j], gva[:, j], 1.0 / HD, EPS, ALU.mult, ALU.add).then_inc(gva_ready, 1)
            dve.wait_ge(grs_ready, 1)
            step(v.reciprocal(grs[:], grs[:]))
            for j in range(NT):
                y = xn_tok[:, j]
                step(v.tensor_tensor(heads(y), heads(y), spread(grs[:, j]), ALU.mult))
                dve.wait_ge(bonus_ready, j + 1)
                step(v.tensor_tensor(y, y, g_tok[:, j], ALU.mult))
                v.tensor_tensor(y, y, bonus[:, j], ALU.add).then_inc(y_ready, 1)

            def add_to_h(src):
                def add(j):
                    src_ap, s, n = src(j)
                    dve.wait_ge(s, n)
                    v.tensor_tensor(h_tok[:, j], h_tok[:, j], src_ap, ALU.add).then_inc(h_ready, 1)
                return add

            layernorm(1, add_to_h(lambda j: (ps(3 + j % 2, 0, D), wo_mm, j + 1)))

            abs_sums(1, w2t, KD, KH)
            abs_total(1, KH, 6)
            step(signs(1, w2t, 6))
            v.memset(w2g[:, :, D:D + 1], 1.0)
            for k in range(KH):
                ins = v.tensor_scalar(w2g[:, k, 0:D], w2t[:, k], pvec[:, LN2G + k:LN2G + k + 1], None, ALU.mult)
            ins.then_inc(tern_ready, 1)
            for m in range(1, KH):
                if m == 5:
                    dve.wait_ge(rows2_mm, 1)
                    v.tensor_copy(row2[0:1, 0], ps(6, 0, D, 1))
                    v.scalar_tensor_tensor(row2[0:1, 1], ps(7, 0, D, 1), tern[0:1, 4:5], brow[0:1, 1],
                                           ALU.mult, ALU.add).then_inc(rows2_set, 1)
                dve.wait_ge(f1_ready, m + 1)
                ins = v.tensor_tensor(sqT[:, 0], sqT[:, 0], sqT[:, m], ALU.add)
                if m < KH - 1:
                    step(ins)
            ins.then_inc(sqsum_ready, 1)

            def ffn_stats(j):
                dve.wait_ge(f2_mm, j + 1)
                b = 6 + j % 2
                v.tensor_scalar(fst[:, j, 0:1], ps(b, D, D + 1), -1.0 / HID, None, ALU.mult)
                step(v.tensor_scalar(fst[:, j, 1:2], ps(b, 300, 301), 1.0 / HID, EPS, ALU.mult, ALU.add))
                step(v.tensor_tensor(fst[:, j, 2:3], fst[:, j, 0:1], fst[:, j, 0:1], ALU.mult))
                v.tensor_tensor(fst[:, j, 3:4], fst[:, j, 1:2], fst[:, j, 2:3], ALU.subtract).then_inc(fv_ready, 1)
                step(v.scalar_tensor_tensor(xn_tok[:, j], bc2[:, 0], fst[:, j, 0:1], ps(b, 0, D), ALU.mult, ALU.add))

            def ffn_apply(j):
                dve.wait_ge(frs_ready, j + 1)
                step(v.tensor_tensor(fst[:, j, 5:6], fst[:, j, 4:5], tern[:, 4:5], ALU.mult))
                step(v.scalar_tensor_tensor(xn_tok[:, j], xn_tok[:, j], fst[:, j, 5:6], bc2[:, 1], ALU.mult, ALU.add))
                v.tensor_tensor(h_tok[:, j], h_tok[:, j], xn_tok[:, j], ALU.add).then_inc(h_ready, 1)

            dve.wait_ge(bc2_set, 1)
            dve.wait_ge(xT_mm, 2 * NT)

            def ffn(j):
                ffn_stats(j)
                ffn_apply(j)

            layernorm(2, ffn)

            dve.wait_ge(l_late, 16 * 5)
            dve.wait_ge(f2_mm, NT)
            v.memset(qm, 0.0).then_inc(qm_zero, 1)
            step(v.tensor_scalar(thr[:], thr[:], 0.0, 1.0, ALU.max, ALU.min))
            step(v.tensor_scalar(thr[:], thr[:], 4.0, None, ALU.mult))
            step(v.tensor_scalar(thr5[:], cst[:, C_PADROW:C_PADROW + 5], thr[:], None, ALU.add))

            def plain():
                v.memset(cell[:, 0:1], 0.0)

            def keep_mask(n, s):
                v.tensor_tensor(keep[:, s], scS[:, s], cthr[:, s].unsqueeze(2).broadcast_to([P, 5, T]), ALU.is_ge)\
                    .then_inc(keep_ready, 1)

            def sum_probs(n, s):
                dve.wait_ge(pm_ready, n + 1)
                v.tensor_reduce(rinv[:, s], pm[:, s], X, ALU.add).then_inc(sum_ready, 1)

            def invert_sums(n, s):
                dve.wait_ge(sum_ready, n + 1)
                v.reciprocal(rinv[:, s], rinv[:, s]).then_inc(rinv_ready, 1)

            def topk(n, s):
                sc = [scS[:, s, i] for i in range(5)]
                done = lambda c: dve.wait_ge(top_step, n * 6 + c)
                dve.wait_ge(sc_ready, n + 1)
                if past(n, 1):
                    done(0)
                    keep_mask(n - 1, 1 - s)
                else:
                    plain()
                for i in range(5):
                    ins = v.max(mx[:, s, i, 0:8], sc[i])
                ins.then_inc(top_step, 1)
                done(1)
                v.tensor_scalar(nb[:, s], mx[:, s, :, 0], -0.25, None, ALU.mult).then_inc(nb_ready, 1)
                for i in range(5):
                    ins = v.match_replace(without8[:, i], mx[:, s, i, 0:8], sc[i], NEG)
                ins.then_inc(top_step, 1)
                done(2)
                sum_probs(n - 1, 1 - s) if past(n, 1) else plain()
                for i in range(5):
                    ins = v.max(mx[:, s, i, 8:16], without8[:, i])
                ins.then_inc(top_step, 1)
                done(3)
                invert_sums(n - 1, 1 - s) if past(n, 1) else plain()
                for i in range(5):
                    ins = v.match_replace(without16[:, i], mx[:, s, i, 8:16], without8[:, i], NEG)
                ins.then_inc(top_step, 1)
                done(4)
                plain()
                for i in range(5):
                    ins = v.max(mx[:, s, i, 16:24], without16[:, i])
                ins.then_inc(top_step, 1)
                done(5)
                v.tensor_tensor(cthr[:, s], mx[:, s, :, KEEP - 1], thr5[:], ALU.max).then_inc(top_step, 1)

            pipeline(dve, [(topk, 0)], B, 2, 2)
            dve.wait_ge(top_step, 6 * B)
            keep_mask(B - 1, 1)
            sum_probs(B - 1, 1)
            invert_sums(B - 1, 1)

            layernorm(3, add_to_h(lambda j: (ps(2 + j % 2, 0, D), ao_mm, j + 1)))

            def wide(x, n=NE):
                return x.unsqueeze(2).broadcast_to([P, NT, n])

            em = cst[:, C_E:C_E + NE].unsqueeze(1).broadcast_to([P, NT, NE])
            dve.wait_ge(score_in, 1)
            step(v.tensor_reduce(rt5[:, 0], lg[:], X, ALU.max))
            step(v.tensor_tensor(rt1[:], lg[:], wide(rt5[:, 0]), ALU.is_equal))
            v.tensor_tensor(rt1[:], rt1[:], em, ALU.mult).then_inc(score_in, 1)
            dve.wait_ge(score_in, 2)
            step(v.tensor_reduce(rt5[:, 2], rt1[:], X, ALU.min))
            step(v.tensor_tensor(oh[:], em, wide(rt5[:, 2]), ALU.is_equal))
            valid = cst[:, C_VALID:C_VALID + NT]
            v.tensor_tensor(oh[:], oh[:], wide(valid), ALU.mult).then_inc(oh_ready, 1)

            def shared_act(f):
                dve.wait_ge(sh_silu, f + 1)
                dve.wait_ge(sh_mm, 2 * f + 2)
                v.tensor_tensor(shT[:, f], gshT, psum[:, 6 * 512:6 * 512 + NP], ALU.mult).then_inc(sh_ready, 1)

            shared_act(0)
            dve.wait_ge(cnt_mm, 1)
            dve.wait_ge(oh_ready, 1)
            step(v.tensor_tensor(rt1[:], oh[:], ps(3, 0, NT * NE).rearrange("p (j e) -> p j e", j=NT), ALU.mult))
            step(v.tensor_reduce(rt5[:, 3], rt1[:], X, ALU.add))
            cnt = ps(3, NT * NE, (NT + 1) * NE)
            step(v.tensor_scalar(ex16[:, 0], cnt, float(C), None, ALU.is_gt))
            for m in range(2, XTRA + 1):
                step(v.scalar_tensor_tensor(ex16[:, 0], cnt, float(C * m), ex16[:, 0], ALU.is_gt, ALU.add))
            step(v.tensor_tensor_scan(ex16[:, 1], ones[:, 0:NE], ex16[:, 0], 0.0, ALU.mult, ALU.add))
            step(v.tensor_tensor(ex16[:, 2], ex16[:, 1], ex16[:, 0], ALU.subtract))
            step(v.tensor_tensor(rt1[:], oh[:], ex16[:, 2].unsqueeze(1).broadcast_to([P, NT, NE]), ALU.mult))
            step(v.tensor_reduce(rt5[:, 4], rt1[:], X, ALU.add))
            step(v.tensor_scalar(rt5[:, 4], rt5[:, 4], float(NE - 1), None, ALU.add))
            v.tensor_scalar(rt5[:, 5], rt5[:, 2], float(NE), None, ALU.add)
            step(v.tensor_scalar(rt5[:, 6], rt5[:, 3], float(C), None, ALU.is_lt))
            step(v.tensor_tensor(rt5[:, 5], rt5[:, 5], rt5[:, 4], ALU.subtract))
            step(v.tensor_tensor(rt5[:, 5], rt5[:, 5], rt5[:, 6], ALU.mult))
            step(v.tensor_tensor(rt5[:, 5], rt5[:, 5], rt5[:, 4], ALU.add))
            step(v.scalar_tensor_tensor(rt5[:, 5], rt5[:, 5], float(C), rt5[:, 3], ALU.mult, ALU.add))
            step(v.tensor_tensor(rt5[:, 5], rt5[:, 5], valid, ALU.mult))
            v.tensor_tensor(slot[:], rt5[:, 5], cst[:, C_TROW:C_TROW + NT], ALU.add).then_inc(slot_ready, 1)
            v.tensor_scalar(ctlf[:, 0:NE], cst[:, C_E:C_E + NE], float(NE), None, ALU.add)
            step(v.tensor_tensor(xk[:], ex16[:, 1].unsqueeze(1).broadcast_to([P, XTRA, NE]),
                                 cst[:, C_K:C_K + XTRA].unsqueeze(2).broadcast_to([P, XTRA, NE]), ALU.is_le))
            step(v.tensor_reduce(ctlf[:, NE:NE + XTRA], xk[:], X, ALU.add))
            step(v.tensor_scalar(ctlf[:, NE:NE + XTRA], ctlf[:, NE:NE + XTRA], float(NE - 1), None, ALU.min))
            total, rings = ex16[:, 1, NE - 1:NE], ctlf[:, NE + XTRA:NE + XTRA + 1]
            step(v.tensor_scalar(rings, total, 0.0, None, ALU.is_gt))
            for m in range(RING, XTRA, RING):
                step(v.scalar_tensor_tensor(rings, total, float(m), rings, ALU.is_gt, ALU.add))
            v.tensor_copy(ctl[:], ctlf[:]).then_inc(ctl_ready, 1)

            for f in range(1, KF):
                shared_act(f)

            def expert_act(e, s):
                dve.wait_ge(silu_ready, e + 1)
                if past(e, 2):
                    dve.wait_ge(y_mm, e - 1)
                v.tensor_tensor(actE[:, s % 2], sgE[:, s % 2], ps(3 + 2 * (s % 2), 0, KF * C), ALU.mult)\
                    .then_inc(act_ready, 1)

            dve.wait_ge(ctl_ready, 1)
            more = dve.value_load(ctl[0:1, NE + XTRA:NE + XTRA + 1], min_val=0, max_val=XTRA // RING)
            pipeline_rings(dve, [(expert_act, 0)], more)
            for j in range(NT + 1):
                if j < NT:
                    dve.wait_ge(sd_mm, j + 1)
                    v.tensor_tensor(ysum[:, j], h_tok[:, j], ps(4 + j % 2, 0, D), ALU.add).then_inc(ysum_ready, 1)
                if j >= 1:
                    dve.wait_ge(yg_loaded[j - 1], 16)
                    dve.wait_ge(ysum_ready, j)
                    v.tensor_tensor(xn_tok[:, j - 1], ysum[:, j - 1], ygat[:, j - 1], ALU.add).then_inc(res_ready, 1)

        @block.gpsimd
        def _(pool):
            g = nc.gpsimd
            pool.wait_ge(consts_set, 2)
            g.memset(cell[:, 1:2], 0.0).then_inc(scan_pool, 1)

            def ln_pow(s, j):
                pool.wait_ge(ve_ready, NT * s + j + 1)
                g.tensor_tensor(rstd[:, j:j + 1], ve[:, j:j + 1], neghalf[:, 0:1], ALU.pow).then_inc(rstd_ready, 1)

            for j in range(NT):
                ln_pow(0, j)

            def key_pow(j):
                pool.wait_ge(ss_ready, j + 1)
                g.tensor_tensor(rn[:], ss[:], neghalf[:], ALU.pow).then_inc(rn_ready, 1)

            def rk(j):
                pool.wait_ge(k_packed, j + 1)
                pool.wait_ge(rv_packed, j + 1)
                dst = bonus[:, j].rearrange("p (h c) -> p h c", h=HG)
                g.tensor_tensor(dst, pack[:, j, :, PR], pack[:, j, :, PK], ALU.mult).then_inc(pool_step, 1)
                pool.wait_ge(pool_step, j + 1)
                g.tensor_tensor(bonus[:, j], bonus[:, j], rows[:, RK_], ALU.mult).then_inc(rk_ready, 1)

            def scan(j):
                pool.wait_ge(scan_loaded, LOADED + 16 * j)
                pool.wait_ge(scan_dve, 2)

                def group(g, steps):
                    for u in range(steps):
                        t, lead = g * GT + u, int(u == 0)
                        done = g * (GT * SCAN_POOL) + (u * SCAN_POOL + 1)
                        at, now = g * (GT * SCAN_DVE), u * SCAN_DVE + 2
                        pool.wait_ge(scan_pool, done)
                        nc.gpsimd.tensor_tensor(kv[:, 256:512].rearrange("p (i j) -> p i j", i=HD),
                                         tcol(t, PV)[:, 1].unsqueeze(2).broadcast_to([P, HD, HD]),
                                         tcol(t, PK)[:, 1].unsqueeze(1).broadcast_to([P, HD, HD]), ALU.mult)\
                            .then_inc(scan_pool, 1)
                        pool.wait_ge(scan_dve, at + (now - 1))
                        nc.gpsimd.tensor_tensor(s4(decayed), s4(state), along_i(tcol(t, PW)), ALU.mult)\
                            .then_inc(scan_pool, 1)
                        pool.wait_ge(scan_pool, done + 2)
                        pool.wait_ge(scan_dve, at + (now + 1 + lead))
                        nc.gpsimd.tensor_tensor(carried, decayed, kv, ALU.add).then_inc(scan_pool, 1)

                scan_groups(j, group)

            key_pow(0)
            key_pow(1)
            scan(0)
            rk(0)
            key_pow(2)
            scan(1)
            rk(1)
            key_pow(3)
            scan(2)
            rk(2)
            key_pow(4)
            scan(3)
            rk(3)
            scan(4)
            rk(4)
            for j in range(NT):
                pool.wait_ge(bs_ready, j + 1)
                g.tensor_tensor(bonus[:, j].rearrange("p (h o c) -> p h o c", h=HG, o=2),
                                pack[:, j, :, PV].rearrange("p h (o c) -> p h o c", o=2),
                                bs[:, j].rearrange("p (h o) -> p h o", h=HG).unsqueeze(3).broadcast_to([P, HG, 2, HD]),
                                ALU.mult).then_inc(pool_step, 1)
                pool.wait_ge(pool_step, NT + 2 * j + 1)
                g.tensor_tensor(bonus[:, j], bonus[:, j], rows[:, GNB], ALU.add).then_inc(pool_step, 1)
            for j in range(NT):
                pool.wait_ge(g_ready, j + 1)
                pool.wait_ge(pool_step, 3 * NT)
                g.tensor_tensor(bonus[:, j], bonus[:, j], g_tok[:, j], ALU.mult).then_inc(pool_step, 1)
                pool.wait_ge(pool_step, 3 * NT + j + 1)
                g.tensor_tensor(g_tok[:, j], g_tok[:, j], rows[:, GNW], ALU.mult).then_inc(bonus_ready, 1)
            for j in range(NT):
                ln_pow(1, j)
            for j in range(NT):
                pool.wait_ge(fv_ready, j + 1)
                g.tensor_tensor(fst[:, j, 4:5], fst[:, j, 3:4], neghalf[:, 0:1], ALU.pow).then_inc(frs_ready, 1)
                ln_pow(2, j)

            pool.wait_ge(qm_zero, 1)
            pool.wait_ge(q_ready, 2)
            pool.wait_ge(l_mid, 48)
            mask = cst[:, C_HM:C_HM + HG].unsqueeze(1).unsqueeze(3).broadcast_to([P, KD, HG, T])

            def mask_q(n, s):
                if past(n, 2):
                    pool.wait_ge(sc_mm, n - 1)
                src = qT[:, :, bass.ds(n * T, T)].unsqueeze(2).broadcast_to([P, KD, HG, T])
                dst = qm[:, s].rearrange("p (k n) -> p k n", k=KD)[:, :, 0:HG * T]
                g.tensor_tensor(dst.rearrange("p k (h q) -> p k h q", h=HG), src, mask, ALU.mult)\
                    .then_inc(qm_ready, 1)

            def mask_p(n, s):
                pool.wait_ge(exp_ready, n + 1)
                pool.wait_ge(keep_ready, n + 1)
                if past(n, 2):
                    pool.wait_ge(pt_mm, n - 1)
                g.tensor_tensor(pm[:, s], ex[:, s], keep[:, s], ALU.mult).then_inc(pm_ready, 1)

            def norm_p(n, s):
                pool.wait_ge(rinv_ready, n + 1)
                g.tensor_tensor(pm[:, s], pm[:, s], rinv[:, s].unsqueeze(2).broadcast_to([P, 5, T]), ALU.mult)\
                    .then_inc(pn_ready, 1)

            def probs(n, s):
                mask_p(n, s)
                if not isinstance(n, int) or n + 2 < B:
                    mask_q(n + 2, s)
                norm_p(n, s)

            mask_q(0, 0)
            mask_q(1, 1)
            pipeline(pool, [(probs, 0)], B - 2, 2, 2)
            probs(B - 2, 0)
            probs(B - 1, 1)

            for j in range(NT):
                ln_pow(3, j)
            pool.wait_ge(slot_ready, 1)
            pool.wait_ge(xs_ready, 1)
            n_zero = -(-(TRASH + P) // P) + -(-(TRASH + P - NE * C) // P)
            pool.wait_ge(zero_out, 16 * n_zero)
            for j in range(NT):
                g.indirect_dma_start(xs_dram, bass.IndirectOffsetOnAxis(slot[:, j:j + 1], 0), xs_tok[:, j], None)\
                    .then_inc(xs_out[j], 16)
            pool.wait_ge(ctl_ready, 1)
            more = pool.value_load(ctl[0:1, NE + XTRA:NE + XTRA + 1], min_val=0, max_val=XTRA // RING)
            for half in range(2):
                pool.wait_ge(ys_out[half], more * (8 * RING) + 8 * NE)
            g.tensor_tensor(cell[:, 1:2], neghalf[:, 0:1], neghalf[:, 0:1], ALU.add)
            for j in range(NT):
                g.indirect_dma_start(ygat[:, j], None, ys_dram, bass.IndirectOffsetOnAxis(slot[:, j:j + 1], 0))\
                    .then_inc(yg_loaded[j], 16)


def kernel(x, cls_tok, **w):
    import numpy as np
    import concourse.bacc as bacc
    from concourse import mybir as mb
    from concourse.bass_utils import run_bass_kernel_spmd

    def chunks(m):
        k, n = m.shape
        return m.reshape(k // P, P, n).transpose(1, 0, 2).reshape(P, -1)

    def cols(v):
        return v.reshape(-1, P).T

    t0, a0, f0, a1, f1 = "L0_tok_", "L0_attn_", "L0_ffn_", "L1_attn_", "L1_ffn_"
    w = {k: np.asarray(m) for k, m in w.items()}
    x = np.asarray(x)
    patches = x.reshape(B, 3, 6, 16, 6, 16).transpose(1, 3, 5, 2, 4, 0).reshape(768, 36 * B)
    sel = np.zeros((40, NP), np.float32)
    for n in range(NTOK):
        sel[n // B, n] = 1
        if n // B == 1:
            sel[39, n] = 1
        if n // B >= 2:
            sel[38, n] = 1
    cst = np.zeros((P, NCST), np.float32)
    cst[NH * T - 4 * P:, C_PADROW + 4] = NEG
    cst[:, C_E:C_E + NE] = np.arange(NE) - NE
    tok = np.arange(NP).reshape(NT, P).T
    cst[:, C_VALID:C_VALID + NT] = tok < NTOK
    cst[:, C_TROW:C_TROW + NT] = np.where(tok < NTOK, 0, TRASH + tok - NTOK)
    cst[:, C_K:C_K + XTRA] = np.arange(XTRA)
    cst[:, C_HM:C_HM + HG] = np.arange(P)[:, None] // HD == np.arange(HG)
    arrays = {
        "xT": np.concatenate([chunks(patches[:, max(2 * B, j * P) - 2 * B:min(NTOK, (j + 1) * P) - 2 * B])
                              for j in range(NT)], 1),
        "tokw": chunks(w[t0 + "W"].T),
        "cls_tok": np.asarray(cls_tok).reshape(1, D),
        "pos": w[t0 + "pos_embedding"].reshape(T - 1, D),
        "tok_b": w[t0 + "b"].reshape(1, D),
        "tok_cls": w[t0 + "cls_token"].reshape(1, D),
        "sel": sel,
        "ident": np.eye(P, dtype=np.float32),
        "tri": np.triu(np.ones((P, P), np.float32), 1),
        "cst": cst,
        "zero": np.zeros((P, D), np.float32),
        "pvec": np.concatenate([cols(w[a0 + n]) for n in ("x_r", "x_w", "x_k", "x_v", "x_a")]
                               + [cols(w[f0 + n]) for n in ("ln1_g", "ln1_b", "b1", "ln2_g", "ln2_b")], 1),
        "rows": np.concatenate([w[a0 + n].reshape(-1) for n in ("k_k", "k_a", "r_k", "gn_weight", "gn_bias")])[None],
        "brow": np.concatenate([w[a0 + "g_lora_bias"], w[f0 + "b2"], w[a1 + "bo"]])[None],
        "w4": np.concatenate([chunks(w[a0 + n]) for n in ("W_r", "W_k", "W_v", "W_o")], 1),
        "lora_a": chunks(np.concatenate([w[a0 + n + "_lora_a"] for n in "wag"], 1)),
        "wlb": w[a0 + "w_lora_b"], "wlbias": w[a0 + "w_lora_bias"][None],
        "alb": w[a0 + "a_lora_b"], "albias": w[a0 + "a_lora_bias"][None],
        "glb": w[a0 + "g_lora_b"],
        "w1t": chunks(w[f0 + "w1"].T), "w2t": chunks(w[f0 + "w2"].T),
        "wat": np.concatenate([chunks(w[a1 + n].T) for n in ("Wq", "Wk", "Wv", "Wo")], 1),
        "thr": w[a1 + "adaptive_threshold"].reshape(1, 1),
        "wrt": chunks(w[f1 + "w_router"].T),
        "gate_up": w[f1 + "gate_up_proj"], "down": w[f1 + "down_proj"],
        "wsh": chunks(np.concatenate([w[f1 + "w_gate"].T, w[f1 + "w_up"].T], 1)),
        "wsd": chunks(w[f1 + "w_down"].T),
    }
    arrays = {n: np.ascontiguousarray(m) for n, m in arrays.items()}
    nc = bacc.Bacc("TRN2", target_bir_lowering=False, num_devices=1)
    arrays = {"in_" + n: m for n, m in arrays.items()}
    args = {n[3:]: nc.dram_tensor(n, m.shape, mb.dt.from_np(m.dtype), kind="ExternalInput").ap()
            for n, m in arrays.items()}
    out = nc.dram_tensor("out", [NTOK, D], F32, kind="ExternalOutput").ap()
    build(nc, args, out)
    r = run_bass_kernel_spmd(nc, [arrays], core_ids=[0])
    return r.results[0]["out"].reshape(T, B, D).transpose(1, 0, 2)
```
